# Optimizing a Trainium2 kernel written in Bass

```python
import numpy as np
import jax
import jax.numpy as jnp

def _softmax(x, axis=-1):
    return jax.nn.softmax(x, axis=axis)

def _gelu(x):
    return jax.nn.gelu(x, approximate=True)

def _silu(x):
    return jax.nn.silu(x)

def _sigmoid(x):
    return jax.nn.sigmoid(x)

def _layernorm(x, axis=-1, eps=1e-05):
    m = jnp.mean(x, axis=axis, keepdims=True)
    v = jnp.var(x, axis=axis, keepdims=True)
    return (x - m) / jnp.sqrt(v + eps)

def _scatter_add(tgt, idx, src, axis=0):
    return tgt.at[idx].add(src)

def _segment_sum(src, seg, n):
    return jax.ops.segment_sum(src, seg, n)
kernel_name = 'mk_gnn_resnorm_d4_gnn_r32_ae50f5'

def setup_inputs(seed: int=0):
    np.random.seed(seed)
    _w = jnp.asarray

    def _rec_inputs():
        import jax
        import jax.numpy as jnp
        _gk = jax.random.key(seed)
        x = -0.000202 + 1 * jax.random.normal(jax.random.fold_in(_gk, 1), (3125, 128), jnp.float32)
        src = jax.random.randint(jax.random.fold_in(_gk, 2), (100000,), 0, 3125, jnp.int32)
        dst = jnp.minimum((3125 * jax.random.uniform(jax.random.fold_in(_gk, 3), (100000,)) ** 2.0).astype(jnp.int32), 99999)
        _o = jnp.argsort(dst, stable=True)
        src = src[_o]
        dst = dst[_o]
        edge_type_500 = jax.random.randint(jax.random.fold_in(_gk, 14), (100000,), 0, 500, jnp.int32)
        return (x, src, dst, edge_type_500)
    x, src, dst, edge_type_500 = _rec_inputs()

    def _L0_gnn_setup():
        import jax, jax.numpy as jnp
        import numpy as np
        N_NODES = 50000
        N_EDGES = 18750
        N_RELS = 500
        D = 128
        key = jax.random.key(seed)
        ks = jax.random.split(key, 8)
        h = jax.random.normal(ks[0], (N_NODES, D), dtype=jnp.float32)
        norm = jax.random.uniform(ks[1], (N_NODES, 1), dtype=jnp.float32)
        rel_emb = jax.random.normal(ks[2], (N_RELS, D), dtype=jnp.float32)
        lim = np.sqrt(6.0 / (D + D)) * np.sqrt(2.0)
        W_neighbor = jax.random.uniform(ks[3], (D, D), dtype=jnp.float32, minval=-lim, maxval=lim)
        loop_weight = jax.random.uniform(ks[4], (D, D), dtype=jnp.float32, minval=-lim, maxval=lim)
        edge_src = jax.random.randint(ks[5], (N_EDGES,), 0, N_NODES, dtype=jnp.int64 if jax.config.jax_enable_x64 else jnp.int32)
        edge_dst = jax.random.randint(ks[6], (N_EDGES,), 0, N_NODES, dtype=edge_src.dtype)
        edge_type = jax.random.randint(ks[7], (N_EDGES,), 0, N_RELS, dtype=edge_src.dtype)
        return {'h': h, 'norm': norm, 'rel_emb': rel_emb, 'W_neighbor': W_neighbor, 'loop_weight': loop_weight, 'edge_src': edge_src, 'edge_dst': edge_dst, 'edge_type': edge_type}
    _L0_gnn_all = _L0_gnn_setup()
    _L0_gnn_in = {k: v for k, v in _L0_gnn_all.items() if k in ('rel_emb', 'W_neighbor', 'loop_weight')}
    del _L0_gnn_all

    def _L1_gnn_setup():
        import jax, jax.numpy as jnp
        import numpy as np
        N = 50000
        E = 25000
        F = 128
        UNITS = 128
        ATT_UNITS = 128
        HEADS = 8

        def segment_softmax(scores, seg, num_segments):
            smax = jax.ops.segment_max(scores, seg, num_segments=num_segments)
            sexp = jnp.exp(scores - smax[seg])
            ssum = jax.ops.segment_sum(sexp, seg, num_segments=num_segments)
            return sexp / ssum[seg]
        key = jax.random.key(seed)
        ks = jax.random.split(key, 6)
        s = 1.0 / np.sqrt(F).astype(np.float32)
        return {'x': jax.random.normal(ks[0], (N, F), dtype=jnp.float32), 'edge_index': jax.random.randint(ks[1], (2, E), 0, N, dtype=jnp.int32), 'query_kernel': jax.random.normal(ks[2], (F, ATT_UNITS), dtype=jnp.float32) * s, 'query_bias': jnp.zeros((ATT_UNITS,), jnp.float32), 'key_kernel': jax.random.normal(ks[3], (F, ATT_UNITS), dtype=jnp.float32) * s, 'key_bias': jnp.zeros((ATT_UNITS,), jnp.float32), 'kernel': jax.random.normal(ks[4], (F, UNITS), dtype=jnp.float32) * s, 'bias': jnp.zeros((UNITS,), jnp.float32)}
    _L1_gnn_all = _L1_gnn_setup()
    _L1_gnn_in = {k: v for k, v in _L1_gnn_all.items() if k in ('query_kernel', 'query_bias', 'key_kernel', 'key_bias', 'kernel', 'bias')}
    del _L1_gnn_all

    def _L2_gnn_setup():
        import jax, jax.numpy as jnp
        import numpy as np
        N_NODES = 3125
        N_EDGES = 50000
        D_IN = 128
        D_OUT = 128
        key = jax.random.key(seed)
        k1, k2, k3, k4 = jax.random.split(key, 4)
        feat = jax.random.normal(k1, (N_NODES, D_IN), dtype=jnp.float32)
        weight = jax.random.normal(k2, (D_IN, D_OUT), dtype=jnp.float32) * (1.0 / np.sqrt(D_IN))
        src = jax.random.randint(k3, (N_EDGES,), 0, N_NODES, dtype=jnp.int64)
        dst = jax.random.randint(k4, (N_EDGES,), 0, N_NODES, dtype=jnp.int64)
        return {'feat': feat, 'weight': weight, 'src': src, 'dst': dst}
    _L2_gnn_all = _L2_gnn_setup()
    _L2_gnn_in = {k: v for k, v in _L2_gnn_all.items() if k in ('weight',)}
    del _L2_gnn_all

    def _L3_gnn_setup():
        import jax, jax.numpy as jnp
        import numpy as np
        N_NODES = 50000

        def _gcn_norm(edge_index, num_nodes):
            loop = jnp.arange(num_nodes, dtype=edge_index.dtype)
            src = jnp.concatenate([edge_index[0], loop])
            dst = jnp.concatenate([edge_index[1], loop])
            deg = jax.ops.segment_sum(jnp.ones_like(dst, dtype=jnp.float32), dst, num_segments=num_nodes)
            dinv = jnp.where(deg > 0, jax.lax.rsqrt(deg), 0.0)
            norm = dinv[src] * dinv[dst]
            return (src, dst, norm)

        def _gcn_layer(x, W, b, src, dst, norm, num_nodes):
            h = x @ W
            msg = h[src] * norm[:, None]
            agg = jax.ops.segment_sum(msg, dst, num_segments=num_nodes)
            return agg + b
        key = jax.random.key(seed)
        ks = jax.random.split(key, 5)
        N, E, F, H, O = (N_NODES, 25000, 128, 128, 128)
        x = jax.random.normal(ks[0], (N, F), dtype=jnp.float32)
        edge_index = jax.random.randint(ks[1], (2, E), 0, N, dtype=jnp.int64)
        W1 = jax.random.normal(ks[2], (F, H), dtype=jnp.float32) * (1.0 / np.sqrt(F))
        b1 = jnp.zeros((H,), dtype=jnp.float32)
        W2 = jax.random.normal(ks[3], (H, O), dtype=jnp.float32) * (1.0 / np.sqrt(H))
        b2 = jnp.zeros((O,), dtype=jnp.float32)
        return {'x': x, 'edge_index': edge_index, 'W1': W1, 'b1': b1, 'W2': W2, 'b2': b2}
    _L3_gnn_all = _L3_gnn_setup()
    _L3_gnn_in = {k: v for k, v in _L3_gnn_all.items() if k in ('W1', 'b1', 'W2', 'b2')}
    del _L3_gnn_all
    return {'x': x, 'src': src, 'dst': dst, 'edge_type_500': edge_type_500, 'L0_gnn_rel_emb': _L0_gnn_in['rel_emb'], 'L0_gnn_W_neighbor': _L0_gnn_in['W_neighbor'], 'L0_gnn_loop_weight': _L0_gnn_in['loop_weight'], 'L1_gnn_query_kernel': _L1_gnn_in['query_kernel'], 'L1_gnn_query_bias': _L1_gnn_in['query_bias'], 'L1_gnn_key_kernel': _L1_gnn_in['key_kernel'], 'L1_gnn_key_bias': _L1_gnn_in['key_bias'], 'L1_gnn_kernel': _L1_gnn_in['kernel'], 'L1_gnn_bias': _L1_gnn_in['bias'], 'L2_gnn_weight': _L2_gnn_in['weight'], 'L3_gnn_W1': _L3_gnn_in['W1'], 'L3_gnn_b1': _L3_gnn_in['b1'], 'L3_gnn_W2': _L3_gnn_in['W2'], 'L3_gnn_b2': _L3_gnn_in['b2']}

def reference(x, src, dst, edge_type_500, L0_gnn_rel_emb, L0_gnn_W_neighbor, L0_gnn_loop_weight, L1_gnn_query_kernel, L1_gnn_query_bias, L1_gnn_key_kernel, L1_gnn_key_bias, L1_gnn_kernel, L1_gnn_bias, L2_gnn_weight, L3_gnn_W1, L3_gnn_b1, L3_gnn_W2, L3_gnn_b2):
    import jax
    import jax.numpy as jnp

    def _L0_gnn_ref(h, norm, rel_emb, W_neighbor, loop_weight, edge_src, edge_dst, edge_type):
        import jax, jax.numpy as jnp
        import numpy as np
        N_NODES = 50000
        N_EDGES = 18750
        N_RELS = 500
        D = 128
        loop_message = h @ loop_weight
        relation = rel_emb[edge_type]
        node = h[edge_src]
        msg = (node + relation) @ W_neighbor
        agg = jax.ops.segment_sum(msg, edge_dst, num_segments=h.shape[0])
        node_repr = agg * norm
        node_repr = jax.nn.relu(node_repr + loop_message)
        return node_repr

    def _L1_gnn_ref(x, edge_index, query_kernel, query_bias, key_kernel, key_bias, kernel, bias):
        import jax, jax.numpy as jnp
        import numpy as np
        N = 50000
        E = 25000
        F = 128
        UNITS = 128
        ATT_UNITS = 128
        HEADS = 8

        def segment_softmax(scores, seg, num_segments):
            smax = jax.ops.segment_max(scores, seg, num_segments=num_segments)
            sexp = jnp.exp(scores - smax[seg])
            ssum = jax.ops.segment_sum(sexp, seg, num_segments=num_segments)
            return sexp / ssum[seg]
        num_nodes = x.shape[0]
        loop = jnp.arange(num_nodes, dtype=edge_index.dtype)
        row = jnp.concatenate([edge_index[0], loop])
        col = jnp.concatenate([edge_index[1], loop])
        Q = jax.nn.relu(x @ query_kernel + query_bias)[row]
        K = jax.nn.relu(x @ key_kernel + key_bias)[col]
        V = (x @ kernel)[col]
        Qh = Q.reshape(-1, HEADS, ATT_UNITS // HEADS)
        Kh = K.reshape(-1, HEADS, ATT_UNITS // HEADS)
        att = jnp.sum(Qh * Kh, axis=-1)
        alpha = segment_softmax(att, row, num_nodes)
        Vh = V.reshape(-1, HEADS, UNITS // HEADS)
        msg = Vh * alpha[:, :, None]
        out = jax.ops.segment_sum(msg, row, num_segments=num_nodes)
        out = out.reshape(num_nodes, UNITS)
        out = out + bias
        return out

    def _L2_gnn_ref(feat, weight, src, dst):
        import jax, jax.numpy as jnp
        import numpy as np
        N_NODES = 3125
        N_EDGES = 50000
        D_IN = 128
        D_OUT = 128
        n = feat.shape[0]
        ones = jnp.ones(src.shape[0], dtype=feat.dtype)
        out_deg = jnp.clip(jax.ops.segment_sum(ones, src, num_segments=n), 1.0)
        feat_src = feat * (out_deg ** (-0.5))[:, None]
        agg = jax.ops.segment_sum(feat_src[src], dst, num_segments=n)
        rst = agg @ weight
        in_deg = jnp.clip(jax.ops.segment_sum(ones, dst, num_segments=n), 1.0)
        rst = rst * (in_deg ** (-0.5))[:, None]
        return rst

    def _L3_gnn_ref(x, edge_index, W1, b1, W2, b2):
        import jax, jax.numpy as jnp
        import numpy as np
        N_NODES = 50000

        def _gcn_norm(edge_index, num_nodes):
            loop = jnp.arange(num_nodes, dtype=edge_index.dtype)
            src = jnp.concatenate([edge_index[0], loop])
            dst = jnp.concatenate([edge_index[1], loop])
            deg = jax.ops.segment_sum(jnp.ones_like(dst, dtype=jnp.float32), dst, num_segments=num_nodes)
            dinv = jnp.where(deg > 0, jax.lax.rsqrt(deg), 0.0)
            norm = dinv[src] * dinv[dst]
            return (src, dst, norm)

        def _gcn_layer(x, W, b, src, dst, norm, num_nodes):
            h = x @ W
            msg = h[src] * norm[:, None]
            agg = jax.ops.segment_sum(msg, dst, num_segments=num_nodes)
            return agg + b
        N = x.shape[0]
        src, dst, norm = _gcn_norm(edge_index, N)
        x = jax.nn.relu(_gcn_layer(x, W1, b1, src, dst, norm, N))
        x = _gcn_layer(x, W2, b2, src, dst, norm, N)
        return x
    edge_index = jnp.stack([src, dst])
    deg = jnp.maximum(jax.ops.segment_sum(jnp.ones(dst.shape, jnp.float32), dst, num_segments=3125), 1.0)
    deg_isqrt = deg ** (-0.5)
    x = _layernorm(x + _L0_gnn_ref(x, deg_isqrt[:, None], L0_gnn_rel_emb, L0_gnn_W_neighbor, L0_gnn_loop_weight, src, dst, edge_type_500), axis=-1)
    x = _layernorm(x + _L1_gnn_ref(x, edge_index, L1_gnn_query_kernel, L1_gnn_query_bias, L1_gnn_key_kernel, L1_gnn_key_bias, L1_gnn_kernel, L1_gnn_bias), axis=-1)
    x = _layernorm(x + _L2_gnn_ref(x, L2_gnn_weight, src, dst), axis=-1)
    x = _layernorm(x + _L3_gnn_ref(x, edge_index, L3_gnn_W1, L3_gnn_b1, L3_gnn_W2, L3_gnn_b2), axis=-1)
    return x

_drawn_inputs = setup_inputs


def setup_inputs(seed=0):
    import zlib

    import numpy as np

    out = dict(_drawn_inputs(seed))
    spreads = {'L1_gnn_query_bias': (0.0, 0.1),
     'L1_gnn_key_bias': (0.0, 0.304),
     'L1_gnn_bias': (0.0, 0.1),
     'L3_gnn_b1': (0.0, 0.1),
     'L3_gnn_b2': (0.0, 0.1)}
    factors = {}
    for name, (base, spread) in spreads.items():
        noise = np.random.default_rng([zlib.crc32(name.encode()), seed]).standard_normal(out[name].shape)
        drawn = base * np.exp(spread * noise) if base else spread * noise
        out[name] = jnp.asarray(drawn.astype(out[name].dtype))
    for name, factor in factors.items():
        out[name] = (out[name] * factor).astype(out[name].dtype)
    return out
```

```python
import concourse.bass as bass
from concourse import mybir
from contextlib import ExitStack

F32, BF16, F16, I32 = mybir.dt.float32, mybir.dt.bfloat16, mybir.dt.float16, mybir.dt.int32
ALU = mybir.AluOpType
ACT = mybir.ActivationFunctionType
AX = mybir.AxisListType
ds = bass.ds

N = 3125
E = 100000
D = 128
P = 128
NREL = 500
SB = -(-N // P)
TB = -(-NREL // P)
CW = 448
NC = -(-N // CW)
NP = NC * CW
EPS = 1e-5
RB = 112
RPC = CW // RB
NRB = NP // RB
W = 12
ND = SB * P
TG = 112
NG = 7
NT = TG * NG
TF = E // P
TR = E - TF * P
U = 4
NU = NT // U


class Steps:

    def __init__(self, eng, sem, base=0):
        self.eng, self.sem, self.base, self.n = eng, sem, base, 0

    def done(self, ins):
        self.n += 1
        ins.then_inc(self.sem, 1)

    def done_here(self):
        self.n += 1
        self.eng.sem_inc(self.sem, 1)

    def wait(self):
        self.eng.wait_ge(self.sem, self.base + self.n)

    def link(self, ins):
        self.done(ins)
        self.wait()


def hold(eng, sem, value, passed):
    eng.wait_ge(sem, value)
    eng.sem_inc(passed, 1)


class Mem:
    pass


def allocate(nc, ctx):
    m = Mem()
    sb = lambda name, shape, dt: ctx.enter_context(nc.sbuf_tensor(name, shape, dt))
    m.ident = sb("ident", [P, P], F32)
    m.identb = sb("identb", [P, P], BF16)
    m.eps = sb("eps", [P, RPC], F32)
    m.passed = ctx.enter_context(nc.semaphore("passed"))
    m.minus_half = sb("minus_half", [P, SB + NRB], F32)
    m.ps = ctx.enter_context(nc.psum_tensor("ps", [P, 8, 512], F32))
    m.bank = [m.ps[:, i, :] for i in range(8)]
    return m


def edge_tables(nc, m, src, dst, typ, base_d, t):
    with ExitStack() as ctx:
        sb = lambda name, shape, dt: ctx.enter_context(nc.sbuf_tensor(name, shape, dt))
        flat = m.at[:, :, :].rearrange("p b d -> p (b d)")[0:TG, :].bitcast(F32)
        size, at = NG * P, [0]

        def carve(k, dt):
            at[0] += k * size
            return flat[:, at[0] - k * size:at[0]].bitcast(dt).rearrange("p (k g e) -> p k g e", k=k, e=P)

        raw = carve(3, I32)
        low = carve(2, I32)
        blk = carve(2, I32)
        fl = carve(7, F32)
        dstf = carve(1, F32)[:, 0]
        bf = carve(2, F32)
        mn = sb("mn", [TG, NG], F32)
        mx = sb("mx", [TG, NG], F32)
        mni = sb("mni", [TG, NG], I32)
        span = sb("span", [TG, NG], F32)
        worst = sb("worst", [TG, 1], F32)
        badf = sb("badf", [1, 1], F32)
        loaded = ctx.enter_context(nc.semaphore("edges_loaded"))
        based = ctx.enter_context(nc.semaphore("bases_stored"))
        baseb = ctx.enter_context(nc.semaphore("bases_back"))
        ready = ctx.enter_context(nc.semaphore("tables_ready"))
        mnready = ctx.enter_context(nc.semaphore("mins_ready"))
        idr = ctx.enter_context(nc.semaphore("ident_ready"))
        turned = ctx.enter_context(nc.semaphore("tables_turned"))
        freed = ctx.enter_context(nc.semaphore("banks_freed"))
        dstep = ctx.enter_context(nc.semaphore("dve_step"))
        zeroed = ctx.enter_context(nc.semaphore("pool_step"))
        block = ctx.enter_context(nc.Block())
        G6 = (NG - 1) * TG * P

        @block.sync
        def _(sp):
            for k, a in enumerate((dst, src, typ)):
                sp.dma_start(raw[:, k, 0:NG - 1, :],
                             a[0:G6].rearrange("(g p e) -> p g e", g=NG - 1, e=P)).then_inc(loaded, 16)
                sp.dma_start(raw[0:TF - (NG - 1) * TG, k, NG - 1, :],
                             a[G6:TF * P].rearrange("(p e) -> p e", e=P)).then_inc(loaded, 16)
                r = TF - (NG - 1) * TG
                sp.dma_start(raw[r:r + 1, k, NG - 1, 0:TR], a[TF * P:E].rearrange("(p e) -> p e", p=1))\
                  .then_inc(loaded, 16)
                sp.dma_start(raw[r:r + 1, k, NG - 1, TR:P], a[E - P + TR:E].rearrange("(p e) -> p e", p=1))\
                  .then_inc(loaded, 16)
                for q in range(r + 1, TG):
                    sp.dma_start(raw[q:q + 1, k, NG - 1, :], a[E - P:E].rearrange("(p e) -> p e", p=1))\
                      .then_inc(loaded, 16)
            sp.wait_ge(mnready, 1)
            sp.dma_start(base_d.rearrange("(g p) -> p g", p=TG), mni[:, :],
                         allow_slow_non_contiguous=True).then_inc(based, 16)
            sp.wait_ge(based, 16)
            sp.dma_start(t.base[0:1, :], base_d.rearrange("(a n) -> a n", a=1)).then_inc(baseb, 16)
            sp.wait_ge(baseb, 16)

        @block.gpsimd
        def _(pool):
            pool.memset(m.ident[:, :], 0.0)
            pool.memset(m.identb[:, :], 0.0).then_inc(zeroed, 1)
            pool.wait_ge(zeroed, 1)
            pool.affine_select(out=m.ident[:, :], in_=m.ident[:, :], compare_op=ALU.not_equal, fill=1.0,
                               base=0, pattern=[[-1, P]], channel_multiplier=1).then_inc(idr, 1)
            pool.memset(m.minus_half[:, :], -0.5)
            pool.memset(m.eps[:, :], EPS)
            pool.affine_select(out=m.identb[:, :], in_=m.identb[:, :], compare_op=ALU.not_equal, fill=1.0,
                               base=0, pattern=[[-1, P]], channel_multiplier=1)
            pool.iota(t.iota[:, :], [[1, W * SB]], base=0, channel_multiplier=0,
                      allow_small_or_imprecise_dtypes=True)

        @block.vector
        def _(v):
            s = Steps(v, dstep)
            v.wait_ge(loaded, 16 * 3 * (4 + TG - 1 - (TF - (NG - 1) * TG)))
            for k in range(2):
                s.done(v.tensor_single_scalar(blk[:, k], raw[:, 1 + k], 7, op=ALU.arith_shift_right))
                s.done(v.tensor_single_scalar(low[:, k], raw[:, 1 + k], P - 1, op=ALU.bitwise_and))
            s.link(v.tensor_copy(dstf[:, :, :], raw[:, 0]))
            s.done(v.tensor_copy(bf[:, :], blk[:, :]))
            s.done(v.tensor_copy(fl[:, 2:4], low[:, :]))
            s.done(v.tensor_reduce(mn[:, :], dstf[:, :, :], axis=AX.X, op=ALU.min))
            s.link(v.tensor_reduce(mx[:, :], dstf[:, :, :], axis=AX.X, op=ALU.max))
            s.done(v.tensor_copy(mni[:, :], mn[:, :]))
            s.link(v.tensor_tensor(span[:, :], mx[:, :], mn[:, :], op=ALU.subtract))
            s.link(v.tensor_reduce(worst[:, :], span[:, :], axis=AX.X, op=ALU.max))
            nb = mn[:, :].unsqueeze(2).to_broadcast([TG, NG, P])
            s.done(v.tensor_copy(fl[:, 4], dstf[:, :, :]))
            s.done(v.tensor_single_scalar(fl[:, 5:7], bf[:, :], float(W), op=ALU.mult))
            v.memset(badf[:, :], 0.0).then_inc(mnready, 1)
            s.wait()
            s.link(v.tensor_tensor(dstf[:, :, :], dstf[:, :, :], nb, op=ALU.subtract))
            s.done(v.scalar_tensor_tensor(fl[:, 0], bf[:, 0], float(W), dstf[:, :, :], op0=ALU.mult, op1=ALU.add))
            v.scalar_tensor_tensor(fl[:, 1], bf[:, 1], float(W), dstf[:, :, :], op0=ALU.mult, op1=ALU.add)\
             .then_inc(ready, 1)
            for j in range(14):
                k, h = j // 2, j % 2
                n = 4 * TG if h == 0 else 3 * TG
                v.wait_ge(turned, j + 1)
                v.tensor_copy(t.key[k][:, h * 4 * TG:h * 4 * TG + n], m.bank[j % 6][:, 0:n]).then_inc(freed, 1)
            v.wait_ge(freed, 14)
            for k in (2, 3):
                s.done(v.memset(t.key[k][TR:64, TF:TF + 1], -1.0))
                s.done(v.memset(t.key[k][64:P, TF:TF + 1], -1.0))
                s.done(v.memset(t.key[k][:, TF + 1:NT], -1.0))
            v.wait_ge(turned, 15)
            s.link(v.tensor_reduce(badf[:, :], m.bank[7][0:1, 0:TG], axis=AX.X, op=ALU.max))
            s.link(v.tensor_single_scalar(badf[:, :], badf[:, :], float(W - 1), op=ALU.is_gt))
            s.link(v.tensor_copy(t.bad[0:1, 0:1], badf[:, :]))

        @block.tensor
        def _(pe):
            pe.wait_ge(idr, 1)
            pe.wait_ge(ready, 1)
            for j in range(14):
                k, h = j // 2, j % 2
                if j >= 6:
                    pe.wait_ge(freed, j - 5)
                for g in range(4 if h == 0 else 3):
                    last = nc.tensor.transpose(m.bank[j % 6][:, g * TG:(g + 1) * TG], fl[:, k, 4 * h + g, :],
                                               m.ident[0:TG, 0:TG])
                last.then_inc(turned, 1)
            nc.tensor.transpose(m.bank[7][0:1, 0:TG], worst[:, 0:1], m.ident[0:TG, 0:TG]).then_inc(turned, 1)


def count_edges(nc, m, t):
    with ExitStack() as ctx:
        sb = lambda name, shape, dt: ctx.enter_context(nc.sbuf_tensor(name, shape, dt))
        widths = (W * SB, W * TB, P, P)
        hot = [[sb(f"hot{k}{h}", [P, U, n], BF16) for h in range(2)] for k, n in enumerate(widths)]
        names = ("hot_ready mm_done bank_free src_added any_keys any_hot any_used any_summed any_copied").split()
        (hot_ready, mm_done, bank_free, src_added, any_keys, any_hot, any_used, any_summed, any_copied) = \
            (ctx.enter_context(nc.semaphore(n)) for n in names)
        block = ctx.enter_context(nc.Block())
        NW = -(-N // W)

        @block.vector
        def _(v):
            v.sem_inc(any_copied, 1)
            v.memset(m.at[:, :, :].bitcast(F32), 0.0).then_inc(bank_free, 2 * U - 1)
            v.memset(t.rt[:, :, :].bitcast(F32), 0.0).then_inc(bank_free, 1)
            v.wait_ge(bank_free, 2 * U)
            v.sem_inc(src_added, 1)

            def one_hots(r, h, ready):
                for k in range(4):
                    n = widths[k]
                    last = v.tensor_tensor(hot[k][h][:, :, :],
                                           t.iota[:, 0:n].unsqueeze(1).to_broadcast([P, U, n]),
                                           t.key[k][:, ds(U * r, U)].unsqueeze(2).to_broadcast([P, U, n]),
                                           op=ALU.is_equal)
                last.then_inc(ready, 1)

            def add(r, h):
                _, base = nc.values_load_multi_w_load_instructions(
                    t.base[0:1, ds(U * r, U)], engines=(mybir.EngineType.DVE,), min_val=0, max_val=N - 1,
                    skip_runtime_bounds_check_because="minima of node numbers")
                for u in range(U):
                    v.wait_ge(mm_done, U * r + u + 1)
                    v.wait_ge(src_added, U * r + u + 1)
                    wa = m.at[:, :, ds(base[u], W)]
                    v.tensor_tensor(wa, wa, m.bank[U * h + u][:, 0:W * SB].rearrange("p (b d) -> p b d", d=W),
                                    op=ALU.add).then_inc(src_added, 1)
                    v.wait_ge(bank_free, U * r + 2 * U + u)
                    wr = t.rt[:, :, ds(base[u], W)]
                    v.tensor_tensor(wr, wr, m.bank[U * h + u][:, W * SB:W * (SB + TB)]
                                    .rearrange("p (b d) -> p b d", d=W), op=ALU.add).then_inc(bank_free, 1)

            bad = v.value_load(t.bad[0:1, 0:1], min_val=0, max_val=1)
            with v.If(bad == 0):
                one_hots(0, 0, hot_ready)
                with v.Fori(0, NU // 2 - 1) as i:
                    one_hots(2 * i + 1, 1, hot_ready)
                    add(2 * i, 0)
                    one_hots(2 * i + 2, 0, hot_ready)
                    add(2 * i + 1, 1)
                one_hots(NU - 1, 1, hot_ready)
                add(NU - 2, 0)
                add(NU - 1, 1)
            with v.Else():
                FAR = 10000.0
                v.sem_inc(any_used, 2)
                with v.Fori(0, NW) as w:
                    s = Steps(v, any_keys, 8 * w)
                    v.wait_ge(any_used, NU * w + 2)
                    s.done(v.tensor_scalar(t.key[0][:, :], t.key[4][:, :], float(W), FAR, op0=ALU.is_ge, op1=ALU.mult))
                    s.link(v.tensor_scalar(t.key[1][:, :], t.key[4][:, :], 0.0, FAR, op0=ALU.is_lt, op1=ALU.mult))
                    s.link(v.tensor_tensor(t.key[0][:, :], t.key[0][:, :], t.key[1][:, :], op=ALU.add))
                    s.link(v.tensor_tensor(t.key[0][:, :], t.key[0][:, :], t.key[4][:, :], op=ALU.add))
                    s.link(v.tensor_tensor(t.key[1][:, :], t.key[0][:, :], t.key[6][:, :], op=ALU.add))
                    s.link(v.tensor_tensor(t.key[0][:, :], t.key[0][:, :], t.key[5][:, :], op=ALU.add))
                    s.link(v.tensor_single_scalar(t.key[4][:, :], t.key[4][:, :], float(-W), op=ALU.add))
                    s.done_here()
                    with v.Fori(0, NU // 2) as i:
                        for h in range(2):
                            v.wait_ge(any_used, NU * w + 2 * i + h + 1)
                            one_hots(2 * i + h, h, any_hot)
                    v.wait_ge(any_summed, w + 1)
                    v.tensor_copy(m.at[:, :, ds(w * W, W)],
                                  m.bank[0][:, 0:W * SB].rearrange("p (b d) -> p b d", d=W))
                    v.tensor_copy(t.rt[:, :, ds(w * W, W)],
                                  m.bank[1][:, 0:W * TB].rearrange("p (b d) -> p b d", d=W)).then_inc(any_copied, 1)

        @block.tensor
        def _(pe):
            bad = pe.value_load(t.bad[0:1, 0:1], min_val=0, max_val=1)
            with pe.If(bad == 0):
                with pe.Fori(0, NU // 2) as i:
                    for h in range(2):
                        r = 2 * i + h
                        pe.wait_ge(hot_ready, r + 1)
                        for u in range(U):
                            pe.wait_ge(bank_free, U * r + u + 1)
                            nc.tensor.matmul(m.bank[U * h + u][:, 0:W * SB], hot[2][h][:, u, :],
                                             hot[0][h][:, u, :], start=True, stop=True)
                            nc.tensor.matmul(m.bank[U * h + u][:, W * SB:W * (SB + TB)], hot[3][h][:, u, :],
                                             hot[1][h][:, u, :], start=True, stop=True).then_inc(mm_done, 1)
            with pe.Else():
                with pe.Fori(0, NW) as w:
                    pe.wait_ge(any_copied, 1 + w)

                    def pair(i, first, final):
                        for h in range(2):
                            pe.wait_ge(any_hot, NU * w + 2 * i + h + 1)
                            for u in range(U):
                                start, stop = first and h + u == 0, final and h == 1 and u == U - 1
                                nc.tensor.matmul(m.bank[0][:, 0:W * SB], hot[2][h][:, u, :],
                                                 hot[0][h][:, u, :], start=start, stop=stop)
                                last = nc.tensor.matmul(m.bank[1][:, 0:W * TB], hot[3][h][:, u, :],
                                                        hot[1][h][:, u, :], start=start, stop=stop)
                            last.then_inc(any_used, 1)

                    pair(0, True, False)
                    with pe.Fori(1, NU // 2 - 1) as i:
                        pair(i, False, False)
                    pair(NU // 2 - 1, False, True)
                    pe.sem_inc(any_summed, 1)


def chunk_rows(a, c):
    return a[ds(c * CW, CW), :].rearrange("(j p) f -> p j f", p=RB)


def split3(v, s, parts, x):
    s.link(v.tensor_copy(parts[0], x))
    s.link(v.tensor_tensor(x, x, parts[0], op=ALU.subtract))
    s.link(v.tensor_copy(parts[1], x))
    s.link(v.tensor_tensor(parts[2], x, parts[1], op=ALU.subtract))


def load_and_split(nc, m, tag, rows, scale, parts):
    with ExitStack() as ctx:
        x = ctx.enter_context(nc.sbuf_tensor(f"{tag}_split_x", [P, SB, D], F32))
        loaded = ctx.enter_context(nc.semaphore(f"{tag}_all_loaded"))
        step = ctx.enter_context(nc.semaphore(f"{tag}_split_step"))
        block = ctx.enter_context(nc.Block())

        @block.sync
        def _(sp):
            sp.dma_start(x[:, :, :], rows.rearrange("(b p) f -> p b f", p=P)).then_inc(loaded, 16)

        @block.vector
        def _(v):
            s = Steps(v, step)
            v.wait_ge(loaded, 16)
            if scale is not None:
                s.link(v.tensor_tensor(x[:, :, :], x[:, :, :], scale[:, :].unsqueeze(2).to_broadcast([P, SB, D]),
                                       op=ALU.mult))
            split3(v, s, [q[:, :, :] for q in parts], x[:, :, :])


def relation_sums(nc, m, t, rel, aggr_d):
    with ExitStack() as ctx:
        sb = lambda name, shape, dt: ctx.enter_context(nc.sbuf_tensor(name, shape, dt))
        x = sb("rel_x", [P, TB, D], F32)
        parts = [sb(f"rel_part{k}", [P, TB, D], BF16) for k in range(3)]
        out = sb("rel_out", [P, CW], F32)
        loaded = ctx.enter_context(nc.semaphore("rel_loaded"))
        zeroed = ctx.enter_context(nc.semaphore("rel_zeroed"))
        step = ctx.enter_context(nc.semaphore("rel_step"))
        split = ctx.enter_context(nc.semaphore("rel_split"))
        summed = ctx.enter_context(nc.semaphore("rel_summed"))
        copied = ctx.enter_context(nc.semaphore("rel_copied"))
        stored = ctx.enter_context(nc.semaphore("rel_stored"))
        out_free = ctx.enter_context(nc.semaphore("rel_out_free"))
        block = ctx.enter_context(nc.Block())
        full = NREL // P

        @block.sync
        def _(sp):
            sp.sem_inc(out_free, 1)
            sp.wait_ge(zeroed, 1)
            sp.dma_start(x[:, 0:full, :], rel[0:full * P, :].rearrange("(b p) f -> p b f", p=P))\
              .then_inc(loaded, 16)
            sp.dma_start(x[0:NREL - full * P, full, :], rel[full * P:NREL, :]).then_inc(loaded, 16)
            with sp.Fori(0, NC) as c:
                hold(sp, copied, 1 + c + 1, m.passed)
                sp.dma_start(aggr_d[:, ds(c * CW, CW)], out[:, :]).then_inc(stored, 16)
                hold(sp, stored, 16 * (c + 1), m.passed)
                sp.sem_inc(out_free, 1)

        @block.vector
        def _(v):
            v.sem_inc(copied, 1)
            s = Steps(v, step)
            v.memset(x[:, :, :], 0.0).then_inc(zeroed, 1)
            v.wait_ge(loaded, 32)
            split3(v, s, [q[:, :, :] for q in parts], x[:, :, :])
            v.memset(out[:, 0:1], 0.0).then_inc(split, 1)
            with v.Fori(0, NC) as c:
                v.wait_ge(summed, c + 1)
                v.wait_ge(out_free, c + 1)
                v.tensor_copy(out[:, :], m.bank[0][:, 0:CW]).then_inc(copied, 1)

        @block.tensor
        def _(pe):
            pe.wait_ge(split, 1)
            with pe.Fori(0, NC) as c:
                pe.wait_ge(copied, 1 + c)
                for k in range(3):
                    for b in range(TB):
                        last = nc.tensor.matmul(m.bank[0][:, 0:CW], parts[k][:, b, :],
                                                t.rt[:, b, ds(c * CW, CW)],
                                                start=k + b == 0, stop=k == 2 and b == TB - 1)
                last.then_inc(summed, 1)


def degrees(nc, m, deg_d):
    with ExitStack() as ctx:
        sb = lambda name, shape, dt: ctx.enter_context(nc.sbuf_tensor(name, shape, dt))
        ones = sb("deg_ones", [P, 1], BF16)
        row = sb("deg_row", [1, ND], F32)
        junk = sb("deg_junk", [P, NP], BF16)
        outdeg = sb("out_deg", [P, SB], F32)
        rowed = ctx.enter_context(nc.semaphore("deg_rowed"))
        oned = ctx.enter_context(nc.semaphore("deg_oned"))
        summed = ctx.enter_context(nc.semaphore("deg_summed"))
        stored = ctx.enter_context(nc.semaphore("deg_stored"))
        loaded = ctx.enter_context(nc.semaphore("deg_loaded"))
        outed = ctx.enter_context(nc.semaphore("deg_outed"))
        clipped = ctx.enter_context(nc.semaphore("deg_clipped"))
        block = ctx.enter_context(nc.Block())

        @block.sync
        def _(sp):
            sp.wait_ge(rowed, NC + 2)
            sp.dma_start(deg_d.rearrange("(a n) -> a n", a=1), row[:, :]).then_inc(stored, 16)
            sp.wait_ge(stored, 16)
            with nc.allow_non_contiguous_dma(reason="one short vector"):
                sp.dma_start(m.in_norm[:, :], deg_d[0:NP].rearrange("(b p) -> p b", p=RB)).then_inc(loaded, 16)
                sp.dma_start(m.loop_norm[:, :], deg_d[0:NP].rearrange("(b p) -> p b", p=RB)).then_inc(loaded, 16)
                sp.dma_start(m.loop_norm_s[:, :], deg_d.rearrange("(b p) -> p b", p=P)).then_inc(loaded, 16)
            sp.wait_ge(loaded, 48)

        @block.tensor
        def _(pe):
            pe.wait_ge(oned, 1)
            with pe.Fori(0, NC) as c:
                pe.wait_ge(rowed, c + 1)
                for b in range(SB):
                    last = nc.tensor.matmul(m.bank[0][0:1, 0:CW], ones[:, 0:1], m.at[:, b, ds(c * CW, CW)],
                                            start=b == 0, stop=b == SB - 1)
                last.then_inc(summed, 1)

        @block.scalar
        def _(act):
            for b in range(SB):
                if b:
                    act.wait_ge(outed, b)
                nc.scalar.activation(junk[:, :], m.at[:, b, 0:NP], ACT.Copy, accum_out=outdeg[:, b:b + 1])\
                  .then_inc(outed, 1)

        @block.gpsimd
        def _(pool):
            pool.wait_ge(clipped, 4)
            for a in (m.in_norm, m.loop_norm, m.loop_norm_s, m.out_norm):
                pool.tensor_tensor(a[:, :], a[:, :], m.minus_half[0:a.shape[0], 0:a.shape[1]], op=ALU.pow)

        @block.vector
        def _(v):
            v.memset(ones[:, :], 1.0).then_inc(oned, 1)
            v.memset(row[:, :], 0.0).then_inc(rowed, 1)
            v.wait_ge(rowed, 1)
            with v.Fori(0, NC) as c:
                v.wait_ge(summed, c + 1)
                v.tensor_copy(row[0:1, ds(c * CW, CW)], m.bank[0][0:1, 0:CW]).then_inc(rowed, 1)
            v.memset(ones[:, :], 1.0).then_inc(rowed, 1)
            v.wait_ge(loaded, 48)
            v.wait_ge(outed, SB)
            v.tensor_single_scalar(m.in_norm[:, :], m.in_norm[:, :], 1.0, op=ALU.max).then_inc(clipped, 1)
            v.tensor_single_scalar(m.loop_norm[:, :], m.loop_norm[:, :], 1.0, op=ALU.add).then_inc(clipped, 1)
            v.tensor_single_scalar(m.loop_norm_s[:, :], m.loop_norm_s[:, :], 1.0, op=ALU.add).then_inc(clipped, 1)
            v.tensor_single_scalar(m.out_norm[:, :], outdeg[:, :], 1.0, op=ALU.max).then_inc(clipped, 1)


def layer_norm(v, s, m, y, o, st, mv, sd, normed, rooted, c):
    for j in range(RPC):
        s.done(v.bn_stats(st[:, j, :], y[:, j, :]))
    s.wait()
    s.done_here()
    for j in range(RPC):
        last = v.bn_aggr(mv[:, j, :], st[:, j, :])
    last.then_inc(normed, 1)
    v.wait_ge(rooted, 2 * c + 2)
    for j in range(RPC):
        last = v.tensor_scalar(o[:, j, :], y[:, j, :], mv[:, j, 0:1], sd[:, j:j + 1],
                               op0=ALU.subtract, op1=ALU.mult)
    return last


def inverse_roots(pool, m, mv, sd, normed, rooted, c):
    pool.wait_ge(normed, c + 1)
    pool.tensor_tensor(sd[:, :], mv[:, :, 1], m.eps[0:RB, :], op=ALU.add).then_inc(rooted, 1)
    pool.wait_ge(rooted, 2 * c + 1)
    pool.tensor_tensor(sd[:, :], sd[:, :], m.minus_half[0:RB, 0:RPC], op=ALU.pow).then_inc(rooted, 1)


def store_rows(sp, out, o, c, stored):
    if out.shape[0] >= NP or not isinstance(c, int) or c < NC - 1:
        sp.dma_start(chunk_rows(out, c), o[:, :, :]).then_inc(stored, 16)
        return 16
    full = (N - c * CW) // RB
    at = c * CW + full * RB
    sp.dma_start(out[c * CW:at, :].rearrange("(j p) f -> p j f", p=RB), o[:, 0:full, :]).then_inc(stored, 16)
    sp.dma_start(out[at:N, :], o[0:N - at, full, :]).then_inc(stored, 16)
    return 32


def graph_conv(nc, m, tag, parts, weight, post, out, residual=None, bias=None, loop_weight=None, aggr_d=None,
               relu=False, norm=True):
    with ExitStack() as ctx:
        sb = lambda name, shape, dt: ctx.enter_context(nc.sbuf_tensor(f"{tag}_{name}", shape, dt))
        w = sb("w", [P, D], F32)
        wl = sb("wl", [P, D], F32)
        bb = sb("bias", [RB, D], F32)
        aggt = sb("aggt", [P, CW], F32)
        aggr = sb("aggr", [P, CW], F32)
        xr = sb("xr", [RB, RPC, D], F32)
        xt = sb("xt", [P, CW], F32)
        y = sb("y", [RB, RPC, D], F32)
        o = sb("o", [RB, RPC, D], F32)
        st = sb("st", [RB, RPC, 6], F32)
        mv = sb("mv", [RB, RPC, 2], F32)
        sd = sb("sd", [RB, RPC], F32)
        names = ("w_loaded rows_loaded rows_used summed aggt_ready turned xt_ready mixed step "
                 "normed rooted finished stored out_free").split()
        sems = {n: ctx.enter_context(nc.semaphore(f"{tag}_{n}")) for n in names}
        (w_loaded, rows_loaded, rows_used, summed, aggt_ready, turned, xt_ready, mixed, step,
         normed, rooted, finished, stored, out_free) = (sems[n] for n in names)
        block = ctx.enter_context(nc.Block())
        nw = 1 + (bias is not None) + (loop_weight is not None)
        nl = (residual is not None) + (aggr_d is not None)
        bank_agg, bank_t, bank_rows, bank_loop = m.bank[0:4]

        @block.sync
        def _(sp):
            sp.sem_inc(out_free, 1)
            sp.dma_start(w[:, :], weight).then_inc(w_loaded, 16)
            if loop_weight is not None:
                sp.dma_start(wl[:, :], loop_weight).then_inc(w_loaded, 16)
            if bias is not None:
                sp.dma_start(bb[:, :], bias.unsqueeze(0).to_broadcast([RB, D])).then_inc(w_loaded, 16)

            def body(c):
                if nl:
                    hold(sp, rows_used, 1 + c, m.passed)
                if residual is not None:
                    sp.dma_start(xr[:, :, :], chunk_rows(residual, c)).then_inc(rows_loaded, 16)
                if aggr_d is not None:
                    sp.dma_start(aggr[:, :], aggr_d[:, ds(c * CW, CW)]).then_inc(rows_loaded, 16)
                hold(sp, finished, 1 + c + 1, m.passed)
                n = store_rows(sp, out, o, c, stored)
                sp.wait_ge(stored, 16 * c + n)
                sp.sem_inc(out_free, 1)

            with sp.Fori(0, NC - 1) as c:
                body(c)
            body(NC - 1)

        @block.tensor
        def _(pe):
            pe.sem_inc(mixed, 1)
            pe.wait_ge(w_loaded, 16 * nw)
            with pe.Fori(0, NC) as c:
                for k in range(3):
                    for b in range(SB):
                        last = nc.tensor.matmul(bank_agg[:, 0:CW], parts[k][:, b, :], m.at[:, b, ds(c * CW, CW)],
                                                start=k + b == 0, stop=k == 2 and b == SB - 1)
                last.then_inc(summed, 1)
                if loop_weight is not None:
                    pe.wait_ge(rows_loaded, 16 * nl * (c + 1))
                    for j in range(RPC):
                        last = nc.tensor.transpose(bank_t[:, j * RB:(j + 1) * RB], xr[:, j, :], m.ident[0:RB, 0:RB])
                    last.then_inc(turned, 1)
                    pe.wait_ge(xt_ready, c + 1)
                    pe.wait_ge(finished, 1 + c)
                    for j in range(RPC):
                        nc.tensor.matmul(bank_loop[0:RB, j * D:(j + 1) * D], xt[:, j * RB:(j + 1) * RB], wl[:, :],
                                         start=True, stop=True)
                pe.wait_ge(aggt_ready, c + 1)
                pe.wait_ge(finished, 1 + c)
                for j in range(RPC):
                    last = nc.tensor.matmul(bank_rows[0:RB, j * D:(j + 1) * D], aggt[:, j * RB:(j + 1) * RB],
                                            w[:, :], start=True, stop=True)
                last.then_inc(mixed, 1)

        @block.scalar
        def _(act):
            with act.Fori(0, NC) as c:
                if aggr_d is None:
                    act.wait_ge(summed, c + 1)
                    act.wait_ge(mixed, 1 + c)
                    nc.scalar.activation(aggt[:, :], bank_agg[:, 0:CW], ACT.Copy).then_inc(aggt_ready, 1)
                if loop_weight is not None:
                    act.wait_ge(turned, c + 1)
                    act.wait_ge(mixed, 1 + c)
                    nc.scalar.activation(xt[:, :], bank_t[:, 0:CW], ACT.Copy).then_inc(xt_ready, 1)

        @block.gpsimd
        def _(pool):
            if norm:
                with pool.Fori(0, NC) as c:
                    inverse_roots(pool, m, mv, sd, normed, rooted, c)

        @block.vector
        def _(v):
            v.sem_inc(finished, 1)
            v.sem_inc(rows_used, 1)
            flat = [RB, RPC, D]

            def body(c, s):
                if aggr_d is not None:
                    v.wait_ge(summed, c + 1)
                    v.wait_ge(rows_loaded, 16 * nl * (c + 1))
                    v.wait_ge(mixed, 1 + c)
                    v.tensor_tensor(aggt[:, :], aggr[:, :], bank_agg[:, 0:CW], op=ALU.add).then_inc(aggt_ready, 1)
                v.wait_ge(mixed, 1 + c + 1)
                rows = bank_rows[0:RB, :].rearrange("p (j f) -> p j f", f=D)
                s.link(v.tensor_tensor(y[:, :, :], rows, post[:, ds(c * RPC, RPC)].unsqueeze(2).to_broadcast(flat),
                                       op=ALU.mult))
                if bias is not None:
                    s.link(v.tensor_tensor(y[:, :, :], y[:, :, :], bb[:, :].unsqueeze(1).to_broadcast(flat),
                                           op=ALU.add))
                if loop_weight is not None:
                    s.link(v.tensor_tensor(y[:, :, :], y[:, :, :],
                                           bank_loop[0:RB, :].rearrange("p (j f) -> p j f", f=D), op=ALU.add))
                if relu:
                    s.link(v.tensor_single_scalar(y[:, :, :], y[:, :, :], 0.0, op=ALU.max))
                if residual is not None:
                    v.wait_ge(rows_loaded, 16 * nl * (c + 1))
                    s.link(v.tensor_tensor(y[:, :, :], y[:, :, :], xr[:, :, :], op=ALU.add))
                if nl:
                    v.sem_inc(rows_used, 1)
                v.wait_ge(out_free, c + 1)
                if norm:
                    layer_norm(v, s, m, y, o, st, mv, sd, normed, rooted, c).then_inc(finished, 1)
                else:
                    v.tensor_copy(o[:, :, :], y[:, :, :]).then_inc(finished, 1)
                return s.n

            v.wait_ge(w_loaded, 16 * nw)
            n = 1 + (bias is not None) + (loop_weight is not None) + relu + (residual is not None) + \
                (RPC + 1 if norm else 0)
            with v.Fori(0, NC) as c:
                s = Steps(v, step, n * c)
                assert body(c, s) == n


HEADS = 8
HD = D // HEADS
NX = 6
KS = NX * HD
KM = KS + 3
Q_PIECES = (0, 1, 0, 1, 2, 0)
K_PIECES = (0, 0, 1, 1, 0, 2)
VW = 32
DG = 5
NDG = SB // DG


def add_loops(nc, m, tag, sign):
    with ExitStack() as ctx:
        block = ctx.enter_context(nc.Block())

        @block.vector
        def _(v):
            for b in range(SB):
                a = m.at[:, b, b * P:(b + 1) * P]
                v.tensor_tensor(a, a, m.identb[:, :], op=ALU.add if sign > 0 else ALU.subtract)


def turn_counts(nc, m, ad):
    with ExitStack() as ctx:
        rows = [ctx.enter_context(nc.sbuf_tensor(f"turn_rows{h}", [P, ND], BF16)) for h in range(2)]
        turned = ctx.enter_context(nc.semaphore("turn_turned"))
        evac = [ctx.enter_context(nc.semaphore(f"turn_evac{h}")) for h in range(2)]
        stored = [ctx.enter_context(nc.semaphore(f"turn_stored{h}")) for h in range(2)]
        rows_free = [ctx.enter_context(nc.semaphore(f"turn_rows_free{h}")) for h in range(2)]
        block = ctx.enter_context(nc.Block())
        first, second = 16, SB - 16

        @block.tensor
        def _(pe):
            with pe.Fori(0, SB) as i:
                for half, (lo, n) in enumerate(((0, first), (first, second))):
                    pe.wait_ge(evac[half], i + 1)
                    for b in range(n):
                        last = nc.tensor.matmul(m.bank[4 * half + b // 4][:, (b % 4) * P:(b % 4 + 1) * P],
                                                m.at[:, lo + b, ds(i * P, P)], m.identb[:, :],
                                                start=True, stop=True)
                    last.then_inc(turned, 1)

        def copy_out(half, copy, wait, i, h):
            wait(turned, 2 * i + 1 + half)
            lo, n = ((0, first), (first, second))[half]
            full = n // 4
            copy(rows[h][:, lo * P:(lo + 4 * full) * P].rearrange("p (k n) -> p k n", n=512),
                 m.ps[:, 4 * half:4 * half + full, :], n % 4 == 0)
            if n % 4:
                copy(rows[h][:, (lo + 4 * full) * P:(lo + n) * P],
                     m.ps[:, 4 * half + full, 0:(n % 4) * P], True)

        @block.scalar
        def _(act):
            act.sem_inc(evac[0], 1)
            def copy(out, in_, last):
                ins = nc.scalar.activation(out, in_, ACT.Copy)
                if last:
                    ins.then_inc(evac[0], 1)

            def body(i, h, uses):
                act.wait_ge(rows_free[h], uses + 1)
                copy_out(0, copy, act.wait_ge, i, h)

            body(0, 0, 0)
            with act.Fori(0, SB // 2) as k:
                body(2 * k + 1, 1, k)
                body(2 * k + 2, 0, k + 1)

        @block.vector
        def _(v):
            v.sem_inc(evac[1], 1)
            def copy(out, in_, last):
                ins = v.tensor_copy(out, in_)
                if last:
                    ins.then_inc(evac[1], 1)

            def body(i, h, uses):
                v.wait_ge(rows_free[h], uses + 1)
                copy_out(1, copy, v.wait_ge, i, h)

            body(0, 0, 0)
            with v.Fori(0, SB // 2) as k:
                body(2 * k + 1, 1, k)
                body(2 * k + 2, 0, k + 1)

        @block.sync
        def _(sp):
            sp.sem_inc(rows_free[0], 1)
            sp.sem_inc(rows_free[1], 1)

            def body(i, h, uses):
                hold(sp, evac[0], 1 + i + 1, m.passed)
                hold(sp, evac[1], 1 + i + 1, m.passed)
                sp.dma_start(ad[ds(i * P, P), :], rows[h][:, 0:NP]).then_inc(stored[h], 16)
                hold(sp, stored[h], 16 * uses, m.passed)
                sp.sem_inc(rows_free[h], 1)

            body(0, 0, 1)
            with sp.Fori(0, SB // 2) as k:
                body(2 * k + 1, 1, k + 1)
                body(2 * k + 2, 0, k + 2)


def project(nc, m, x1, wq, bq, wk, bk, wv, qs, ks, vd):
    with ExitStack() as ctx:
        sb = lambda name, shape, dt: ctx.enter_context(nc.sbuf_tensor("prj_" + name, shape, dt))
        w = sb("w", [P, 3, D], F32)
        b2 = sb("b2", [P, 2], F32)
        xr = sb("xr", [RB, RPC, D], F32)
        xt = sb("xt", [P, CW], F32)
        qk = [sb(f"qk{k}", [P, CW], F32) for k in range(2)]
        pieces = [sb(f"pieces{k}", [P, 3, CW], BF16) for k in range(2)]
        vals = sb("vals", [RB, RPC, HEADS, VW], F32)
        onesb = sb("onesb", [3, ND], BF16)
        zeros = sb("zeros", [P, HEADS, ND - NP], BF16)
        zerov = sb("zerov", [ND - NP, HEADS * VW], F32)
        names = "w_loaded rows_loaded turned xt_ready made relued step split valued stored vset oned padded out_free".split()
        sems = {n: ctx.enter_context(nc.semaphore("prj_" + n)) for n in names}
        w_loaded, rows_loaded, turned, xt_ready, made, relued, step, split, valued, stored, vset, oned, \
            padded, out_free = \
            (sems[n] for n in names)
        block = ctx.enter_context(nc.Block())
        per = 2 * NX + 1

        @block.sync
        def _(sp):
            sp.sem_inc(out_free, 1)
            for k, a in enumerate((wq, wk, wv)):
                sp.dma_start(w[:, k, :], a).then_inc(w_loaded, 16)
            for k, a in enumerate((bq, bk)):
                sp.dma_start(b2[:, k:k + 1], a.rearrange("(p a) -> p a", a=1)).then_inc(w_loaded, 16)
            sp.wait_ge(oned, 1)
            for h in range(HEADS):
                sp.dma_start(ks[KS:KM, h, :], onesb[:, :]).then_inc(padded, 16)
            for a in (qs, ks):
                sp.dma_start(a[0:KS, :, NP:ND], zeros[0:KS, :, :]).then_inc(padded, 16)
            sp.dma_start(vd[NP:ND, :], zerov[:, :]).then_inc(padded, 16)
            with sp.Fori(0, NC) as c:
                hold(sp, turned, 1 + c, m.passed)
                sp.dma_start(xr[:, :, :], chunk_rows(x1, c)).then_inc(rows_loaded, 16)
                hold(sp, valued, 1 + c + 1, m.passed)
                sp.dma_start(vd[ds(c * CW, CW), :].rearrange("(j p) f -> p j f", p=RB),
                             vals[:, :, :, :].rearrange("p j h w -> p j (h w)")).then_inc(stored, 16)
                hold(sp, split, 1 + 2 * (c + 1), m.passed)
                for k, (pcs, a) in enumerate(((Q_PIECES, qs), (K_PIECES, ks))):
                    for g in range(NX):
                        sp.dma_start(a[g * HD:(g + 1) * HD, :, ds(c * CW, CW)].rearrange("r h n -> h r n"),
                                     pieces[k][:, pcs[g], :]).then_inc(stored, 16)
                hold(sp, stored, 16 * per * (c + 1), m.passed)
                sp.sem_inc(out_free, 1)
            sp.wait_ge(padded, 16 * (3 + HEADS))

        @block.tensor
        def _(pe):
            pe.sem_inc(turned, 1)
            pe.sem_inc(made, 1)
            pe.wait_ge(w_loaded, 80)
            with pe.Fori(0, NC) as c:
                pe.wait_ge(rows_loaded, 16 * (c + 1))
                for j in range(RPC):
                    last = nc.tensor.transpose(m.bank[0][:, j * RB:(j + 1) * RB], xr[:, j, :], m.ident[0:RB, 0:RB])
                last.then_inc(turned, 1)
                pe.wait_ge(xt_ready, c + 1)
                for k in range(2):
                    pe.wait_ge(relued, 1 + 2 * c)
                    nc.tensor.matmul(m.bank[1 + k][:, 0:CW], w[:, k, :], xt[:, :], start=True, stop=True)\
                      .then_inc(made, 1)
                pe.wait_ge(valued, 1 + c)
                for j in range(RPC):
                    last = nc.tensor.matmul(m.bank[3][0:RB, j * D:(j + 1) * D], xt[:, j * RB:(j + 1) * RB],
                                            w[:, 2, :], start=True, stop=True)
                last.then_inc(made, 1)

        @block.scalar
        def _(act):
            act.sem_inc(relued, 1)
            act.wait_ge(w_loaded, 80)
            with act.Fori(0, NC) as c:
                act.wait_ge(turned, 1 + c + 1)
                act.wait_ge(made, 1 + 3 * c)
                nc.scalar.activation(xt[:, :], m.bank[0][:, 0:CW], ACT.Copy).then_inc(xt_ready, 1)
                act.wait_ge(split, 1 + 2 * c)
                for k in range(2):
                    act.wait_ge(made, 1 + 3 * c + k + 1)
                    nc.scalar.activation(qk[k][:, :], m.bank[1 + k][:, 0:CW], ACT.Relu, bias=b2[:, k:k + 1])\
                      .then_inc(relued, 1)

        @block.vector
        def _(v):
            v.sem_inc(valued, 1)
            v.sem_inc(split, 1)
            v.memset(zeros[:, :, :], 0.0)
            v.memset(zerov[:, :], 0.0)
            v.memset(onesb[:, :], 1.0).then_inc(oned, 1)
            v.memset(vals[:, :, :, HD + 1:VW], 0.0)
            v.memset(vals[:, :, :, HD:HD + 1], 1.0).then_inc(vset, 1)
            v.wait_ge(vset, 1)
            with v.Fori(0, NC) as c:
                s = Steps(v, step, 6 * c)
                v.wait_ge(out_free, c + 1)
                for k in range(2):
                    v.wait_ge(relued, 1 + 2 * c + k + 1)
                    s.link(v.tensor_copy(pieces[k][:, 0, :], qk[k][:, :]))
                    s.link(v.tensor_tensor(qk[k][:, :], qk[k][:, :], pieces[k][:, 0, :], op=ALU.subtract))
                    s.link(v.tensor_copy(pieces[k][:, 1, :], qk[k][:, :]))
                    v.tensor_tensor(pieces[k][:, 2, :], qk[k][:, :], pieces[k][:, 1, :], op=ALU.subtract)\
                     .then_inc(split, 1)
                v.wait_ge(made, 1 + 3 * c + 3)
                v.tensor_copy(vals[:, :, :, 0:HD],
                              m.bank[3][0:RB, :].rearrange("p (j h f) -> p j h f", j=RPC, h=HEADS))\
                 .then_inc(valued, 1)


def score_maxima(nc, m, qs, ks):
    with ExitStack() as ctx:
        sb = lambda name, shape, dt: ctx.enter_context(nc.sbuf_tensor("max_" + name, shape, dt))
        HH = HEADS // 2
        mall = sb("mall", [P, SB, HEADS], F32)
        with ExitStack() as c2:
            sb2 = lambda name, shape, dt: c2.enter_context(nc.sbuf_tensor("max_" + name, shape, dt))
            kk = sb2("keys", [KS, HH, NP], BF16)
            q = [sb2(f"q{i}", [KS, HH, P], BF16) for i in range(2)]
            mask = sb2("mask", [P, NC, CW], BF16)
            junk = [sb2(f"junk{i}", [P, 4 - i, CW], BF16) for i in range(2)]
            mx = sb2("mx", [P, HH, 2], F32)
            names = "keys_loaded q_used scored maxed masked stepped".split()
            sems = {n: c2.enter_context(nc.semaphore("max_" + n)) for n in names}
            keys_loaded, q_used, scored, maxed, masked, stepped = (sems[n] for n in names)
            block = c2.enter_context(nc.Block())
            q_loaded = [c2.enter_context(nc.semaphore(f"max_q_loaded{i}")) for i in range(2)]
            banks = (slice(0, 4), slice(4, NC))
            per = 2 * HH

            @block.sync
            def _(sp):
                for hh in range(2):
                    at = hh * SB
                    if hh:
                        sp.wait_ge(q_used, SB + 1)
                    sp.dma_start(kk[:, :, :], ks[0:KS, hh * HH:(hh + 1) * HH, 0:NP]).then_inc(keys_loaded, 16)

                    def load(b, slot, used):
                        if used is not None:
                            hold(sp, q_used, used + 1, m.passed)
                        sp.dma_start(q[slot][:, :, :], qs[0:KS, hh * HH:(hh + 1) * HH, ds(b * P, P)])\
                          .then_inc(q_loaded[slot], 16)

                    load(0, at % 2, None if hh == 0 else at - 1)
                    with sp.Fori(0, SB // 2) as i:
                        load(2 * i + 1, (at + 1) % 2, at + 2 * i)
                        load(2 * i + 2, at % 2, at + 2 * i + 1)

            @block.tensor
            def _(pe):
                for hh in range(2):
                    at = hh * SB

                    def scores(b, slot, uses):
                        r = at + b
                        pe.wait_ge(q_loaded[slot], 16 * uses)
                        for h in range(HH):
                            for part in range(2):
                                pe.wait_ge(maxed, per * r + 2 * h + part + 1)
                                for k in range(4 - part):
                                    last = nc.tensor.matmul(m.bank[4 * part + k][:, 0:CW], q[slot][:, h, :],
                                                            kk[:, h, (4 * part + k) * CW:(4 * part + k + 1) * CW],
                                                            start=True, stop=True)
                                last.then_inc(scored, 1)

                    pe.wait_ge(keys_loaded, 16 * (hh + 1))
                    scores(0, at % 2, at // 2 + 1)
                    with pe.Fori(0, SB // 2) as i:
                        scores(2 * i + 1, (at + 1) % 2, (at + 1) // 2 + 1 + i)
                        scores(2 * i + 2, at % 2, (at + 2) // 2 + 1 + i)

            @block.vector
            def _(v):
                v.sem_inc(q_used, 1)
                v.memset(mx[:, :, :], 0.0).then_inc(maxed, 2)
                v.wait_ge(maxed, 2)
                for hh in range(2):
                    at = hh * SB
                    with v.Fori(0, SB) as b:
                        r = at + b
                        v.tensor_single_scalar(mask[:, :, :],
                                               m.at[:, ds(b, 1), 0:NP].rearrange("p a (k n) -> p (a k) n", n=CW),
                                               1.0, op=ALU.min).then_inc(masked, 1)
                        v.wait_ge(masked, r + 1)
                        for h in range(HH):
                            for part in range(2):
                                v.wait_ge(scored, per * r + 2 * h + part + 1)
                                hold(v, maxed, per * r + 2 * h + part + 1, m.passed)
                                v.tensor_tensor_reduce(
                                    out=junk[part][:, :, :],
                                    in0=m.ps[:, banks[part], 0:CW], in1=mask[:, banks[part], :], scale=1.0, scalar=0.0, op0=ALU.mult, op1=ALU.max, accum_out=mx[:, h, part:part + 1])\
                                 .then_inc(maxed, 1)
                        v.wait_ge(maxed, per * (r + 1) + 2)
                        v.tensor_tensor(mall[:, ds(b, 1), hh * HH:(hh + 1) * HH].rearrange("p a h -> p (a h)"),
                                        mx[:, :, 0], mx[:, :, 1], op=ALU.max).then_inc(q_used, 1)
                        v.wait_ge(q_used, r + 2)
        with ExitStack() as c2:
            sb2 = lambda name, shape, dt: c2.enter_context(nc.sbuf_tensor("neg_" + name, shape, dt))
            pcs = sb2("pieces", [P, SB, 3, HEADS], BF16)
            rows = sb2("rows", [3 * HEADS, ND], BF16)
            step = c2.enter_context(nc.semaphore("neg_step"))
            split = c2.enter_context(nc.semaphore("neg_split"))
            turned = c2.enter_context(nc.semaphore("neg_turned"))
            rowed = c2.enter_context(nc.semaphore("neg_rowed"))
            stored = c2.enter_context(nc.semaphore("neg_stored"))
            block = c2.enter_context(nc.Block())

            @block.vector
            def _(v):
                s = Steps(v, step)
                s.link(v.tensor_single_scalar(mall[:, :, :], mall[:, :, :], -1.0, op=ALU.mult))
                split3(v, s, [pcs[:, :, k, :] for k in range(3)], mall[:, :, :])
                v.memset(rows[0:1, 0:1], 0.0).then_inc(split, 1)
                v.wait_ge(split, 1)
                v.wait_ge(turned, 1)
                v.tensor_copy(rows[:, 0:6 * 512].rearrange("p (k n) -> p k n", n=512), m.ps[0:3 * HEADS, 0:6, :])
                v.tensor_copy(rows[:, 6 * 512:ND], m.ps[0:3 * HEADS, 6, 0:P]).then_inc(rowed, 1)

            @block.tensor
            def _(pe):
                pe.wait_ge(split, 1)
                for b in range(SB):
                    last = nc.tensor.matmul(m.bank[b // 4][0:3 * HEADS, (b % 4) * P:(b % 4 + 1) * P],
                                            pcs[:, b, :, :], m.identb[:, :], start=True, stop=True)
                last.then_inc(turned, 1)

            @block.sync
            def _(sp):
                sp.wait_ge(rowed, 1)
                for k in range(3):
                    sp.dma_start(qs[KS + k, :, :], rows[k * HEADS:(k + 1) * HEADS, :]).then_inc(stored, 16)
                sp.wait_ge(stored, 48)


def attend(nc, m, x1, qs, ks, vd, ad, bias, out):
    with ExitStack() as ctx:
        sb = lambda name, shape, dt: ctx.enter_context(nc.sbuf_tensor("att_" + name, shape, dt))
        q = sb("q", [KM, HEADS, CW], BF16)
        k = [sb(f"k{i}", [KM, HEADS, P], BF16) for i in range(DG)]
        vv = [sb(f"v{i}", [P, HEADS, VW], F32) for i in range(DG)]
        a = [sb(f"a{i}", [P, CW], BF16) for i in range(DG)]
        e = [sb(f"e{i}", [P, 2, CW], F32) for i in range(2)]
        p = [sb(f"p{i}", [P, 2, CW], F32) for i in range(2)]
        acc = e[0]
        bb = sb("bias", [RB, D], F32)
        xr = sb("xr", [RB, RPC, D], F32)
        y = sb("y", [RB, RPC, D], F32)
        o = sb("o", [RB, RPC, D], F32)
        rden = sb("rden", [RB, 2, RPC, HEADS // 2], F32)
        st = sb("st", [RB, RPC, 6], F32)
        mv = sb("mv", [RB, RPC, 2], F32)
        sd = sb("sd", [RB, RPC], F32)
        names = ("b_loaded q_loaded x_loaded scored exped weighed summed acc_ready turned step "
                 "normed rooted finished stored out_free").split()
        sems = {n: ctx.enter_context(nc.semaphore("att_" + n)) for n in names}
        (b_loaded, q_loaded, x_loaded, scored, exped, weighed, summed, acc_ready, turned, step,
         normed, rooted, finished, stored, out_free) = (sems[n] for n in names)
        slot_loaded = [ctx.enter_context(nc.semaphore(f"att_slot{i}")) for i in range(DG)]
        block = ctx.enter_context(nc.Block())
        HP = HEADS // 2
        PB = SB * HP
        E0, W0, S0 = 2, 2, DG * HP

        @block.sync
        def _(sp):
            with sp.Fori(0, NC) as c:
                hold(sp, turned, 1 + c, m.passed)
                sp.dma_start(q[:, :, :], qs[:, :, ds(c * CW, CW)]).then_inc(q_loaded, 16)
                with sp.Fori(0, NDG) as g:
                    for i in range(DG):
                        hold(sp, summed, HP * ((c * NDG + g) * DG + i + 1), m.passed)
                        row = (g * DG + i) * P
                        sp.dma_start(k[i][:, :, :], ks[:, :, ds(row, P)]).then_inc(slot_loaded[i], 16)
                        sp.dma_start(a[i][:, :], ad[ds(row, P), ds(c * CW, CW)]).then_inc(slot_loaded[i], 16)
                        sp.dma_start(vv[i][:, :, :], vd[ds(row, P), :].rearrange("p (h w) -> p h w", w=VW))\
                          .then_inc(slot_loaded[i], 16)

        @block.gpsimd
        def _(pool):
            pool.sem_inc(out_free, 1)
            pool.dma_start(bb[:, :], bias.unsqueeze(0).to_broadcast([RB, D])).then_inc(b_loaded, 16)
            with pool.Fori(0, NC) as c:
                hold(pool, finished, 1 + c, m.passed)
                pool.dma_start(xr[:, :, :], chunk_rows(x1, c)).then_inc(x_loaded, 16)
                inverse_roots(pool, m, mv, sd, normed, rooted, c)
                hold(pool, finished, 1 + c + 1, m.passed)
                pool.dma_start(chunk_rows(out, c), o[:, :, :]).then_inc(stored, 16)
                hold(pool, stored, 16 * (c + 1), m.passed)
                pool.sem_inc(out_free, 1)

        @block.tensor
        def _(pe):
            pe.sem_inc(turned, 1)
            with pe.Fori(0, NC) as c:
                pe.wait_ge(q_loaded, 16 * (c + 1))

                def scores(n, i, h):
                    pe.wait_ge(exped, n - 1 + E0)
                    for z in range(2):
                        last = nc.tensor.matmul(m.bank[2 * (h % 2) + z][:, 0:CW], k[i][:, 2 * h + z, :],
                                                q[:, 2 * h + z, :], start=True, stop=True)
                    last.then_inc(scored, 1)

                def sums(n, i, h, start, stop):
                    pe.wait_ge(weighed, n + 1 + W0)
                    for z in range(2):
                        head = 2 * h + z
                        at = VW * (head % 4)
                        last = nc.tensor.matmul(m.bank[4 + head // 4][at:at + VW, 0:CW],
                                                vv[i][:, head, :], p[h % 2][:, z, :], start=start, stop=stop)
                    last.then_inc(summed, 1)

                def group(g, first, final):
                    n0 = (c * SB + g * DG) * HP
                    for i in range(DG):
                        pe.wait_ge(slot_loaded[i], 48 * (c * NDG + g + 1))
                        for h in range(HP):
                            j = i * HP + h
                            scores(n0 + j, i, h)
                            if j:
                                sums(n0 + j - 1, (j - 1) // HP, (j - 1) % HP, first and j <= HP,
                                     final and j > (DG - 1) * HP)
                    sums(n0 + DG * HP - 1, DG - 1, HP - 1, False, final)

                group(0, True, False)
                with pe.Fori(1, NDG - 1) as g:
                    group(g, False, False)
                group(NDG - 1, False, True)
                pe.wait_ge(acc_ready, c + 1)
                for z in range(2):
                    for j in range(RPC):
                        last = nc.tensor.transpose(m.bank[6 + z][0:RB, j * P:(j + 1) * P],
                                                   acc[:, z, j * RB:(j + 1) * RB], m.ident[:, :])
                last.then_inc(turned, 1)

        @block.scalar
        def _(act):
            act.sem_inc(exped, E0)
            with act.Fori(0, NC) as c:
                with act.Fori(0, SB) as d:
                    for h in range(HP):
                        n = (c * SB + d) * HP + h
                        act.wait_ge(scored, n + 1)
                        act.wait_ge(weighed, n - 1 + W0)
                        nc.scalar.activation(e[h % 2][:, :, :], m.ps[:, 2 * (h % 2):2 * (h % 2) + 2, 0:CW],
                                             ACT.Exp).then_inc(exped, 1)

        @block.vector
        def _(v):
            v.sem_inc(finished, 1)
            v.sem_inc(weighed, W0)
            v.sem_inc(summed, S0)
            v.wait_ge(b_loaded, 16)
            with v.Fori(0, NC) as c:
                with v.Fori(0, NDG) as g:
                    for i in range(DG):
                        v.wait_ge(slot_loaded[i], 48 * (c * NDG + g + 1))
                        for h in range(HP):
                            n = ((c * NDG + g) * DG + i) * HP + h
                            v.wait_ge(exped, n + 1 + E0)
                            v.wait_ge(summed, n - 1 + S0)
                            v.scalar_tensor_tensor(p[h % 2][:, :, :], e[h % 2][:, :, :], 1.0,
                                                   a[i][:, :].unsqueeze(1).to_broadcast([P, 2, CW]),
                                                   op0=ALU.min, op1=ALU.mult).then_inc(weighed, 1)
                s = Steps(v, step, (6 + RPC + 1) * c)
                v.wait_ge(summed, PB * (c + 1) + S0)
                v.wait_ge(weighed, PB * (c + 1) + W0)
                v.tensor_copy(acc[:, :, :], m.ps[:, 4:6, 0:CW]).then_inc(acc_ready, 1)
                v.wait_ge(turned, 1 + c + 1)
                sums = [m.bank[6 + z][0:RB, :].rearrange("p (j h w) -> p j h w", j=RPC, w=VW) for z in range(2)]
                for z in range(2):
                    s.done(v.reciprocal(rden[:, z, :, :], sums[z][:, :, :, HD]))
                s.wait()
                half = D // 2
                for z in range(2):
                    s.done(v.tensor_tensor(y[:, :, z * half:(z + 1) * half].rearrange("p j (h f) -> p j h f", f=HD),
                                           sums[z][:, :, :, 0:HD],
                                           rden[:, z, :, :].unsqueeze(3).to_broadcast([RB, RPC, HEADS // 2, HD]),
                                           op=ALU.mult))
                v.wait_ge(x_loaded, 16 * (c + 1))
                s.link(v.tensor_tensor(xr[:, :, :], xr[:, :, :], bb[:, :].unsqueeze(1).to_broadcast([RB, RPC, D]),
                                       op=ALU.add))
                s.link(v.tensor_tensor(y[:, :, :], y[:, :, :], xr[:, :, :], op=ALU.add))
                v.wait_ge(out_free, c + 1)
                layer_norm(v, s, m, y, o, st, mv, sd, normed, rooted, c).then_inc(finished, 1)
                assert s.n == 6 + RPC + 1


def pad_input(nc, m, x, x_pad, states):
    with ExitStack() as ctx:
        zeros = ctx.enter_context(nc.sbuf_tensor("pad_zeros", [ND - N, D], F32))
        zeroed = ctx.enter_context(nc.semaphore("pad_zeroed"))
        stored = ctx.enter_context(nc.semaphore("pad_stored"))
        block = ctx.enter_context(nc.Block())

        @block.vector
        def _(v):
            v.memset(zeros[:, :], 0.0).then_inc(zeroed, 1)

        @block.sync
        def _(sp):
            sp.dma_start(x_pad[0:N, :], x).then_inc(stored, 16)
            sp.wait_ge(zeroed, 1)
            sp.dma_start(x_pad[N:ND, :], zeros[:, :]).then_inc(stored, 16)
            for a in states:
                sp.dma_start(a[NP:ND, :], zeros[0:ND - NP, :]).then_inc(stored, 16)
            sp.wait_ge(stored, 16 * (2 + len(states)))


def build_program(nc, x, src, dst, edge_type_500, L0_gnn_rel_emb, L0_gnn_W_neighbor, L0_gnn_loop_weight,
                  L1_gnn_query_kernel, L1_gnn_query_bias, L1_gnn_key_kernel, L1_gnn_key_bias, L1_gnn_kernel,
                  L1_gnn_bias, L2_gnn_weight, L3_gnn_W1, L3_gnn_b1, L3_gnn_W2, L3_gnn_b2, out):
    def dram(name, shape, dt):
        return nc.dram_tensor(name, shape, dt, kind="Internal").ap()

    x0, x1, x2, x3, x4 = (dram(f"state{i}", [ND, D], F32) for i in range(5))
    base_d, deg_d, aggr_d = dram("base_d", [NT], I32), dram("deg_d", [ND], F32), dram("aggr_d", [P, NP], F32)
    qs, ks = (dram(n, [KM, HEADS, ND], BF16) for n in ("queries", "keys"))
    vd, ad = dram("values", [ND, HEADS * VW], F32), dram("counts_turned", [ND, NP], BF16)

    with ExitStack() as ctx:
        sb = lambda name, shape, dt: ctx.enter_context(nc.sbuf_tensor(name, shape, dt))
        m = allocate(nc, ctx)
        m.in_norm = sb("in_norm", [RB, NRB], F32)
        m.loop_norm = sb("loop_norm", [RB, NRB], F32)
        m.loop_norm_s = sb("loop_norm_s", [P, SB], F32)
        m.out_norm = sb("out_norm", [P, SB], F32)
        m.at = sb("at", [P, SB, ND], BF16)
        pad_input(nc, m, x, x0, (x1, x2, x3, x4))
        with ExitStack() as tctx:
            t = Mem()
            tb = lambda name, shape, dt: tctx.enter_context(nc.sbuf_tensor(name, shape, dt))
            t.bad = tb("bad", [1, 1], I32)
            t.iota = tb("iota", [P, W * SB], F16)
            t.base = tb("base", [1, NT], I32)
            t.key = [tb(f"key{k}", [P, NT], F32 if k == 4 else F16) for k in range(7)]
            with ExitStack() as ectx:
                edge_tables(nc, m, src, dst, edge_type_500, base_d, t)
            t.rt = tb("rt", [P, TB, NP], BF16)
            count_edges(nc, m, t)
            relation_sums(nc, m, t, L0_gnn_rel_emb, aggr_d)
        degrees(nc, m, deg_d)

        def conv(tag, rows, scale, *args, **kwargs):
            with ExitStack() as c2:
                parts = [c2.enter_context(nc.sbuf_tensor(f"{tag}_part{k}", [P, SB, D], BF16)) for k in range(3)]
                load_and_split(nc, m, tag, rows, scale, parts)
                graph_conv(nc, m, tag, parts, *args, **kwargs)

        conv("L0", x0, None, L0_gnn_W_neighbor, m.in_norm, x1, residual=x0, loop_weight=L0_gnn_loop_weight,
             aggr_d=aggr_d, relu=True)
        add_loops(nc, m, "L1", 1)
        turn_counts(nc, m, ad)
        project(nc, m, x1, L1_gnn_query_kernel, L1_gnn_query_bias, L1_gnn_key_kernel, L1_gnn_key_bias,
                L1_gnn_kernel, qs, ks, vd)
        score_maxima(nc, m, qs, ks)
        attend(nc, m, x1, qs, ks, vd, ad, L1_gnn_bias, x2)
        add_loops(nc, m, "L2", -1)
        conv("L2", x2, m.out_norm, L2_gnn_weight, m.in_norm, x3, residual=x2)
        add_loops(nc, m, "L3", 1)
        conv("L3a", x3, m.loop_norm_s, L3_gnn_W1, m.loop_norm, x4, bias=L3_gnn_b1, relu=True, norm=False)
        conv("L3b", x4, m.loop_norm_s, L3_gnn_W2, m.loop_norm, out, residual=x3, bias=L3_gnn_b2)


_NAMES = ["x", "src", "dst", "edge_type_500", "L0_gnn_rel_emb", "L0_gnn_W_neighbor", "L0_gnn_loop_weight",
          "L1_gnn_query_kernel", "L1_gnn_query_bias", "L1_gnn_key_kernel", "L1_gnn_key_bias", "L1_gnn_kernel",
          "L1_gnn_bias", "L2_gnn_weight", "L3_gnn_W1", "L3_gnn_b1", "L3_gnn_W2", "L3_gnn_b2"]


def kernel(**inputs):
    import numpy as np
    import concourse.bacc as bacc
    from concourse.bass_utils import run_bass_kernel_spmd

    nc = bacc.Bacc("TRN2", target_bir_lowering=False, num_devices=1)
    arrays, args = {}, []
    for name in _NAMES:
        a = np.ascontiguousarray(inputs[name])
        arrays[f"in_{name}"] = a
        args.append(nc.dram_tensor(f"in_{name}", a.shape, mybir.dt.from_np(a.dtype), kind="ExternalInput").ap())
    args.append(nc.dram_tensor("out", (N, D), F32, kind="ExternalOutput").ap())
    build_program(nc, *args)
    result = run_bass_kernel_spmd(nc, [arrays], core_ids=[0])
    return result.results[0]["out"]
```

```python
import concourse.bass as bass
from concourse import mybir
from contextlib import ExitStack

F32, BF16, F16, I32 = mybir.dt.float32, mybir.dt.bfloat16, mybir.dt.float16, mybir.dt.int32
ALU = mybir.AluOpType
ACT = mybir.ActivationFunctionType
AX = mybir.AxisListType
ds = bass.ds

N = 3125
E = 100000
D = 128
P = 128
NREL = 500
SB = -(-N // P)
TB = -(-NREL // P)
CW = 448
NC = -(-N // CW)
NP = NC * CW
EPS = 1e-5
RB = 112
RPC = CW // RB
NRB = NP // RB
W = 12
ND = SB * P
TG = 112
NG = 7
NT = TG * NG
TF = E // P
TR = E - TF * P
U = 4
NU = NT // U


class Steps:

    def __init__(self, eng, sem, base=0):
        self.eng, self.sem, self.base, self.n = eng, sem, base, 0

    def done(self, ins):
        self.n += 1
        ins.then_inc(self.sem, 1)

    def done_here(self):
        self.n += 1
        self.eng.sem_inc(self.sem, 1)

    def wait(self):
        self.eng.wait_ge(self.sem, self.base + self.n)

    def link(self, ins):
        self.done(ins)
        self.wait()


def hold(eng, sem, value, passed):
    eng.wait_ge(sem, value)
    eng.sem_inc(passed, 1)


class Mem:
    pass


def allocate(nc, ctx):
    m = Mem()
    sb = lambda name, shape, dt: ctx.enter_context(nc.sbuf_tensor(name, shape, dt))
    m.ident = sb("ident", [P, P], F32)
    m.identb = sb("identb", [P, P], BF16)
    m.eps = sb("eps", [P, RPC], F32)
    m.passed = ctx.enter_context(nc.semaphore("passed"))
    m.minus_half = sb("minus_half", [P, SB + NRB], F32)
    m.ps = ctx.enter_context(nc.psum_tensor("ps", [P, 8, 512], F32))
    m.bank = [m.ps[:, i, :] for i in range(8)]
    return m


def edge_tables(nc, m, src, dst, typ, base_d, t):
    with ExitStack() as ctx:
        sb = lambda name, shape, dt: ctx.enter_context(nc.sbuf_tensor(name, shape, dt))
        flat = m.at[:, :, :].rearrange("p b d -> p (b d)")[0:TG, :].bitcast(F32)
        size, at = NG * P, [0]

        def carve(k, dt):
            at[0] += k * size
            return flat[:, at[0] - k * size:at[0]].bitcast(dt).rearrange("p (k g e) -> p k g e", k=k, e=P)

        raw = carve(3, I32)
        low = carve(2, I32)
        blk = carve(2, I32)
        fl = carve(7, F32)
        dstf = carve(1, F32)[:, 0]
        bf = carve(2, F32)
        mn = sb("mn", [TG, NG], F32)
        mx = sb("mx", [TG, NG], F32)
        mni = sb("mni", [TG, NG], I32)
        span = sb("span", [TG, NG], F32)
        worst = sb("worst", [TG, 1], F32)
        badf = sb("badf", [1, 1], F32)
        loaded = ctx.enter_context(nc.semaphore("edges_loaded"))
        based = ctx.enter_context(nc.semaphore("bases_stored"))
        baseb = ctx.enter_context(nc.semaphore("bases_back"))
        ready = ctx.enter_context(nc.semaphore("tables_ready"))
        mnready = ctx.enter_context(nc.semaphore("mins_ready"))
        idr = ctx.enter_context(nc.semaphore("ident_ready"))
        turned = ctx.enter_context(nc.semaphore("tables_turned"))
        freed = ctx.enter_context(nc.semaphore("banks_freed"))
        dstep = ctx.enter_context(nc.semaphore("dve_step"))
        zeroed = ctx.enter_context(nc.semaphore("pool_step"))
        block = ctx.enter_context(nc.Block())
        G6 = (NG - 1) * TG * P

        @block.sync
        def _(sp):
            for k, a in enumerate((dst, src, typ)):
                sp.dma_start(raw[:, k, 0:NG - 1, :],
                             a[0:G6].rearrange("(g p e) -> p g e", g=NG - 1, e=P)).then_inc(loaded, 16)
                sp.dma_start(raw[0:TF - (NG - 1) * TG, k, NG - 1, :],
                             a[G6:TF * P].rearrange("(p e) -> p e", e=P)).then_inc(loaded, 16)
                r = TF - (NG - 1) * TG
                sp.dma_start(raw[r:r + 1, k, NG - 1, 0:TR], a[TF * P:E].rearrange("(p e) -> p e", p=1))\
                  .then_inc(loaded, 16)
                sp.dma_start(raw[r:r + 1, k, NG - 1, TR:P], a[E - P + TR:E].rearrange("(p e) -> p e", p=1))\
                  .then_inc(loaded, 16)
                for q in range(r + 1, TG):
                    sp.dma_start(raw[q:q + 1, k, NG - 1, :], a[E - P:E].rearrange("(p e) -> p e", p=1))\
                      .then_inc(loaded, 16)
            sp.wait_ge(mnready, 1)
            sp.dma_start(base_d.rearrange("(g p) -> p g", p=TG), mni[:, :],
                         allow_slow_non_contiguous=True).then_inc(based, 16)
            sp.wait_ge(based, 16)
            sp.dma_start(t.base[0:1, :], base_d.rearrange("(a n) -> a n", a=1)).then_inc(baseb, 16)
            sp.wait_ge(baseb, 16)

        @block.gpsimd
        def _(pool):
            pool.memset(m.ident[:, :], 0.0)
            pool.memset(m.identb[:, :], 0.0).then_inc(zeroed, 1)
            pool.wait_ge(zeroed, 1)
            pool.affine_select(out=m.ident[:, :], in_=m.ident[:, :], compare_op=ALU.not_equal, fill=1.0,
                               base=0, pattern=[[-1, P]], channel_multiplier=1).then_inc(idr, 1)
            pool.memset(m.minus_half[:, :], -0.5)
            pool.memset(m.eps[:, :], EPS)
            pool.affine_select(out=m.identb[:, :], in_=m.identb[:, :], compare_op=ALU.not_equal, fill=1.0,
                               base=0, pattern=[[-1, P]], channel_multiplier=1)
            pool.iota(t.iota[:, :], [[1, W * SB]], base=0, channel_multiplier=0,
                      allow_small_or_imprecise_dtypes=True)

        @block.vector
        def _(v):
            s = Steps(v, dstep)
            v.wait_ge(loaded, 16 * 3 * (4 + TG - 1 - (TF - (NG - 1) * TG)))
            for k in range(2):
                s.done(v.tensor_single_scalar(blk[:, k], raw[:, 1 + k], 7, op=ALU.arith_shift_right))
                s.done(v.tensor_single_scalar(low[:, k], raw[:, 1 + k], P - 1, op=ALU.bitwise_and))
            s.link(v.tensor_copy(dstf[:, :, :], raw[:, 0]))
            s.done(v.tensor_copy(bf[:, :], blk[:, :]))
            s.done(v.tensor_copy(fl[:, 2:4], low[:, :]))
            s.done(v.tensor_reduce(mn[:, :], dstf[:, :, :], axis=AX.X, op=ALU.min))
            s.link(v.tensor_reduce(mx[:, :], dstf[:, :, :], axis=AX.X, op=ALU.max))
            s.done(v.tensor_copy(mni[:, :], mn[:, :]))
            s.link(v.tensor_tensor(span[:, :], mx[:, :], mn[:, :], op=ALU.subtract))
            s.link(v.tensor_reduce(worst[:, :], span[:, :], axis=AX.X, op=ALU.max))
            nb = mn[:, :].unsqueeze(2).to_broadcast([TG, NG, P])
            s.done(v.tensor_copy(fl[:, 4], dstf[:, :, :]))
            s.done(v.tensor_single_scalar(fl[:, 5:7], bf[:, :], float(W), op=ALU.mult))
            v.memset(badf[:, :], 0.0).then_inc(mnready, 1)
            s.wait()
            s.link(v.tensor_tensor(dstf[:, :, :], dstf[:, :, :], nb, op=ALU.subtract))
            s.done(v.scalar_tensor_tensor(fl[:, 0], bf[:, 0], float(W), dstf[:, :, :], op0=ALU.mult, op1=ALU.add))
            v.scalar_tensor_tensor(fl[:, 1], bf[:, 1], float(W), dstf[:, :, :], op0=ALU.mult, op1=ALU.add)\
             .then_inc(ready, 1)
            for j in range(14):
                k, h = j // 2, j % 2
                n = 4 * TG if h == 0 else 3 * TG
                v.wait_ge(turned, j + 1)
                v.tensor_copy(t.key[k][:, h * 4 * TG:h * 4 * TG + n], m.bank[j % 6][:, 0:n]).then_inc(freed, 1)
            v.wait_ge(freed, 14)
            for k in (2, 3):
                s.done(v.memset(t.key[k][TR:64, TF:TF + 1], -1.0))
                s.done(v.memset(t.key[k][64:P, TF:TF + 1], -1.0))
                s.done(v.memset(t.key[k][:, TF + 1:NT], -1.0))
            v.wait_ge(turned, 15)
            s.link(v.tensor_reduce(badf[:, :], m.bank[7][0:1, 0:TG], axis=AX.X, op=ALU.max))
            s.link(v.tensor_single_scalar(badf[:, :], badf[:, :], float(W - 1), op=ALU.is_gt))
            s.link(v.tensor_copy(t.bad[0:1, 0:1], badf[:, :]))

        @block.tensor
        def _(pe):
            pe.wait_ge(idr, 1)
            pe.wait_ge(ready, 1)
            for j in range(14):
                k, h = j // 2, j % 2
                if j >= 6:
                    pe.wait_ge(freed, j - 5)
                for g in range(4 if h == 0 else 3):
                    last = nc.tensor.transpose(m.bank[j % 6][:, g * TG:(g + 1) * TG], fl[:, k, 4 * h + g, :],
                                               m.ident[0:TG, 0:TG])
                last.then_inc(turned, 1)
            nc.tensor.transpose(m.bank[7][0:1, 0:TG], worst[:, 0:1], m.ident[0:TG, 0:TG]).then_inc(turned, 1)


def count_edges(nc, m, t):
    with ExitStack() as ctx:
        sb = lambda name, shape, dt: ctx.enter_context(nc.sbuf_tensor(name, shape, dt))
        widths = (W * SB, W * TB, P, P)
        hot_row = [sb(f"hot_row{h}", [P, 2, U, P], BF16) for h in range(2)]
        hot = [[sb(f"hot{k}{h}", [P, U, widths[k]], BF16) for h in range(2)] for k in range(2)]
        hot += [[hot_row[h][:, k] for h in range(2)] for k in range(2)]
        off = [t.far[:, h * U * P:(h + 1) * U * P].bitcast(F16).rearrange("p (k u n) -> p k u n", k=2, n=P)
               for h in range(2)]
        names = ("col_ready row_off row_abs row_ready mm_done bank_free src_added any_keys any_hot any_used "
                 "any_copied").split()
        (col_ready, row_off, row_abs, row_ready, mm_done, bank_free, src_added, any_keys, any_hot, any_used,
         any_copied) = \
            (ctx.enter_context(nc.semaphore(n)) for n in names)
        block = ctx.enter_context(nc.Block())
        NW = -(-N // W)

        @block.vector
        def _(v):
            v.sem_inc(any_copied, 1)
            v.memset(m.at[:, :, :].bitcast(F32), 0.0).then_inc(bank_free, 2 * U - 1)
            v.memset(t.rt[:, :, :].bitcast(F32), 0.0).then_inc(bank_free, 1)
            v.wait_ge(bank_free, 2 * U)
            v.sem_inc(src_added, 1)

            def iota_by(n):
                return t.iota[:, 0:n].unsqueeze(1).to_broadcast([P, U, n])

            def keys_of(k, r, n):
                return t.key[k][:, ds(U * r, U)].unsqueeze(2).to_broadcast([P, U, n])

            def type_columns(r, h):
                n = widths[1]
                v.tensor_tensor(hot[1][h][:, :, :], iota_by(n), keys_of(1, r, n), op=ALU.is_equal)

            def source_columns(r, h, u):
                v.tensor_scalar(hot[0][h][:, u, :], t.iota[:, 0:widths[0]], t.key[0][:, ds(U * r + u, 1)], None,
                                op0=ALU.is_equal).then_inc(col_ready, 1)

            def add(r, h, u, base):
                v.wait_ge(mm_done, U * r + u + 1 + 2 * U)
                v.wait_ge(src_added, U * r + u + 1)
                wa = m.at[:, :, ds(base, W)]
                v.tensor_tensor(wa, wa, m.bank[U * h + u][:, 0:W * SB].rearrange("p (b d) -> p b d", d=W),
                                op=ALU.add).then_inc(src_added, 1)
                v.wait_ge(bank_free, U * r + 2 * U + u)
                wr = t.rt[:, :, ds(base, W)]
                v.tensor_tensor(wr, wr, m.bank[U * h + u][:, W * SB:W * (SB + TB)]
                                .rearrange("p (b d) -> p b d", d=W), op=ALU.add).then_inc(bank_free, 1)

            def bases(r, n):
                return nc.values_load_multi_w_load_instructions(
                    t.base[0:1, ds(U * r, n)], engines=(mybir.EngineType.DVE,), min_val=0, max_val=N - 1,
                    skip_runtime_bounds_check_because="minima of node numbers")[1]

            bad = v.value_load(t.bad[0:1, 0:1], min_val=0, max_val=1)
            with v.If(bad == 0):
                type_columns(0, 0)
                for u in range(U):
                    source_columns(0, 0, u)

                def two_rounds(i, final):
                    base = bases(2 * i, 2 * U)
                    for h in range(2):
                        more = not (final and h)
                        if more:
                            type_columns(2 * i + h + 1, 1 - h)
                        for u in range(U):
                            if more:
                                source_columns(2 * i + h + 1, 1 - h, u)
                            add(2 * i + h, h, u, base[U * h + u])

                with v.Fori(0, NU // 2 - 1) as i:
                    two_rounds(i, False)
                two_rounds(NU // 2 - 1, True)
            with v.Else():
                FAR = 10000.0
                v.sem_inc(any_used, 2)
                with v.Fori(0, NW) as w:
                    s = Steps(v, any_keys, 8 * w)
                    v.wait_ge(any_used, NU * w + 2)
                    s.done(v.tensor_scalar(t.key[0][:, :], t.key[4][:, :], float(W), FAR, op0=ALU.is_ge, op1=ALU.mult))
                    s.link(v.tensor_scalar(t.key[1][:, :], t.key[4][:, :], 0.0, FAR, op0=ALU.is_lt, op1=ALU.mult))
                    s.link(v.tensor_tensor(t.key[0][:, :], t.key[0][:, :], t.key[1][:, :], op=ALU.add))
                    s.link(v.tensor_tensor(t.key[0][:, :], t.key[0][:, :], t.key[4][:, :], op=ALU.add))
                    s.link(v.tensor_tensor(t.key[1][:, :], t.key[0][:, :], t.key[6][:, :], op=ALU.add))
                    s.link(v.tensor_tensor(t.key[0][:, :], t.key[0][:, :], t.key[5][:, :], op=ALU.add))
                    s.link(v.tensor_single_scalar(t.key[4][:, :], t.key[4][:, :], float(-W), op=ALU.add))
                    s.done_here()
                    with v.Fori(0, NU // 2) as i:
                        for h in range(2):
                            v.wait_ge(any_used, NU * w + 2 * i + h + 1)
                            for k in range(4):
                                n = widths[k]
                                last = v.tensor_tensor(hot[k][h][:, :, :], iota_by(n),
                                                       keys_of(k, 2 * i + h, n), op=ALU.is_equal)
                            last.then_inc(any_hot, 1)
                    v.wait_ge(any_used, NU * w + NU + 2)
                    v.tensor_copy(m.at[:, :, ds(w * W, W)],
                                  m.bank[0][:, 0:W * SB].rearrange("p (b d) -> p b d", d=W))
                    v.tensor_copy(t.rt[:, :, ds(w * W, W)],
                                  m.bank[1][:, 0:W * TB].rearrange("p (b d) -> p b d", d=W)).then_inc(any_copied, 1)

        @block.tensor
        def _(pe):
            bad = pe.value_load(t.bad[0:1, 0:1], min_val=0, max_val=1)
            with pe.If(bad == 0):
                pe.sem_inc(mm_done, 2 * U)
                with pe.Fori(0, NU // 2) as i:
                    for h in range(2):
                        r = 2 * i + h
                        pe.wait_ge(row_ready, r + 3)
                        for u in range(U):
                            pe.wait_ge(col_ready, U * r + u + 1)
                            pe.wait_ge(bank_free, U * r + u + 1)
                            nc.tensor.matmul(m.bank[U * h + u][:, 0:W * SB], hot[2][h][:, u, :],
                                             hot[0][h][:, u, :], start=True, stop=True)
                            nc.tensor.matmul(m.bank[U * h + u][:, W * SB:W * (SB + TB)], hot[3][h][:, u, :],
                                             hot[1][h][:, u, :], start=True, stop=True).then_inc(mm_done, 1)
            with pe.Else():
                with pe.Fori(0, NW) as w:
                    pe.wait_ge(any_copied, 1 + w)

                    def pair(i, first, final):
                        for h in range(2):
                            pe.wait_ge(any_hot, NU * w + 2 * i + h + 1)
                            for u in range(U):
                                start, stop = first and h + u == 0, final and h == 1 and u == U - 1
                                nc.tensor.matmul(m.bank[0][:, 0:W * SB], hot[2][h][:, u, :],
                                                 hot[0][h][:, u, :], start=start, stop=stop)
                                last = nc.tensor.matmul(m.bank[1][:, 0:W * TB], hot[3][h][:, u, :],
                                                        hot[1][h][:, u, :], start=start, stop=stop)
                            last.then_inc(any_used, 1)

                    pair(0, True, False)
                    with pe.Fori(1, NU // 2 - 1) as i:
                        pair(i, False, False)
                    pair(NU // 2 - 1, False, True)


        @block.gpsimd
        def _(pool):
            bad = pool.value_load(t.bad[0:1, 0:1], min_val=0, max_val=1)
            with pool.If(bad == 0):
                with pool.Fori(0, NU // 2) as i:
                    for h in range(2):
                        r = 2 * i + h
                        pool.wait_ge(row_ready, r + 1)
                        for k in range(2):
                            pool.tensor_tensor(off[h][:, k], t.iota[:, 0:P].unsqueeze(1).to_broadcast([P, U, P]),
                                               t.key[2 + k][:, ds(U * r, U)].unsqueeze(2).to_broadcast([P, U, P]),
                                               op=ALU.subtract).then_inc(row_off, 1)

        @block.scalar
        def _(act):
            bad = act.value_load(t.bad[0:1, 0:1], min_val=0, max_val=1)
            with act.If(bad == 0):
                act.sem_inc(row_ready, 2)
                with act.Fori(0, NU // 2) as i:
                    for h in range(2):
                        r = 2 * i + h
                        act.wait_ge(row_off, 2 * r + 2)
                        nc.scalar.activation(off[h], off[h], ACT.Abs).then_inc(row_abs, 1)
                        act.wait_ge(row_abs, r + 1)
                        act.wait_ge(mm_done, U * r + U)
                        nc.scalar.activation(hot_row[h][:, :, :, :], off[h], ACT.Relu, scale=-1.0, bias=1.0)\
                          .then_inc(row_ready, 1)


def chunk_rows(a, c):
    return a[ds(c * CW, CW), :].rearrange("(j p) f -> p j f", p=RB)


def split3(v, s, parts, x):
    s.link(v.tensor_copy(parts[0], x))
    s.link(v.tensor_tensor(x, x, parts[0], op=ALU.subtract))
    s.link(v.tensor_copy(parts[1], x))
    s.link(v.tensor_tensor(parts[2], x, parts[1], op=ALU.subtract))


def load_and_split(nc, m, tag, rows, scale, parts):
    with ExitStack() as ctx:
        x = ctx.enter_context(nc.sbuf_tensor(f"{tag}_split_x", [P, SB, D], F32))
        loaded = ctx.enter_context(nc.semaphore(f"{tag}_all_loaded"))
        step = ctx.enter_context(nc.semaphore(f"{tag}_split_step"))
        block = ctx.enter_context(nc.Block())

        @block.sync
        def _(sp):
            sp.dma_start(x[:, :, :], rows.rearrange("(b p) f -> p b f", p=P)).then_inc(loaded, 16)

        @block.vector
        def _(v):
            s = Steps(v, step)
            v.wait_ge(loaded, 16)
            if scale is not None:
                s.link(v.tensor_tensor(x[:, :, :], x[:, :, :], scale[:, :].unsqueeze(2).to_broadcast([P, SB, D]),
                                       op=ALU.mult))
            split3(v, s, [q[:, :, :] for q in parts], x[:, :, :])


def relation_sums(nc, m, t, rel, aggr_d):
    with ExitStack() as ctx:
        sb = lambda name, shape, dt: ctx.enter_context(nc.sbuf_tensor(name, shape, dt))
        x = sb("rel_x", [P, TB, D], F32)
        parts = [sb(f"rel_part{k}", [P, TB, D], BF16) for k in range(3)]
        out = sb("rel_out", [P, CW], F32)
        loaded = ctx.enter_context(nc.semaphore("rel_loaded"))
        zeroed = ctx.enter_context(nc.semaphore("rel_zeroed"))
        step = ctx.enter_context(nc.semaphore("rel_step"))
        split = ctx.enter_context(nc.semaphore("rel_split"))
        summed = ctx.enter_context(nc.semaphore("rel_summed"))
        copied = ctx.enter_context(nc.semaphore("rel_copied"))
        stored = ctx.enter_context(nc.semaphore("rel_stored"))
        out_free = ctx.enter_context(nc.semaphore("rel_out_free"))
        block = ctx.enter_context(nc.Block())
        full = NREL // P

        @block.sync
        def _(sp):
            sp.sem_inc(out_free, 1)
            sp.wait_ge(zeroed, 1)
            sp.dma_start(x[:, 0:full, :], rel[0:full * P, :].rearrange("(b p) f -> p b f", p=P))\
              .then_inc(loaded, 16)
            sp.dma_start(x[0:NREL - full * P, full, :], rel[full * P:NREL, :]).then_inc(loaded, 16)
            with sp.Fori(0, NC) as c:
                hold(sp, copied, 1 + c + 1, m.passed)
                sp.dma_start(aggr_d[:, ds(c * CW, CW)], out[:, :]).then_inc(stored, 16)
                hold(sp, stored, 16 * (c + 1), m.passed)
                sp.sem_inc(out_free, 1)

        @block.vector
        def _(v):
            v.sem_inc(copied, 1)
            s = Steps(v, step)
            v.memset(x[:, :, :], 0.0).then_inc(zeroed, 1)
            v.wait_ge(loaded, 32)
            split3(v, s, [q[:, :, :] for q in parts], x[:, :, :])
            v.memset(out[:, 0:1], 0.0).then_inc(split, 1)
            with v.Fori(0, NC) as c:
                v.wait_ge(summed, c + 1)
                v.wait_ge(out_free, c + 1)
                v.tensor_copy(out[:, :], m.bank[0][:, 0:CW]).then_inc(copied, 1)

        @block.tensor
        def _(pe):
            pe.wait_ge(split, 1)
            with pe.Fori(0, NC) as c:
                pe.wait_ge(copied, 1 + c)
                for k in range(3):
                    for b in range(TB):
                        last = nc.tensor.matmul(m.bank[0][:, 0:CW], parts[k][:, b, :],
                                                t.rt[:, b, ds(c * CW, CW)],
                                                start=k + b == 0, stop=k == 2 and b == TB - 1)
                last.then_inc(summed, 1)


def degrees(nc, m, deg_d):
    with ExitStack() as ctx:
        sb = lambda name, shape, dt: ctx.enter_context(nc.sbuf_tensor(name, shape, dt))
        ones = sb("deg_ones", [P, 1], BF16)
        row = sb("deg_row", [1, ND], F32)
        junk = sb("deg_junk", [P, NP], BF16)
        outdeg = sb("out_deg", [P, SB], F32)
        rowed = ctx.enter_context(nc.semaphore("deg_rowed"))
        oned = ctx.enter_context(nc.semaphore("deg_oned"))
        summed = ctx.enter_context(nc.semaphore("deg_summed"))
        stored = ctx.enter_context(nc.semaphore("deg_stored"))
        loaded = ctx.enter_context(nc.semaphore("deg_loaded"))
        outed = ctx.enter_context(nc.semaphore("deg_outed"))
        clipped = ctx.enter_context(nc.semaphore("deg_clipped"))
        block = ctx.enter_context(nc.Block())

        @block.sync
        def _(sp):
            sp.wait_ge(rowed, NC + 2)
            sp.dma_start(deg_d.rearrange("(a n) -> a n", a=1), row[:, :]).then_inc(stored, 16)
            sp.wait_ge(stored, 16)
            with nc.allow_non_contiguous_dma(reason="one short vector"):
                sp.dma_start(m.in_norm[:, :], deg_d[0:NP].rearrange("(b p) -> p b", p=RB)).then_inc(loaded, 16)
                sp.dma_start(m.loop_norm[:, :], deg_d[0:NP].rearrange("(b p) -> p b", p=RB)).then_inc(loaded, 16)
                sp.dma_start(m.loop_norm_s[:, :], deg_d.rearrange("(b p) -> p b", p=P)).then_inc(loaded, 16)
            sp.wait_ge(loaded, 48)

        @block.tensor
        def _(pe):
            pe.wait_ge(oned, 1)
            with pe.Fori(0, NC) as c:
                pe.wait_ge(rowed, c + 1)
                for b in range(SB):
                    last = nc.tensor.matmul(m.bank[0][0:1, 0:CW], ones[:, 0:1], m.at[:, b, ds(c * CW, CW)],
                                            start=b == 0, stop=b == SB - 1)
                last.then_inc(summed, 1)

        @block.scalar
        def _(act):
            for b in range(SB):
                if b:
                    act.wait_ge(outed, b)
                nc.scalar.activation(junk[:, :], m.at[:, b, 0:NP], ACT.Copy, accum_out=outdeg[:, b:b + 1])\
                  .then_inc(outed, 1)

        @block.gpsimd
        def _(pool):
            pool.wait_ge(clipped, 4)
            for a in (m.in_norm, m.loop_norm, m.loop_norm_s, m.out_norm):
                pool.tensor_tensor(a[:, :], a[:, :], m.minus_half[0:a.shape[0], 0:a.shape[1]], op=ALU.pow)

        @block.vector
        def _(v):
            v.memset(ones[:, :], 1.0).then_inc(oned, 1)
            v.memset(row[:, :], 0.0).then_inc(rowed, 1)
            v.wait_ge(rowed, 1)
            with v.Fori(0, NC) as c:
                v.wait_ge(summed, c + 1)
                v.tensor_copy(row[0:1, ds(c * CW, CW)], m.bank[0][0:1, 0:CW]).then_inc(rowed, 1)
            v.memset(ones[:, :], 1.0).then_inc(rowed, 1)
            v.wait_ge(loaded, 48)
            v.wait_ge(outed, SB)
            v.tensor_single_scalar(m.in_norm[:, :], m.in_norm[:, :], 1.0, op=ALU.max).then_inc(clipped, 1)
            v.tensor_single_scalar(m.loop_norm[:, :], m.loop_norm[:, :], 1.0, op=ALU.add).then_inc(clipped, 1)
            v.tensor_single_scalar(m.loop_norm_s[:, :], m.loop_norm_s[:, :], 1.0, op=ALU.add).then_inc(clipped, 1)
            v.tensor_single_scalar(m.out_norm[:, :], outdeg[:, :], 1.0, op=ALU.max).then_inc(clipped, 1)


def layer_norm(v, s, m, y, o, st, mv, sd, normed, rooted, c):
    for j in range(RPC):
        s.done(v.bn_stats(st[:, j, :], y[:, j, :]))
    s.wait()
    s.done_here()
    for j in range(RPC):
        last = v.bn_aggr(mv[:, j, :], st[:, j, :])
    last.then_inc(normed, 1)
    v.wait_ge(rooted, 2 * c + 2)
    for j in range(RPC):
        last = v.tensor_scalar(o[:, j, :], y[:, j, :], mv[:, j, 0:1], sd[:, j:j + 1],
                               op0=ALU.subtract, op1=ALU.mult)
    return last


def inverse_roots(pool, m, mv, sd, normed, rooted, c):
    pool.wait_ge(normed, c + 1)
    pool.tensor_tensor(sd[:, :], mv[:, :, 1], m.eps[0:RB, :], op=ALU.add).then_inc(rooted, 1)
    pool.wait_ge(rooted, 2 * c + 1)
    pool.tensor_tensor(sd[:, :], sd[:, :], m.minus_half[0:RB, 0:RPC], op=ALU.pow).then_inc(rooted, 1)


def store_rows(sp, out, o, c, stored):
    if out.shape[0] >= NP or not isinstance(c, int) or c < NC - 1:
        sp.dma_start(chunk_rows(out, c), o[:, :, :]).then_inc(stored, 16)
        return 16
    full = (N - c * CW) // RB
    at = c * CW + full * RB
    sp.dma_start(out[c * CW:at, :].rearrange("(j p) f -> p j f", p=RB), o[:, 0:full, :]).then_inc(stored, 16)
    sp.dma_start(out[at:N, :], o[0:N - at, full, :]).then_inc(stored, 16)
    return 32


def graph_conv(nc, m, tag, parts, weight, post, out, residual=None, bias=None, loop_weight=None, aggr_d=None,
               relu=False, norm=True):
    with ExitStack() as ctx:
        sb = lambda name, shape, dt: ctx.enter_context(nc.sbuf_tensor(f"{tag}_{name}", shape, dt))
        w = sb("w", [P, D], F32)
        wl = sb("wl", [P, D], F32)
        bb = sb("bias", [RB, D], F32)
        aggt = sb("aggt", [P, CW], F32)
        aggr = sb("aggr", [P, CW], F32)
        xr = sb("xr", [RB, RPC, D], F32)
        xt = sb("xt", [P, CW], F32)
        y = sb("y", [RB, RPC, D], F32)
        o = sb("o", [RB, RPC, D], F32)
        st = sb("st", [RB, RPC, 6], F32)
        mv = sb("mv", [RB, RPC, 2], F32)
        sd = sb("sd", [RB, RPC], F32)
        sem = lambda name, used=True: ctx.enter_context(nc.semaphore(f"{tag}_{name}")) if used else None
        w_loaded, rows_loaded, rows_used, summed, aggt_ready, mixed, step, finished, stored, out_free = \
            (sem(name) for name in "w_loaded rows_loaded rows_used summed aggt_ready mixed step finished stored "
             "out_free".split())
        turned, xt_ready = (sem(name, loop_weight is not None) for name in ("turned", "xt_ready"))
        normed, rooted = (sem(name, norm) for name in ("normed", "rooted"))
        block = ctx.enter_context(nc.Block())
        nw = 1 + (bias is not None) + (loop_weight is not None)
        nl = (residual is not None) + (aggr_d is not None)
        bank_agg, bank_t, bank_rows, bank_loop = m.bank[0:4]

        @block.sync
        def _(sp):
            sp.sem_inc(out_free, 1)
            sp.dma_start(w[:, :], weight).then_inc(w_loaded, 16)
            if loop_weight is not None:
                sp.dma_start(wl[:, :], loop_weight).then_inc(w_loaded, 16)
            if bias is not None:
                sp.dma_start(bb[:, :], bias.unsqueeze(0).to_broadcast([RB, D])).then_inc(w_loaded, 16)

            def body(c):
                if nl:
                    hold(sp, rows_used, 1 + c, m.passed)
                if residual is not None:
                    sp.dma_start(xr[:, :, :], chunk_rows(residual, c)).then_inc(rows_loaded, 16)
                if aggr_d is not None:
                    sp.dma_start(aggr[:, :], aggr_d[:, ds(c * CW, CW)]).then_inc(rows_loaded, 16)
                hold(sp, finished, 1 + c + 1, m.passed)
                n = store_rows(sp, out, o, c, stored)
                sp.wait_ge(stored, 16 * c + n)
                sp.sem_inc(out_free, 1)

            with sp.Fori(0, NC - 1) as c:
                body(c)
            body(NC - 1)

        @block.tensor
        def _(pe):
            pe.sem_inc(mixed, 1)
            pe.wait_ge(w_loaded, 16 * nw)
            with pe.Fori(0, NC) as c:
                for k in range(3):
                    for b in range(SB):
                        last = nc.tensor.matmul(bank_agg[:, 0:CW], parts[k][:, b, :], m.at[:, b, ds(c * CW, CW)],
                                                start=k + b == 0, stop=k == 2 and b == SB - 1)
                last.then_inc(summed, 1)
                if loop_weight is not None:
                    pe.wait_ge(rows_loaded, 16 * nl * (c + 1))
                    for j in range(RPC):
                        last = nc.tensor.transpose(bank_t[:, j * RB:(j + 1) * RB], xr[:, j, :], m.ident[0:RB, 0:RB])
                    last.then_inc(turned, 1)
                    pe.wait_ge(xt_ready, c + 1)
                    pe.wait_ge(finished, 1 + c)
                    for j in range(RPC):
                        nc.tensor.matmul(bank_loop[0:RB, j * D:(j + 1) * D], xt[:, j * RB:(j + 1) * RB], wl[:, :],
                                         start=True, stop=True)
                pe.wait_ge(aggt_ready, c + 1)
                pe.wait_ge(finished, 1 + c)
                for j in range(RPC):
                    last = nc.tensor.matmul(bank_rows[0:RB, j * D:(j + 1) * D], aggt[:, j * RB:(j + 1) * RB],
                                            w[:, :], start=True, stop=True)
                last.then_inc(mixed, 1)

        @block.scalar
        def _(act):
            with act.Fori(0, NC) as c:
                if aggr_d is None:
                    act.wait_ge(summed, c + 1)
                    act.wait_ge(mixed, 1 + c)
                    nc.scalar.activation(aggt[:, :], bank_agg[:, 0:CW], ACT.Copy).then_inc(aggt_ready, 1)
                if loop_weight is not None:
                    act.wait_ge(turned, c + 1)
                    act.wait_ge(mixed, 1 + c)
                    nc.scalar.activation(xt[:, :], bank_t[:, 0:CW], ACT.Copy).then_inc(xt_ready, 1)

        @block.gpsimd
        def _(pool):
            if norm:
                with pool.Fori(0, NC) as c:
                    inverse_roots(pool, m, mv, sd, normed, rooted, c)

        @block.vector
        def _(v):
            v.sem_inc(finished, 1)
            v.sem_inc(rows_used, 1)
            flat = [RB, RPC, D]

            def body(c, s):
                if aggr_d is not None:
                    v.wait_ge(summed, c + 1)
                    v.wait_ge(rows_loaded, 16 * nl * (c + 1))
                    v.wait_ge(mixed, 1 + c)
                    v.tensor_tensor(aggt[:, :], aggr[:, :], bank_agg[:, 0:CW], op=ALU.add).then_inc(aggt_ready, 1)
                v.wait_ge(mixed, 1 + c + 1)
                rows = bank_rows[0:RB, :].rearrange("p (j f) -> p j f", f=D)
                s.link(v.tensor_tensor(y[:, :, :], rows, post[:, ds(c * RPC, RPC)].unsqueeze(2).to_broadcast(flat),
                                       op=ALU.mult))
                if bias is not None:
                    s.link(v.tensor_tensor(y[:, :, :], y[:, :, :], bb[:, :].unsqueeze(1).to_broadcast(flat),
                                           op=ALU.add))
                if loop_weight is not None:
                    s.link(v.tensor_tensor(y[:, :, :], y[:, :, :],
                                           bank_loop[0:RB, :].rearrange("p (j f) -> p j f", f=D), op=ALU.add))
                if relu:
                    s.link(v.tensor_single_scalar(y[:, :, :], y[:, :, :], 0.0, op=ALU.max))
                if residual is not None:
                    v.wait_ge(rows_loaded, 16 * nl * (c + 1))
                    s.link(v.tensor_tensor(y[:, :, :], y[:, :, :], xr[:, :, :], op=ALU.add))
                if nl:
                    v.sem_inc(rows_used, 1)
                v.wait_ge(out_free, c + 1)
                if norm:
                    layer_norm(v, s, m, y, o, st, mv, sd, normed, rooted, c).then_inc(finished, 1)
                else:
                    v.tensor_copy(o[:, :, :], y[:, :, :]).then_inc(finished, 1)
                return s.n

            v.wait_ge(w_loaded, 16 * nw)
            n = 1 + (bias is not None) + (loop_weight is not None) + relu + (residual is not None) + \
                (RPC + 1 if norm else 0)
            with v.Fori(0, NC) as c:
                s = Steps(v, step, n * c)
                assert body(c, s) == n


HEADS = 8
HD = D // HEADS
NX = 6
KS = NX * HD
KM = KS + 3
Q_PIECES = (0, 1, 0, 1, 2, 0)
K_PIECES = (0, 0, 1, 1, 0, 2)
VW = 32
DG = 5
NDG = SB // DG
NS = 3
PARTS = ((0, 3), (3, 5), (5, 7))
NE = 5


def add_loops(nc, m, tag, sign):
    with ExitStack() as ctx:
        block = ctx.enter_context(nc.Block())

        @block.vector
        def _(v):
            for b in range(SB):
                a = m.at[:, b, b * P:(b + 1) * P]
                v.tensor_tensor(a, a, m.identb[:, :], op=ALU.add if sign > 0 else ALU.subtract)


def turn_counts(nc, m, ad):
    with ExitStack() as ctx:
        rows = [ctx.enter_context(nc.sbuf_tensor(f"turn_rows{h}", [P, ND], BF16)) for h in range(2)]
        turned = ctx.enter_context(nc.semaphore("turn_turned"))
        evac = [ctx.enter_context(nc.semaphore(f"turn_evac{h}")) for h in range(2)]
        stored = [ctx.enter_context(nc.semaphore(f"turn_stored{h}")) for h in range(2)]
        rows_free = [ctx.enter_context(nc.semaphore(f"turn_rows_free{h}")) for h in range(2)]
        block = ctx.enter_context(nc.Block())
        first, second = 16, SB - 16

        @block.tensor
        def _(pe):
            with pe.Fori(0, SB) as i:
                for half, (lo, n) in enumerate(((0, first), (first, second))):
                    pe.wait_ge(evac[half], i + 1)
                    for b in range(n):
                        last = nc.tensor.matmul(m.bank[4 * half + b // 4][:, (b % 4) * P:(b % 4 + 1) * P],
                                                m.at[:, lo + b, ds(i * P, P)], m.identb[:, :],
                                                start=True, stop=True)
                    last.then_inc(turned, 1)

        def copy_out(half, copy, wait, i, h):
            wait(turned, 2 * i + 1 + half)
            lo, n = ((0, first), (first, second))[half]
            full = n // 4
            copy(rows[h][:, lo * P:(lo + 4 * full) * P].rearrange("p (k n) -> p k n", n=512),
                 m.ps[:, 4 * half:4 * half + full, :], n % 4 == 0)
            if n % 4:
                copy(rows[h][:, (lo + 4 * full) * P:(lo + n) * P],
                     m.ps[:, 4 * half + full, 0:(n % 4) * P], True)

        @block.scalar
        def _(act):
            act.sem_inc(evac[0], 1)
            def copy(out, in_, last):
                ins = nc.scalar.activation(out, in_, ACT.Copy)
                if last:
                    ins.then_inc(evac[0], 1)

            def body(i, h, uses):
                act.wait_ge(rows_free[h], uses + 1)
                copy_out(0, copy, act.wait_ge, i, h)

            body(0, 0, 0)
            with act.Fori(0, SB // 2) as k:
                body(2 * k + 1, 1, k)
                body(2 * k + 2, 0, k + 1)

        @block.vector
        def _(v):
            v.sem_inc(evac[1], 1)
            def copy(out, in_, last):
                ins = v.tensor_copy(out, in_)
                if last:
                    ins.then_inc(evac[1], 1)

            def body(i, h, uses):
                v.wait_ge(rows_free[h], uses + 1)
                copy_out(1, copy, v.wait_ge, i, h)

            body(0, 0, 0)
            with v.Fori(0, SB // 2) as k:
                body(2 * k + 1, 1, k)
                body(2 * k + 2, 0, k + 1)

        @block.sync
        def _(sp):
            sp.sem_inc(rows_free[0], 1)
            sp.sem_inc(rows_free[1], 1)

            def body(i, h, uses):
                hold(sp, evac[0], 1 + i + 1, m.passed)
                hold(sp, evac[1], 1 + i + 1, m.passed)
                sp.dma_start(ad[ds(i * P, P), :], rows[h][:, 0:NP]).then_inc(stored[h], 16)
                hold(sp, stored[h], 16 * uses, m.passed)
                sp.sem_inc(rows_free[h], 1)

            body(0, 0, 1)
            with sp.Fori(0, SB // 2) as k:
                body(2 * k + 1, 1, k + 1)
                body(2 * k + 2, 0, k + 2)


def project(nc, m, x1, wq, bq, wk, bk, wv, qs, ks, vd):
    with ExitStack() as ctx:
        sb = lambda name, shape, dt: ctx.enter_context(nc.sbuf_tensor("prj_" + name, shape, dt))
        w = sb("w", [P, 3, D], F32)
        b2 = sb("b2", [P, 2], F32)
        xr = sb("xr", [RB, RPC, D], F32)
        xt = sb("xt", [P, CW], F32)
        qk = [sb(f"qk{k}", [P, CW], F32) for k in range(2)]
        pieces = [sb(f"pieces{k}", [P, 3, CW], BF16) for k in range(2)]
        vals = sb("vals", [RB, RPC, HEADS, VW], F32)
        onesb = sb("onesb", [3, ND], BF16)
        zeros = sb("zeros", [P, HEADS, ND - NP], BF16)
        zerov = sb("zerov", [ND - NP, HEADS * VW], F32)
        names = "w_loaded rows_loaded turned xt_ready made relued step split valued stored vset oned padded out_free".split()
        sems = {n: ctx.enter_context(nc.semaphore("prj_" + n)) for n in names}
        w_loaded, rows_loaded, turned, xt_ready, made, relued, step, split, valued, stored, vset, oned, \
            padded, out_free = \
            (sems[n] for n in names)
        block = ctx.enter_context(nc.Block())
        per = 2 * NX + 1

        @block.sync
        def _(sp):
            sp.sem_inc(out_free, 1)
            for k, a in enumerate((wq, wk, wv)):
                sp.dma_start(w[:, k, :], a).then_inc(w_loaded, 16)
            for k, a in enumerate((bq, bk)):
                sp.dma_start(b2[:, k:k + 1], a.rearrange("(p a) -> p a", a=1)).then_inc(w_loaded, 16)
            sp.wait_ge(oned, 1)
            for h in range(HEADS):
                sp.dma_start(ks[KS:KM, h, :], onesb[:, :]).then_inc(padded, 16)
            for a in (qs, ks):
                sp.dma_start(a[0:KS, :, NP:ND], zeros[0:KS, :, :]).then_inc(padded, 16)
            sp.dma_start(vd[NP:ND, :], zerov[:, :]).then_inc(padded, 16)
            with sp.Fori(0, NC) as c:
                hold(sp, turned, 1 + c, m.passed)
                sp.dma_start(xr[:, :, :], chunk_rows(x1, c)).then_inc(rows_loaded, 16)
                hold(sp, valued, 1 + c + 1, m.passed)
                sp.dma_start(vd[ds(c * CW, CW), :].rearrange("(j p) f -> p j f", p=RB),
                             vals[:, :, :, :].rearrange("p j h w -> p j (h w)")).then_inc(stored, 16)
                hold(sp, split, 1 + 2 * (c + 1), m.passed)
                for k, (pcs, a) in enumerate(((Q_PIECES, qs), (K_PIECES, ks))):
                    for g in range(NX):
                        sp.dma_start(a[g * HD:(g + 1) * HD, :, ds(c * CW, CW)].rearrange("r h n -> h r n"),
                                     pieces[k][:, pcs[g], :]).then_inc(stored, 16)
                hold(sp, stored, 16 * per * (c + 1), m.passed)
                sp.sem_inc(out_free, 1)
            sp.wait_ge(padded, 16 * (3 + HEADS))

        @block.tensor
        def _(pe):
            pe.sem_inc(turned, 1)
            pe.sem_inc(made, 1)
            pe.wait_ge(w_loaded, 80)
            with pe.Fori(0, NC) as c:
                pe.wait_ge(rows_loaded, 16 * (c + 1))
                for j in range(RPC):
                    last = nc.tensor.transpose(m.bank[0][:, j * RB:(j + 1) * RB], xr[:, j, :], m.ident[0:RB, 0:RB])
                last.then_inc(turned, 1)
                pe.wait_ge(xt_ready, c + 1)
                for k in range(2):
                    pe.wait_ge(relued, 1 + 2 * c)
                    nc.tensor.matmul(m.bank[1 + k][:, 0:CW], w[:, k, :], xt[:, :], start=True, stop=True)\
                      .then_inc(made, 1)
                pe.wait_ge(valued, 1 + c)
                for j in range(RPC):
                    last = nc.tensor.matmul(m.bank[3][0:RB, j * D:(j + 1) * D], xt[:, j * RB:(j + 1) * RB],
                                            w[:, 2, :], start=True, stop=True)
                last.then_inc(made, 1)

        @block.scalar
        def _(act):
            act.sem_inc(relued, 1)
            act.wait_ge(w_loaded, 80)
            with act.Fori(0, NC) as c:
                act.wait_ge(turned, 1 + c + 1)
                act.wait_ge(made, 1 + 3 * c)
                nc.scalar.activation(xt[:, :], m.bank[0][:, 0:CW], ACT.Copy).then_inc(xt_ready, 1)
                act.wait_ge(split, 1 + 2 * c)
                for k in range(2):
                    act.wait_ge(made, 1 + 3 * c + k + 1)
                    nc.scalar.activation(qk[k][:, :], m.bank[1 + k][:, 0:CW], ACT.Relu, bias=b2[:, k:k + 1])\
                      .then_inc(relued, 1)

        @block.vector
        def _(v):
            v.sem_inc(valued, 1)
            v.sem_inc(split, 1)
            v.memset(zeros[:, :, :], 0.0)
            v.memset(zerov[:, :], 0.0)
            v.memset(onesb[:, :], 1.0).then_inc(oned, 1)
            v.memset(vals[:, :, :, HD + 1:VW], 0.0)
            v.memset(vals[:, :, :, HD:HD + 1], 1.0).then_inc(vset, 1)
            v.wait_ge(vset, 1)
            with v.Fori(0, NC) as c:
                s = Steps(v, step, 6 * c)
                v.wait_ge(out_free, c + 1)
                for k in range(2):
                    v.wait_ge(relued, 1 + 2 * c + k + 1)
                    s.link(v.tensor_copy(pieces[k][:, 0, :], qk[k][:, :]))
                    s.link(v.tensor_tensor(qk[k][:, :], qk[k][:, :], pieces[k][:, 0, :], op=ALU.subtract))
                    s.link(v.tensor_copy(pieces[k][:, 1, :], qk[k][:, :]))
                    v.tensor_tensor(pieces[k][:, 2, :], qk[k][:, :], pieces[k][:, 1, :], op=ALU.subtract)\
                     .then_inc(split, 1)
                v.wait_ge(made, 1 + 3 * c + 3)
                v.tensor_copy(vals[:, :, :, 0:HD],
                              m.bank[3][0:RB, :].rearrange("p (j h f) -> p j h f", j=RPC, h=HEADS))\
                 .then_inc(valued, 1)


def score_maxima(nc, m, qs, ks):
    with ExitStack() as ctx:
        sb = lambda name, shape, dt: ctx.enter_context(nc.sbuf_tensor("max_" + name, shape, dt))
        HH = HEADS // 2
        mall = sb("mall", [P, SB, HEADS], F32)
        with ExitStack() as c2:
            sb2 = lambda name, shape, dt: c2.enter_context(nc.sbuf_tensor("max_" + name, shape, dt))
            kk = sb2("keys", [KS, HH, NP], BF16)
            q = [sb2(f"q{i}", [KS, HH, P], BF16) for i in range(2)]
            mask = [sb2(f"mask{i}", [P, NC, CW], BF16) for i in range(2)]
            mx = [sb2(f"mx{i}", [P, HH, len(PARTS)], F32) for i in range(2)]
            names = "keys_loaded q_used scored maxed masked stepped".split()
            sems = {n: c2.enter_context(nc.semaphore("max_" + n)) for n in names}
            keys_loaded, q_used, scored, maxed, masked, stepped = (sems[n] for n in names)
            block = c2.enter_context(nc.Block())
            q_loaded = [c2.enter_context(nc.semaphore(f"max_q_loaded{i}")) for i in range(2)]
            NPT = len(PARTS)
            per = NPT * HH

            @block.sync
            def _(sp):
                for hh in range(2):
                    at = hh * SB
                    if hh:
                        sp.wait_ge(q_used, SB + 1)
                    sp.dma_start(kk[:, :, :], ks[0:KS, hh * HH:(hh + 1) * HH, 0:NP]).then_inc(keys_loaded, 16)

                    def load(b, slot, used):
                        if used is not None:
                            hold(sp, q_used, used + 1, m.passed)
                        sp.dma_start(q[slot][:, :, :], qs[0:KS, hh * HH:(hh + 1) * HH, ds(b * P, P)])\
                          .then_inc(q_loaded[slot], 16)

                    load(0, at % 2, None if hh == 0 else at - 1)
                    with sp.Fori(0, SB // 2) as i:
                        load(2 * i + 1, (at + 1) % 2, at + 2 * i)
                        load(2 * i + 2, at % 2, at + 2 * i + 1)

            @block.tensor
            def _(pe):
                for hh in range(2):
                    at = hh * SB

                    def scores(b, slot, uses):
                        r = at + b
                        pe.wait_ge(q_loaded[slot], 16 * uses)
                        for h in range(HH):
                            for part, (lo, hi) in enumerate(PARTS):
                                pe.wait_ge(maxed, per * r + NPT * h + part + 1)
                                for k in range(lo, hi):
                                    last = nc.tensor.matmul(m.bank[k][:, 0:CW], q[slot][:, h, :],
                                                            kk[:, h, k * CW:(k + 1) * CW], start=True, stop=True)
                                last.then_inc(scored, 1)

                    pe.wait_ge(keys_loaded, 16 * (hh + 1))
                    scores(0, at % 2, at // 2 + 1)
                    with pe.Fori(0, SB // 2) as i:
                        scores(2 * i + 1, (at + 1) % 2, (at + 1) // 2 + 1 + i)
                        scores(2 * i + 2, at % 2, (at + 2) // 2 + 1 + i)

            @block.scalar
            def _(act):
                def make(b, r):
                    if not (isinstance(r, int) and r < 2):
                        act.wait_ge(q_used, r)
                    return m.at[:, ds(b, 1), 0:NP].rearrange("p a (k n) -> p (a k) n", n=CW)

                for hh in range(2):
                    at = hh * SB
                    nc.scalar.activation(mask[at % 2][:, :, :], make(0, at), ACT.Sign).then_inc(masked, 1)
                    with act.Fori(0, SB // 2) as i:
                        for z in (1, 2):
                            nc.scalar.activation(mask[(at + z) % 2][:, :, :], make(2 * i + z, at + 2 * i + z),
                                                 ACT.Sign).then_inc(masked, 1)

            @block.vector
            def _(v):
                v.sem_inc(q_used, 1)
                v.memset(mx[0][:, :, :], 0.0).then_inc(maxed, NPT)
                v.wait_ge(maxed, NPT)

                def head(r, h, slot):
                    for part, (lo, hi) in enumerate(PARTS):
                        hold(v, scored, per * r + NPT * h + part + 1, m.passed)
                        v.tensor_tensor_reduce(
                            out=m.ps[:, lo:hi, 0:CW], in0=m.ps[:, lo:hi, 0:CW], in1=mask[slot][:, lo:hi, :],
                            scale=1.0, scalar=0.0, op0=ALU.mult, op1=ALU.max,
                            accum_out=mx[slot][:, h, part:part + 1]).then_inc(maxed, 1)

                def finish(b, r, hh, slot):
                    v.wait_ge(maxed, per * (r + 1) + NPT)
                    v.tensor_reduce(mall[:, ds(b, 1), hh * HH:(hh + 1) * HH].rearrange("p a h -> p (a h)"),
                                    mx[slot][:, :, :], axis=AX.X, op=ALU.max).then_inc(q_used, 1)

                for hh in range(2):
                    at = hh * SB

                    def body(b, r, slot, before):
                        hold(v, masked, r + 1, m.passed)
                        head(r, 0, slot)
                        if before is not None:
                            finish(before, r - 1, hh, 1 - slot)
                        for h in range(1, HH):
                            head(r, h, slot)

                    body(0, at, at % 2, None)
                    with v.Fori(0, SB // 2) as i:
                        body(2 * i + 1, at + 2 * i + 1, (at + 1) % 2, 2 * i)
                        body(2 * i + 2, at + 2 * i + 2, at % 2, 2 * i + 1)
                    finish(SB - 1, at + SB - 1, hh, at % 2)
        with ExitStack() as c2:
            sb2 = lambda name, shape, dt: c2.enter_context(nc.sbuf_tensor("neg_" + name, shape, dt))
            pcs = sb2("pieces", [P, SB, 3, HEADS], BF16)
            rows = sb2("rows", [3 * HEADS, ND], BF16)
            step = c2.enter_context(nc.semaphore("neg_step"))
            split = c2.enter_context(nc.semaphore("neg_split"))
            turned = c2.enter_context(nc.semaphore("neg_turned"))
            rowed = c2.enter_context(nc.semaphore("neg_rowed"))
            stored = c2.enter_context(nc.semaphore("neg_stored"))
            block = c2.enter_context(nc.Block())

            @block.vector
            def _(v):
                s = Steps(v, step)
                s.link(v.tensor_single_scalar(mall[:, :, :], mall[:, :, :], -1.0, op=ALU.mult))
                split3(v, s, [pcs[:, :, k, :] for k in range(3)], mall[:, :, :])
                v.memset(rows[0:1, 0:1], 0.0).then_inc(split, 1)
                v.wait_ge(split, 1)
                v.wait_ge(turned, 1)
                v.tensor_copy(rows[:, 0:6 * 512].rearrange("p (k n) -> p k n", n=512), m.ps[0:3 * HEADS, 0:6, :])
                v.tensor_copy(rows[:, 6 * 512:ND], m.ps[0:3 * HEADS, 6, 0:P]).then_inc(rowed, 1)

            @block.tensor
            def _(pe):
                pe.wait_ge(split, 1)
                for b in range(SB):
                    last = nc.tensor.matmul(m.bank[b // 4][0:3 * HEADS, (b % 4) * P:(b % 4 + 1) * P],
                                            pcs[:, b, :, :], m.identb[:, :], start=True, stop=True)
                last.then_inc(turned, 1)

            @block.sync
            def _(sp):
                sp.wait_ge(rowed, 1)
                for k in range(3):
                    sp.dma_start(qs[KS + k, :, :], rows[k * HEADS:(k + 1) * HEADS, :]).then_inc(stored, 16)
                sp.wait_ge(stored, 48)


def attend(nc, m, x1, qs, ks, vd, ad, bias, out):
    with ExitStack() as ctx:
        sb = lambda name, shape, dt: ctx.enter_context(nc.sbuf_tensor("att_" + name, shape, dt))
        q = sb("q", [KM, HEADS, CW], BF16)
        k = [sb(f"k{i}", [KM, HEADS, P], BF16) for i in range(DG)]
        vv = [sb(f"v{i}", [P, HEADS, VW], F32) for i in range(DG)]
        a = [sb(f"a{i}", [P, CW], BF16) for i in range(DG)]
        e = [sb(f"e{i}", [P, 2, CW], F32) for i in range(NE)]
        acc = e[0]
        bb = sb("bias", [RB, D], F32)
        xr = sb("xr", [RB, RPC, D], F32)
        y = sb("y", [RB, RPC, D], F32)
        o = y
        rden = sb("rden", [RB, 2, RPC, HEADS // 2], F32)
        st = sb("st", [RB, RPC, 6], F32)
        mv = sb("mv", [RB, RPC, 2], F32)
        sd = sb("sd", [RB, RPC], F32)
        names = ("b_loaded q_loaded x_loaded scored exped weighed summed acc_ready turned step "
                 "normed rooted finished stored out_free turned_used").split()
        sems = {n: ctx.enter_context(nc.semaphore("att_" + n)) for n in names}
        (b_loaded, q_loaded, x_loaded, scored, exped, weighed, summed, acc_ready, turned, step,
         normed, rooted, finished, stored, out_free, turned_used) = (sems[n] for n in names)
        slot_loaded = [ctx.enter_context(nc.semaphore(f"att_slot{i}")) for i in range(DG)]
        block = ctx.enter_context(nc.Block())
        HP = HEADS // 2
        PB = SB * HP
        E0, S0 = 2, DG * HP // 2

        @block.sync
        def _(sp):
            with sp.Fori(0, NC) as c:
                hold(sp, turned, 1 + c, m.passed)
                sp.dma_start(q[:, :, :], qs[:, :, ds(c * CW, CW)]).then_inc(q_loaded, 16)
                with sp.Fori(0, NDG) as g:
                    for i in range(DG):
                        hold(sp, summed, HP // 2 * ((c * NDG + g) * DG + i + 1), m.passed)
                        row = (g * DG + i) * P
                        sp.dma_start(k[i][:, :, :], ks[:, :, ds(row, P)]).then_inc(slot_loaded[i], 16)
                        sp.dma_start(a[i][:, :], ad[ds(row, P), ds(c * CW, CW)]).then_inc(slot_loaded[i], 16)
                        sp.dma_start(vv[i][:, :, :], vd[ds(row, P), :].rearrange("p (h w) -> p h w", w=VW))\
                          .then_inc(slot_loaded[i], 16)

        @block.gpsimd
        def _(pool):
            pool.sem_inc(out_free, 1)
            pool.dma_start(bb[:, :], bias.unsqueeze(0).to_broadcast([RB, D])).then_inc(b_loaded, 16)
            with pool.Fori(0, NC) as c:
                hold(pool, finished, 1 + c, m.passed)
                pool.dma_start(xr[:, :, :], chunk_rows(x1, c)).then_inc(x_loaded, 16)
                inverse_roots(pool, m, mv, sd, normed, rooted, c)
                hold(pool, finished, 1 + c + 1, m.passed)
                pool.dma_start(chunk_rows(out, c), o[:, :, :]).then_inc(stored, 16)
                hold(pool, stored, 16 * (c + 1), m.passed)
                pool.sem_inc(out_free, 1)

        @block.tensor
        def _(pe):
            pe.sem_inc(turned, 1)
            with pe.Fori(0, NC) as c:
                pe.wait_ge(q_loaded, 16 * (c + 1))

                def scores(n, i, h):
                    j = i * HP + h
                    pe.wait_ge(exped, n - (1 if j < 2 else 2) + E0)
                    for z in range(2):
                        last = nc.tensor.matmul(m.bank[2 * (j % NS) + z][:, 0:CW], k[i][:, 2 * h + z, :],
                                                q[:, 2 * h + z, :], start=True, stop=True)
                    last.then_inc(scored, 1)

                def sums(n, j, start, stop):
                    pe.wait_ge(weighed, n + 1)
                    for z in range(4):
                        head = 2 * (j % HP - 1) + z
                        last = nc.tensor.matmul(m.bank[2 * NS + head // 4][VW * z:VW * (z + 1), 0:CW],
                                                vv[j // HP][:, head, :], e[(j - 1 + z // 2) % NE][:, z % 2, :],
                                                start=start, stop=stop)
                    last.then_inc(summed, 1)

                def group(g, first):
                    n0 = (c * SB + g * DG) * HP
                    for i in range(DG):
                        pe.wait_ge(slot_loaded[i], 48 * (c * NDG + g + 1))
                        for h in range(HP):
                            j = i * HP + h
                            scores(n0 + j, i, h)
                            if j % 2 == 0 and j < 4 and not first:
                                sums(n0 + j - 3, DG * HP + j - 3, False, False)
                            if first and j == 4:
                                pe.wait_ge(turned_used, c + 1)
                            if j % 2 == 0 and j >= 4:
                                sums(n0 + j - 3, j - 3, first and j - 3 < HP, False)

                group(0, True)
                with pe.Fori(1, NDG - 1) as g:
                    group(g, False)
                group(NDG - 1, False)
                n1 = (c + 1) * SB * HP
                for j in (DG * HP - 3, DG * HP - 1):
                    sums(n1 - DG * HP + j, j, False, True)
                pe.wait_ge(acc_ready, c + 1)
                for z in range(2):
                    for j in range(RPC):
                        last = nc.tensor.transpose(m.bank[2 * NS + z][0:RB, j * P:(j + 1) * P],
                                                   acc[:, z, j * RB:(j + 1) * RB], m.ident[:, :])
                last.then_inc(turned, 1)

        @block.scalar
        def _(act):
            act.sem_inc(exped, E0)
            with act.Fori(0, NC) as c:
                act.wait_ge(turned, c + 1)
                with act.Fori(0, NDG) as g:
                    for j in range(DG * HP):
                        n = (c * NDG + g) * DG * HP + j
                        old = j - NE + 1 - (j - NE) % 2
                        act.wait_ge(summed, (c * NDG + g) * (DG * HP // 2) + (old + 1) // 2 + S0)
                        act.wait_ge(scored, n + 1)
                        nc.scalar.activation(e[j % NE][:, :, :], m.ps[:, 2 * (j % NS):2 * (j % NS) + 2, 0:CW],
                                             ACT.Exp).then_inc(exped, 1)

        @block.vector
        def _(v):
            v.sem_inc(finished, 1)
            v.sem_inc(turned_used, 1)
            v.sem_inc(summed, S0)
            v.wait_ge(b_loaded, 16)
            with v.Fori(0, NC) as c:
                with v.Fori(0, NDG) as g:
                    for i in range(DG):
                        v.wait_ge(slot_loaded[i], 48 * (c * NDG + g + 1))
                        for h in range(HP):
                            n = ((c * NDG + g) * DG + i) * HP + h
                            w = e[(i * HP + h) % NE][:, :, :]
                            v.wait_ge(exped, n + 1 + E0)
                            v.scalar_tensor_tensor(w, w, 1.0,
                                                   a[i][:, :].unsqueeze(1).to_broadcast([P, 2, CW]),
                                                   op0=ALU.min, op1=ALU.mult).then_inc(weighed, 1)
                s = Steps(v, step, (6 + RPC + 1) * c)
                v.wait_ge(summed, PB // 2 * (c + 1) + S0)
                v.tensor_copy(acc[:, :, :], m.ps[:, 2 * NS:2 * NS + 2, 0:CW]).then_inc(acc_ready, 1)
                v.wait_ge(turned, 1 + c + 1)
                v.wait_ge(out_free, c + 1)
                sums = [m.bank[2 * NS + z][0:RB, :].rearrange("p (j h w) -> p j h w", j=RPC, w=VW) for z in range(2)]
                for z in range(2):
                    s.done(v.reciprocal(rden[:, z, :, :], sums[z][:, :, :, HD]))
                s.wait()
                half = D // 2
                for z in range(2):
                    s.done(v.tensor_tensor(y[:, :, z * half:(z + 1) * half].rearrange("p j (h f) -> p j h f", f=HD),
                                           sums[z][:, :, :, 0:HD],
                                           rden[:, z, :, :].unsqueeze(3).to_broadcast([RB, RPC, HEADS // 2, HD]),
                                           op=ALU.mult))
                v.wait_ge(x_loaded, 16 * (c + 1))
                s.wait()
                v.sem_inc(turned_used, 1)
                s.link(v.tensor_tensor(xr[:, :, :], xr[:, :, :], bb[:, :].unsqueeze(1).to_broadcast([RB, RPC, D]),
                                       op=ALU.add))
                s.link(v.tensor_tensor(y[:, :, :], y[:, :, :], xr[:, :, :], op=ALU.add))
                layer_norm(v, s, m, y, o, st, mv, sd, normed, rooted, c).then_inc(finished, 1)
                assert s.n == 6 + RPC + 1


def pad_input(nc, m, x, x_pad, states):
    with ExitStack() as ctx:
        zeros = ctx.enter_context(nc.sbuf_tensor("pad_zeros", [ND - N, D], F32))
        zeroed = ctx.enter_context(nc.semaphore("pad_zeroed"))
        stored = ctx.enter_context(nc.semaphore("pad_stored"))
        block = ctx.enter_context(nc.Block())

        @block.vector
        def _(v):
            v.memset(zeros[:, :], 0.0).then_inc(zeroed, 1)

        @block.sync
        def _(sp):
            sp.dma_start(x_pad[0:N, :], x).then_inc(stored, 16)
            sp.wait_ge(zeroed, 1)
            sp.dma_start(x_pad[N:ND, :], zeros[:, :]).then_inc(stored, 16)
            for a in states:
                sp.dma_start(a[NP:ND, :], zeros[0:ND - NP, :]).then_inc(stored, 16)
            sp.wait_ge(stored, 16 * (2 + len(states)))


def build_program(nc, x, src, dst, edge_type_500, L0_gnn_rel_emb, L0_gnn_W_neighbor, L0_gnn_loop_weight,
                  L1_gnn_query_kernel, L1_gnn_query_bias, L1_gnn_key_kernel, L1_gnn_key_bias, L1_gnn_kernel,
                  L1_gnn_bias, L2_gnn_weight, L3_gnn_W1, L3_gnn_b1, L3_gnn_W2, L3_gnn_b2, out):
    def dram(name, shape, dt):
        return nc.dram_tensor(name, shape, dt, kind="Internal").ap()

    x0, x1, x2, x3, x4 = (dram(f"state{i}", [ND, D], F32) for i in range(5))
    base_d, deg_d, aggr_d = dram("base_d", [NT], I32), dram("deg_d", [ND], F32), dram("aggr_d", [P, NP], F32)
    qs, ks = (dram(n, [KM, HEADS, ND], BF16) for n in ("queries", "keys"))
    vd, ad = dram("values", [ND, HEADS * VW], F32), dram("counts_turned", [ND, NP], BF16)

    with ExitStack() as ctx:
        sb = lambda name, shape, dt: ctx.enter_context(nc.sbuf_tensor(name, shape, dt))
        m = allocate(nc, ctx)
        m.in_norm = sb("in_norm", [RB, NRB], F32)
        m.loop_norm = sb("loop_norm", [RB, NRB], F32)
        m.loop_norm_s = sb("loop_norm_s", [P, SB], F32)
        m.out_norm = sb("out_norm", [P, SB], F32)
        m.at = sb("at", [P, SB, ND], BF16)
        pad_input(nc, m, x, x0, (x1, x2, x3, x4))
        with ExitStack() as tctx:
            t = Mem()
            tb = lambda name, shape, dt: tctx.enter_context(nc.sbuf_tensor(name, shape, dt))
            t.bad = tb("bad", [1, 1], I32)
            t.iota = tb("iota", [P, W * SB], F16)
            t.base = tb("base", [1, NT], I32)
            t.key = [tb(f"key{k}", [P, NT], F16) for k in range(4)]
            t.far = tb("far", [P, 2 * NT], F32)
            t.key += [t.far[:, 0:NT], t.far[:, NT:NT + NT // 2].bitcast(F16), t.far[:, NT + NT // 2:2 * NT].bitcast(F16)]
            with ExitStack() as ectx:
                edge_tables(nc, m, src, dst, edge_type_500, base_d, t)
            t.rt = tb("rt", [P, TB, NP], BF16)
            count_edges(nc, m, t)
            relation_sums(nc, m, t, L0_gnn_rel_emb, aggr_d)
        degrees(nc, m, deg_d)

        def conv(tag, rows, scale, *args, **kwargs):
            with ExitStack() as c2:
                parts = [c2.enter_context(nc.sbuf_tensor(f"{tag}_part{k}", [P, SB, D], BF16)) for k in range(3)]
                load_and_split(nc, m, tag, rows, scale, parts)
                graph_conv(nc, m, tag, parts, *args, **kwargs)

        conv("L0", x0, None, L0_gnn_W_neighbor, m.in_norm, x1, residual=x0, loop_weight=L0_gnn_loop_weight,
             aggr_d=aggr_d, relu=True)
        add_loops(nc, m, "L1", 1)
        turn_counts(nc, m, ad)
        project(nc, m, x1, L1_gnn_query_kernel, L1_gnn_query_bias, L1_gnn_key_kernel, L1_gnn_key_bias,
                L1_gnn_kernel, qs, ks, vd)
        score_maxima(nc, m, qs, ks)
        attend(nc, m, x1, qs, ks, vd, ad, L1_gnn_bias, x2)
        add_loops(nc, m, "L2", -1)
        conv("L2", x2, m.out_norm, L2_gnn_weight, m.in_norm, x3, residual=x2)
        add_loops(nc, m, "L3", 1)
        conv("L3a", x3, m.loop_norm_s, L3_gnn_W1, m.loop_norm, x4, bias=L3_gnn_b1, relu=True, norm=False)
        conv("L3b", x4, m.loop_norm_s, L3_gnn_W2, m.loop_norm, out, residual=x3, bias=L3_gnn_b2)


_NAMES = ["x", "src", "dst", "edge_type_500", "L0_gnn_rel_emb", "L0_gnn_W_neighbor", "L0_gnn_loop_weight",
          "L1_gnn_query_kernel", "L1_gnn_query_bias", "L1_gnn_key_kernel", "L1_gnn_key_bias", "L1_gnn_kernel",
          "L1_gnn_bias", "L2_gnn_weight", "L3_gnn_W1", "L3_gnn_b1", "L3_gnn_W2", "L3_gnn_b2"]


def kernel(**inputs):
    import numpy as np
    import concourse.bacc as bacc
    from concourse.bass_utils import run_bass_kernel_spmd

    nc = bacc.Bacc("TRN2", target_bir_lowering=False, num_devices=1)
    arrays, args = {}, []
    for name in _NAMES:
        a = np.ascontiguousarray(inputs[name])
        arrays[f"in_{name}"] = a
        args.append(nc.dram_tensor(f"in_{name}", a.shape, mybir.dt.from_np(a.dtype), kind="ExternalInput").ap())
    args.append(nc.dram_tensor("out", (N, D), F32, kind="ExternalOutput").ap())
    build_program(nc, *args)
    result = run_bass_kernel_spmd(nc, [arrays], core_ids=[0])
    return result.results[0]["out"]
```

```python
import concourse.bass as bass
from concourse import mybir
from contextlib import ExitStack

F32, BF16, F16, I32 = mybir.dt.float32, mybir.dt.bfloat16, mybir.dt.float16, mybir.dt.int32
ALU = mybir.AluOpType
ACT = mybir.ActivationFunctionType
AX = mybir.AxisListType
ds = bass.ds

N = 3125
E = 100000
D = 128
P = 128
NREL = 500
SB = -(-N // P)
TB = -(-NREL // P)
CW = 448
NC = -(-N // CW)
NP = NC * CW
EPS = 1e-5
RB = 112
RPC = CW // RB
NRB = NP // RB
W = 12
ND = SB * P
TG = 112
NG = 7
NT = TG * NG
TF = E // P
TR = E - TF * P
U = 4
NU = NT // U


class Steps:

    def __init__(self, eng, sem, base=0):
        self.eng, self.sem, self.base, self.n = eng, sem, base, 0

    def done(self, ins):
        self.n += 1
        ins.then_inc(self.sem, 1)

    def done_here(self):
        self.n += 1
        self.eng.sem_inc(self.sem, 1)

    def wait(self):
        self.eng.wait_ge(self.sem, self.base + self.n)

    def link(self, ins):
        self.done(ins)
        self.wait()


def hold(eng, sem, value, passed):
    eng.wait_ge(sem, value)
    eng.sem_inc(passed, 1)


class Mem:
    pass


def allocate(nc, ctx):
    m = Mem()
    sb = lambda name, shape, dt: ctx.enter_context(nc.sbuf_tensor(name, shape, dt))
    m.ident = sb("ident", [P, P], F32)
    m.identb = sb("identb", [P, P], BF16)
    m.eps = sb("eps", [P, RPC], F32)
    m.passed = ctx.enter_context(nc.semaphore("passed"))
    m.minus_half = sb("minus_half", [P, SB + NRB], F32)
    m.ps = ctx.enter_context(nc.psum_tensor("ps", [P, 8, 512], F32))
    m.bank = [m.ps[:, i, :] for i in range(8)]
    return m


def edge_tables(nc, m, src, dst, typ, base_d, t):
    with ExitStack() as ctx:
        sb = lambda name, shape, dt: ctx.enter_context(nc.sbuf_tensor(name, shape, dt))
        flat = m.at[:, :, :].rearrange("p b d -> p (b d)")[0:TG, :].bitcast(F32)
        size, at = NG * P, [0]

        def carve(k, dt):
            at[0] += k * size
            return flat[:, at[0] - k * size:at[0]].bitcast(dt).rearrange("p (k g e) -> p k g e", k=k, e=P)

        raw = carve(3, I32)
        low = carve(2, I32)
        blk = carve(2, I32)
        fl = carve(7, F32)
        dstf = carve(1, F32)[:, 0]
        bf = carve(2, F32)
        mn = sb("mn", [TG, NG], F32)
        mx = sb("mx", [TG, NG], F32)
        mni = sb("mni", [TG, NG], I32)
        span = sb("span", [TG, NG], F32)
        worst = sb("worst", [TG, 1], F32)
        badf = sb("badf", [1, 1], F32)
        loaded = ctx.enter_context(nc.semaphore("edges_loaded"))
        based = ctx.enter_context(nc.semaphore("bases_stored"))
        baseb = ctx.enter_context(nc.semaphore("bases_back"))
        ready = ctx.enter_context(nc.semaphore("tables_ready"))
        mnready = ctx.enter_context(nc.semaphore("mins_ready"))
        idr = ctx.enter_context(nc.semaphore("ident_ready"))
        turned = ctx.enter_context(nc.semaphore("tables_turned"))
        freed = ctx.enter_context(nc.semaphore("banks_freed"))
        dstep = ctx.enter_context(nc.semaphore("dve_step"))
        zeroed = ctx.enter_context(nc.semaphore("pool_step"))
        block = ctx.enter_context(nc.Block())
        G6 = (NG - 1) * TG * P

        @block.sync
        def _(sp):
            for k, a in enumerate((dst, src, typ)):
                sp.dma_start(raw[:, k, 0:NG - 1, :],
                             a[0:G6].rearrange("(g p e) -> p g e", g=NG - 1, e=P)).then_inc(loaded, 16)
                sp.dma_start(raw[0:TF - (NG - 1) * TG, k, NG - 1, :],
                             a[G6:TF * P].rearrange("(p e) -> p e", e=P)).then_inc(loaded, 16)
                r = TF - (NG - 1) * TG
                sp.dma_start(raw[r:r + 1, k, NG - 1, 0:TR], a[TF * P:E].rearrange("(p e) -> p e", p=1))\
                  .then_inc(loaded, 16)
                sp.dma_start(raw[r:r + 1, k, NG - 1, TR:P], a[E - P + TR:E].rearrange("(p e) -> p e", p=1))\
                  .then_inc(loaded, 16)
                for q in range(r + 1, TG):
                    sp.dma_start(raw[q:q + 1, k, NG - 1, :], a[E - P:E].rearrange("(p e) -> p e", p=1))\
                      .then_inc(loaded, 16)
            sp.wait_ge(mnready, 1)
            sp.dma_start(base_d.rearrange("(g p) -> p g", p=TG), mni[:, :],
                         allow_slow_non_contiguous=True).then_inc(based, 16)
            sp.wait_ge(based, 16)
            sp.dma_start(t.base[0:1, :], base_d.rearrange("(a n) -> a n", a=1)).then_inc(baseb, 16)
            sp.wait_ge(baseb, 16)

        @block.gpsimd
        def _(pool):
            pool.memset(m.ident[:, :], 0.0)
            pool.memset(m.identb[:, :], 0.0).then_inc(zeroed, 1)
            pool.wait_ge(zeroed, 1)
            pool.affine_select(out=m.ident[:, :], in_=m.ident[:, :], compare_op=ALU.not_equal, fill=1.0,
                               base=0, pattern=[[-1, P]], channel_multiplier=1).then_inc(idr, 1)
            pool.memset(m.minus_half[:, :], -0.5)
            pool.memset(m.eps[:, :], EPS)
            pool.affine_select(out=m.identb[:, :], in_=m.identb[:, :], compare_op=ALU.not_equal, fill=1.0,
                               base=0, pattern=[[-1, P]], channel_multiplier=1)
            pool.iota(t.iota[:, :], [[1, W * SB]], base=0, channel_multiplier=0,
                      allow_small_or_imprecise_dtypes=True)

        @block.vector
        def _(v):
            s = Steps(v, dstep)
            v.wait_ge(loaded, 16 * 3 * (4 + TG - 1 - (TF - (NG - 1) * TG)))
            for k in range(2):
                s.done(v.tensor_single_scalar(blk[:, k], raw[:, 1 + k], 7, op=ALU.arith_shift_right))
                s.done(v.tensor_single_scalar(low[:, k], raw[:, 1 + k], P - 1, op=ALU.bitwise_and))
            s.link(v.tensor_copy(dstf[:, :, :], raw[:, 0]))
            s.done(v.tensor_copy(bf[:, :], blk[:, :]))
            s.done(v.tensor_copy(fl[:, 2:4], low[:, :]))
            s.done(v.tensor_reduce(mn[:, :], dstf[:, :, :], axis=AX.X, op=ALU.min))
            s.link(v.tensor_reduce(mx[:, :], dstf[:, :, :], axis=AX.X, op=ALU.max))
            s.done(v.tensor_copy(mni[:, :], mn[:, :]))
            s.link(v.tensor_tensor(span[:, :], mx[:, :], mn[:, :], op=ALU.subtract))
            s.link(v.tensor_reduce(worst[:, :], span[:, :], axis=AX.X, op=ALU.max))
            nb = mn[:, :].unsqueeze(2).to_broadcast([TG, NG, P])
            s.done(v.tensor_copy(fl[:, 4], dstf[:, :, :]))
            s.done(v.tensor_single_scalar(fl[:, 5:7], bf[:, :], float(W), op=ALU.mult))
            v.memset(badf[:, :], 0.0).then_inc(mnready, 1)
            s.wait()
            s.link(v.tensor_tensor(dstf[:, :, :], dstf[:, :, :], nb, op=ALU.subtract))
            s.done(v.scalar_tensor_tensor(fl[:, 0], bf[:, 0], float(W), dstf[:, :, :], op0=ALU.mult, op1=ALU.add))
            v.scalar_tensor_tensor(fl[:, 1], bf[:, 1], float(W), dstf[:, :, :], op0=ALU.mult, op1=ALU.add)\
             .then_inc(ready, 1)
            for j in range(14):
                k, h = j // 2, j % 2
                n = 4 * TG if h == 0 else 3 * TG
                v.wait_ge(turned, j + 1)
                v.tensor_copy(t.key[k][:, h * 4 * TG:h * 4 * TG + n], m.bank[j % 6][:, 0:n]).then_inc(freed, 1)
            v.wait_ge(freed, 14)
            for k in (2, 3):
                s.done(v.memset(t.key[k][TR:64, TF:TF + 1], -1.0))
                s.done(v.memset(t.key[k][64:P, TF:TF + 1], -1.0))
                s.done(v.memset(t.key[k][:, TF + 1:NT], -1.0))
            v.wait_ge(turned, 15)
            s.link(v.tensor_reduce(badf[:, :], m.bank[7][0:1, 0:TG], axis=AX.X, op=ALU.max))
            s.link(v.tensor_single_scalar(badf[:, :], badf[:, :], float(W - 1), op=ALU.is_gt))
            s.link(v.tensor_copy(t.bad[0:1, 0:1], badf[:, :]))

        @block.tensor
        def _(pe):
            pe.wait_ge(idr, 1)
            pe.wait_ge(ready, 1)
            for j in range(14):
                k, h = j // 2, j % 2
                if j >= 6:
                    pe.wait_ge(freed, j - 5)
                for g in range(4 if h == 0 else 3):
                    last = nc.tensor.transpose(m.bank[j % 6][:, g * TG:(g + 1) * TG], fl[:, k, 4 * h + g, :],
                                               m.ident[0:TG, 0:TG])
                last.then_inc(turned, 1)
            nc.tensor.transpose(m.bank[7][0:1, 0:TG], worst[:, 0:1], m.ident[0:TG, 0:TG]).then_inc(turned, 1)


def count_edges(nc, m, t):
    with ExitStack() as ctx:
        sb = lambda name, shape, dt: ctx.enter_context(nc.sbuf_tensor(name, shape, dt))
        widths = (W * SB, W * TB, P, P)
        hot_row = [sb(f"hot_row{h}", [P, 2, U, P], BF16) for h in range(2)]
        hot = [[sb(f"hot{k}{h}", [P, U, widths[k]], BF16) for h in range(2)] for k in range(2)]
        hot += [[hot_row[h][:, k] for h in range(2)] for k in range(2)]
        off = [t.far[:, h * U * P:(h + 1) * U * P].bitcast(F16).rearrange("p (k u n) -> p k u n", k=2, n=P)
               for h in range(2)]
        names = ("col_ready row_off row_abs row_ready mm_done bank_free src_added any_keys any_hot any_used "
                 "any_copied").split()
        (col_ready, row_off, row_abs, row_ready, mm_done, bank_free, src_added, any_keys, any_hot, any_used,
         any_copied) = \
            (ctx.enter_context(nc.semaphore(n)) for n in names)
        block = ctx.enter_context(nc.Block())
        NW = -(-N // W)
        SZ = 16

        @block.vector
        def _(v):
            v.sem_inc(any_copied, 1)
            v.memset(m.at[:, 0:SZ, :].bitcast(F32), 0.0).then_inc(bank_free, 2 * U - 2)
            v.memset(t.rt[:, :, :].bitcast(F32), 0.0).then_inc(bank_free, 1)
            v.wait_ge(bank_free, 2 * U)
            v.sem_inc(src_added, 1)

            def iota_by(n):
                return t.iota[:, 0:n].unsqueeze(1).to_broadcast([P, U, n])

            def keys_of(k, r, n):
                return t.key[k][:, ds(U * r, U)].unsqueeze(2).to_broadcast([P, U, n])

            def type_columns(r, h):
                n = widths[1]
                v.tensor_tensor(hot[1][h][:, :, :], iota_by(n), keys_of(1, r, n), op=ALU.is_equal)

            def source_columns(r, h, u):
                v.tensor_scalar(hot[0][h][:, u, :], t.iota[:, 0:widths[0]], t.key[0][:, ds(U * r + u, 1)], None,
                                op0=ALU.is_equal).then_inc(col_ready, 1)

            def add(r, h, u, base):
                v.wait_ge(mm_done, U * r + u + 1 + 2 * U)
                v.wait_ge(src_added, U * r + u + 1)
                wa = m.at[:, :, ds(base, W)]
                v.tensor_tensor(wa, wa, m.bank[U * h + u][:, 0:W * SB].rearrange("p (b d) -> p b d", d=W),
                                op=ALU.add).then_inc(src_added, 1)
                v.wait_ge(bank_free, U * r + 2 * U + u)
                wr = t.rt[:, :, ds(base, W)]
                v.tensor_tensor(wr, wr, m.bank[U * h + u][:, W * SB:W * (SB + TB)]
                                .rearrange("p (b d) -> p b d", d=W), op=ALU.add).then_inc(bank_free, 1)

            def bases(r, n):
                return nc.values_load_multi_w_load_instructions(
                    t.base[0:1, ds(U * r, n)], engines=(mybir.EngineType.DVE,), min_val=0, max_val=N - 1,
                    skip_runtime_bounds_check_because="minima of node numbers")[1]

            bad = v.value_load(t.bad[0:1, 0:1], min_val=0, max_val=1)
            with v.If(bad == 0):
                type_columns(0, 0)
                for u in range(U):
                    source_columns(0, 0, u)

                def two_rounds(i, final):
                    base = bases(2 * i, 2 * U)
                    for h in range(2):
                        more = not (final and h)
                        if more:
                            type_columns(2 * i + h + 1, 1 - h)
                        for u in range(U):
                            if more:
                                source_columns(2 * i + h + 1, 1 - h, u)
                            add(2 * i + h, h, u, base[U * h + u])

                with v.Fori(0, NU // 2 - 1) as i:
                    two_rounds(i, False)
                two_rounds(NU // 2 - 1, True)
            with v.Else():
                FAR = 10000.0
                v.sem_inc(any_used, 2)
                with v.Fori(0, NW) as w:
                    s = Steps(v, any_keys, 8 * w)
                    v.wait_ge(any_used, NU * w + 2)
                    s.done(v.tensor_scalar(t.key[0][:, :], t.key[4][:, :], float(W), FAR, op0=ALU.is_ge, op1=ALU.mult))
                    s.link(v.tensor_scalar(t.key[1][:, :], t.key[4][:, :], 0.0, FAR, op0=ALU.is_lt, op1=ALU.mult))
                    s.link(v.tensor_tensor(t.key[0][:, :], t.key[0][:, :], t.key[1][:, :], op=ALU.add))
                    s.link(v.tensor_tensor(t.key[0][:, :], t.key[0][:, :], t.key[4][:, :], op=ALU.add))
                    s.link(v.tensor_tensor(t.key[1][:, :], t.key[0][:, :], t.key[6][:, :], op=ALU.add))
                    s.link(v.tensor_tensor(t.key[0][:, :], t.key[0][:, :], t.key[5][:, :], op=ALU.add))
                    s.link(v.tensor_single_scalar(t.key[4][:, :], t.key[4][:, :], float(-W), op=ALU.add))
                    s.done_here()
                    with v.Fori(0, NU // 2) as i:
                        for h in range(2):
                            v.wait_ge(any_used, NU * w + 2 * i + h + 1)
                            for k in range(4):
                                n = widths[k]
                                last = v.tensor_tensor(hot[k][h][:, :, :], iota_by(n),
                                                       keys_of(k, 2 * i + h, n), op=ALU.is_equal)
                            last.then_inc(any_hot, 1)
                    v.wait_ge(any_used, NU * w + NU + 2)
                    v.tensor_copy(m.at[:, :, ds(w * W, W)],
                                  m.bank[0][:, 0:W * SB].rearrange("p (b d) -> p b d", d=W))
                    v.tensor_copy(t.rt[:, :, ds(w * W, W)],
                                  m.bank[1][:, 0:W * TB].rearrange("p (b d) -> p b d", d=W)).then_inc(any_copied, 1)

        @block.tensor
        def _(pe):
            bad = pe.value_load(t.bad[0:1, 0:1], min_val=0, max_val=1)
            with pe.If(bad == 0):
                pe.sem_inc(mm_done, 2 * U)
                with pe.Fori(0, NU // 2) as i:
                    for h in range(2):
                        r = 2 * i + h
                        pe.wait_ge(row_ready, r + 3)
                        for u in range(U):
                            pe.wait_ge(col_ready, U * r + u + 1)
                            pe.wait_ge(bank_free, U * r + u + 1)
                            nc.tensor.matmul(m.bank[U * h + u][:, 0:W * SB], hot[2][h][:, u, :],
                                             hot[0][h][:, u, :], start=True, stop=True)
                            nc.tensor.matmul(m.bank[U * h + u][:, W * SB:W * (SB + TB)], hot[3][h][:, u, :],
                                             hot[1][h][:, u, :], start=True, stop=True).then_inc(mm_done, 1)
            with pe.Else():
                with pe.Fori(0, NW) as w:
                    pe.wait_ge(any_copied, 1 + w)

                    def pair(i, first, final):
                        for h in range(2):
                            pe.wait_ge(any_hot, NU * w + 2 * i + h + 1)
                            for u in range(U):
                                start, stop = first and h + u == 0, final and h == 1 and u == U - 1
                                nc.tensor.matmul(m.bank[0][:, 0:W * SB], hot[2][h][:, u, :],
                                                 hot[0][h][:, u, :], start=start, stop=stop)
                                last = nc.tensor.matmul(m.bank[1][:, 0:W * TB], hot[3][h][:, u, :],
                                                        hot[1][h][:, u, :], start=start, stop=stop)
                            last.then_inc(any_used, 1)

                    pair(0, True, False)
                    with pe.Fori(1, NU // 2 - 1) as i:
                        pair(i, False, False)
                    pair(NU // 2 - 1, False, True)


        @block.gpsimd
        def _(pool):
            pool.memset(m.at[:, SZ:SB, :].bitcast(F32), 0.0).then_inc(bank_free, 1)
            bad = pool.value_load(t.bad[0:1, 0:1], min_val=0, max_val=1)
            with pool.If(bad == 0):
                with pool.Fori(0, NU // 2) as i:
                    for h in range(2):
                        r = 2 * i + h
                        pool.wait_ge(row_ready, r + 1)
                        for k in range(2):
                            pool.tensor_tensor(off[h][:, k], t.iota[:, 0:P].unsqueeze(1).to_broadcast([P, U, P]),
                                               t.key[2 + k][:, ds(U * r, U)].unsqueeze(2).to_broadcast([P, U, P]),
                                               op=ALU.subtract).then_inc(row_off, 1)

        @block.scalar
        def _(act):
            bad = act.value_load(t.bad[0:1, 0:1], min_val=0, max_val=1)
            with act.If(bad == 0):
                act.sem_inc(row_ready, 2)
                with act.Fori(0, NU // 2) as i:
                    for h in range(2):
                        r = 2 * i + h
                        act.wait_ge(row_off, 2 * r + 2)
                        nc.scalar.activation(off[h], off[h], ACT.Abs).then_inc(row_abs, 1)
                        act.wait_ge(row_abs, r + 1)
                        act.wait_ge(mm_done, U * r + U)
                        nc.scalar.activation(hot_row[h][:, :, :, :], off[h], ACT.Relu, scale=-1.0, bias=1.0)\
                          .then_inc(row_ready, 1)


def chunk_rows(a, c):
    return a[ds(c * CW, CW), :].rearrange("(j p) f -> p j f", p=RB)


def split3(v, s, parts, x):
    s.link(v.tensor_copy(parts[0], x))
    s.link(v.tensor_tensor(x, x, parts[0], op=ALU.subtract))
    s.link(v.tensor_copy(parts[1], x))
    s.link(v.tensor_tensor(parts[2], x, parts[1], op=ALU.subtract))


def column_sums(nc, m, t, rel, aggr_d, deg_d):
    with ExitStack() as ctx:
        sb = lambda name, shape, dt: ctx.enter_context(nc.sbuf_tensor(name, shape, dt))
        x = sb("rel_x", [P, TB, D], F32)
        parts = [sb(f"rel_part{k}", [P, TB, D], BF16) for k in range(3)]
        out = [sb(f"rel_out{h}", [P, CW], F32) for h in range(2)]
        ones = sb("deg_ones", [P, 1], BF16)
        row, tail = t.far[0:1, 0:CW], t.far[0:1, CW:CW + ND - NP]
        sem = lambda name: ctx.enter_context(nc.semaphore(name))
        loaded, step, split, summed = (sem(f"rel_{n}") for n in "loaded step split summed".split())
        copied, stored = sem("rel_copied"), [sem(f"rel_stored{h}") for h in range(2)]
        filled, counted, rowed, row_stored, turned, clipped = \
            (sem(f"deg_{n}") for n in "filled counted rowed row_stored turned clipped".split())
        block = ctx.enter_context(nc.Block())
        full = NREL // P

        @block.sync
        def _(sp):
            sp.wait_ge(filled, 2)
            sp.dma_start(x[:, 0:full, :], rel[0:full * P, :].rearrange("(b p) f -> p b f", p=P))\
              .then_inc(loaded, 16)
            sp.dma_start(x[0:NREL - full * P, full, :], rel[full * P:NREL, :]).then_inc(loaded, 16)
            deg = deg_d.rearrange("(a n) -> a n", a=1)
            sp.dma_start(deg[:, NP:ND], tail[:, :]).then_inc(turned, 16)
            sp.wait_ge(turned, 16)
            for c in range(NC):
                sp.wait_ge(rowed, c + 1)
                sp.dma_start(deg[:, c * CW:(c + 1) * CW], row[:, :]).then_inc(row_stored, 16)
            sp.wait_ge(row_stored, 16 * NC)
            with nc.allow_non_contiguous_dma(reason="one short vector"):
                sp.dma_start(m.in_norm[:, :], deg_d[0:NP].rearrange("(b p) -> p b", p=RB)).then_inc(turned, 16)
                sp.dma_start(m.loop_norm[:, :], deg_d[0:NP].rearrange("(b p) -> p b", p=RB)).then_inc(turned, 16)
                sp.dma_start(m.loop_norm_s[:, :], deg_d.rearrange("(b p) -> p b", p=P)).then_inc(turned, 16)
            for c in range(NC):
                sp.wait_ge(copied, c + 1)
                sp.dma_start(aggr_d[:, c * CW:(c + 1) * CW], out[c % 2][:, :]).then_inc(stored[c % 2], 16)
            for h in range(2):
                sp.wait_ge(stored[h], 16 * ((NC + 1 - h) // 2))
            sp.wait_ge(turned, 64)

        @block.tensor
        def _(pe):
            pe.wait_ge(filled, 1)
            for c in range(NC):
                if c >= 2:
                    pe.wait_ge(rowed, c - 1)
                for b in range(SB):
                    last = nc.tensor.matmul(m.bank[2 + c % 2][0:1, 0:CW], ones[:, 0:1],
                                            m.at[:, b, c * CW:(c + 1) * CW], start=b == 0, stop=b == SB - 1)
                last.then_inc(counted, 1)
            pe.wait_ge(split, 1)
            for c in range(NC):
                if c >= 2:
                    pe.wait_ge(copied, c - 1)
                for k in range(3):
                    for b in range(TB):
                        last = nc.tensor.matmul(m.bank[c % 2][:, 0:CW], parts[k][:, b, :],
                                                t.rt[:, b, c * CW:(c + 1) * CW],
                                                start=k + b == 0, stop=k == 2 and b == TB - 1)
                last.then_inc(summed, 1)

        @block.scalar
        def _(act):
            for c in range(NC):
                act.wait_ge(summed, c + 1)
                if c >= 2:
                    act.wait_ge(stored[c % 2], 16 * (c // 2))
                nc.scalar.activation(out[c % 2][:, :], m.bank[c % 2][:, 0:CW], ACT.Copy).then_inc(copied, 1)

        @block.gpsimd
        def _(pool):
            pool.wait_ge(clipped, 3)
            for a in (m.in_norm, m.loop_norm, m.loop_norm_s):
                pool.tensor_tensor(a[:, :], a[:, :], m.minus_half[0:a.shape[0], 0:a.shape[1]], op=ALU.pow)

        @block.vector
        def _(v):
            v.memset(ones[:, :], 1.0).then_inc(filled, 1)
            v.memset(tail[:, :], 0.0)
            v.memset(x[:, :, :], 0.0).then_inc(filled, 1)
            s = Steps(v, step)
            v.wait_ge(loaded, 32)
            split3(v, s, [q[:, :, :] for q in parts], x[:, :, :])
            s.wait()
            v.sem_inc(split, 1)
            for c in range(NC):
                v.wait_ge(counted, c + 1)
                if c:
                    v.wait_ge(row_stored, 16 * c)
                v.tensor_copy(row[0:1, :], m.bank[2 + c % 2][0:1, 0:CW]).then_inc(rowed, 1)
            v.wait_ge(turned, 64)
            v.tensor_single_scalar(m.in_norm[:, :], m.in_norm[:, :], 1.0, op=ALU.max).then_inc(clipped, 1)
            v.tensor_single_scalar(m.loop_norm[:, :], m.loop_norm[:, :], 1.0, op=ALU.add).then_inc(clipped, 1)
            v.tensor_single_scalar(m.loop_norm_s[:, :], m.loop_norm_s[:, :], 1.0, op=ALU.add).then_inc(clipped, 1)


def layer_norm(v, s, m, y, o, st, mv, sd, normed, rooted, c):
    for j in range(RPC):
        s.done(v.bn_stats(st[:, j, :], y[:, j, :]))
    s.wait()
    s.done_here()
    for j in range(RPC):
        last = v.bn_aggr(mv[:, j, :], st[:, j, :])
    last.then_inc(normed, 1)
    v.wait_ge(rooted, 2 * c + 2)
    for j in range(RPC):
        last = v.tensor_scalar(o[:, j, :], y[:, j, :], mv[:, j, 0:1], sd[:, j:j + 1],
                               op0=ALU.subtract, op1=ALU.mult)
    return last


def inverse_roots(pool, m, mv, sd, normed, rooted, c):
    pool.wait_ge(normed, c + 1)
    pool.tensor_tensor(sd[:, :], mv[:, :, 1], m.eps[0:RB, :], op=ALU.add).then_inc(rooted, 1)
    pool.wait_ge(rooted, 2 * c + 1)
    pool.tensor_tensor(sd[:, :], sd[:, :], m.minus_half[0:RB, 0:RPC], op=ALU.pow).then_inc(rooted, 1)


def store_rows(sp, out, o, c, stored):
    if out.shape[0] >= NP or not isinstance(c, int) or c < NC - 1:
        sp.dma_start(chunk_rows(out, c), o[:, :, :]).then_inc(stored, 16)
        return 16
    full = (N - c * CW) // RB
    at = c * CW + full * RB
    sp.dma_start(out[c * CW:at, :].rearrange("(j p) f -> p j f", p=RB), o[:, 0:full, :]).then_inc(stored, 16)
    sp.dma_start(out[at:N, :], o[0:N - at, full, :]).then_inc(stored, 16)
    return 32


SG = 5
NSG = SB // SG


def graph_conv(nc, m, tag, x, scale, weight, post, out, residual=None, bias=None, loop_weight=None, aggr_d=None,
               relu=False, norm=True, loops=0, out_degree=False):
    with ExitStack() as ctx:
        sb = lambda name, shape, dt: ctx.enter_context(nc.sbuf_tensor(f"{tag}_{name}", shape, dt))
        xs = [sb(f"xs{i}", [P, SG, D], F32) for i in range(2)]
        parts = [sb(f"part{k}", [P, SB, D], BF16) for k in range(3)]
        if out_degree:
            junk = sb("junk", [P, NP], BF16)
        w = sb("w", [P, D], F32)
        wl = sb("wl", [P, D], F32)
        bb = sb("bias", [RB, D], F32)
        aggt = sb("aggt", [P, CW], F32)
        aggr = sb("aggr", [P, CW], F32)
        xr = sb("xr", [RB, RPC, D], F32)
        xt = sb("xt", [P, CW], F32)
        y = sb("y", [RB, RPC, D], F32)
        o = sb("o", [RB, RPC, D], F32)
        st = sb("st", [RB, RPC, 6], F32)
        mv = sb("mv", [RB, RPC, 2], F32)
        sd = sb("sd", [RB, RPC], F32)
        sem = lambda name, used=True: ctx.enter_context(nc.semaphore(f"{tag}_{name}")) if used else None
        w_loaded, rows_loaded, rows_used, summed, aggt_ready, mixed, step, finished, stored, out_free = \
            (sem(name) for name in "w_loaded rows_loaded rows_used summed aggt_ready mixed step finished stored "
             "out_free".split())
        turned, xt_ready = (sem(name, loop_weight is not None) for name in ("turned", "xt_ready"))
        normed, rooted = (sem(name, norm) for name in ("normed", "rooted"))
        split = sem("split")
        xs_loaded = [sem(f"xs_loaded{i}") for i in range(2)]
        looped, counted = sem("looped", loops), sem("counted", out_degree)
        block = ctx.enter_context(nc.Block())
        nw = 1 + (bias is not None) + (loop_weight is not None)
        nl = (residual is not None) + (aggr_d is not None)
        bank_agg, bank_t, bank_rows, bank_loop = m.bank[0:4]

        @block.sync
        def _(sp):
            sp.sem_inc(out_free, 1)
            for g in range(NSG):
                if g >= 2:
                    sp.wait_ge(split, g - 1)
                sp.dma_start(xs[g % 2][:, :, :], x[g * SG * P:(g + 1) * SG * P, :].rearrange("(b p) f -> p b f", p=P))\
                  .then_inc(xs_loaded[g % 2], 16)
            sp.dma_start(w[:, :], weight).then_inc(w_loaded, 16)
            if loop_weight is not None:
                sp.dma_start(wl[:, :], loop_weight).then_inc(w_loaded, 16)
            if bias is not None:
                sp.dma_start(bb[:, :], bias.unsqueeze(0).to_broadcast([RB, D])).then_inc(w_loaded, 16)

            def body(c):
                if nl:
                    hold(sp, rows_used, 1 + c, m.passed)
                if residual is not None:
                    sp.dma_start(xr[:, :, :], chunk_rows(residual, c)).then_inc(rows_loaded, 16)
                if aggr_d is not None:
                    sp.dma_start(aggr[:, :], aggr_d[:, ds(c * CW, CW)]).then_inc(rows_loaded, 16)
                hold(sp, finished, 1 + c + 1, m.passed)
                n = store_rows(sp, out, o, c, stored)
                sp.wait_ge(stored, 16 * c + n)
                sp.sem_inc(out_free, 1)

            with sp.Fori(0, NC - 1) as c:
                body(c)
            body(NC - 1)

        @block.tensor
        def _(pe):
            pe.sem_inc(mixed, 1)
            if loops:
                pe.wait_ge(looped, SB)

            def chunk(c, first):
                for b in range(SB):
                    if first and b % SG == 0:
                        pe.wait_ge(split, b // SG + 1)
                    for k in range(3):
                        last = nc.tensor.matmul(bank_agg[:, 0:CW], parts[k][:, b, :], m.at[:, b, ds(c * CW, CW)],
                                                start=k + b == 0, stop=k == 2 and b == SB - 1)
                last.then_inc(summed, 1)
                if first:
                    pe.wait_ge(w_loaded, 16 * nw)
                if loop_weight is not None:
                    pe.wait_ge(rows_loaded, 16 * nl * (c + 1))
                    for j in range(RPC):
                        last = nc.tensor.transpose(bank_t[:, j * RB:(j + 1) * RB], xr[:, j, :], m.ident[0:RB, 0:RB])
                    last.then_inc(turned, 1)
                    pe.wait_ge(xt_ready, c + 1)
                    pe.wait_ge(finished, 1 + c)
                    for j in range(RPC):
                        nc.tensor.matmul(bank_loop[0:RB, j * D:(j + 1) * D], xt[:, j * RB:(j + 1) * RB], wl[:, :],
                                         start=True, stop=True)
                pe.wait_ge(aggt_ready, c + 1)
                pe.wait_ge(finished, 1 + c)
                for j in range(RPC):
                    last = nc.tensor.matmul(bank_rows[0:RB, j * D:(j + 1) * D], aggt[:, j * RB:(j + 1) * RB],
                                            w[:, :], start=True, stop=True)
                last.then_inc(mixed, 1)

            chunk(0, True)
            with pe.Fori(1, NC) as c:
                chunk(c, False)

        @block.scalar
        def _(act):
            def count(b, before):
                act.wait_ge(counted, before + 1)
                nc.scalar.activation(junk[:, :], m.at[:, ds(b, 1), 0:NP].rearrange("p a n -> p (a n)"), ACT.Copy,
                                     accum_out=m.out_norm[:, ds(b, 1)]).then_inc(counted, 1)

            def body(c):
                if aggr_d is None:
                    act.wait_ge(summed, c + 1)
                    act.wait_ge(mixed, 1 + c)
                    nc.scalar.activation(aggt[:, :], bank_agg[:, 0:CW], ACT.Copy).then_inc(aggt_ready, 1)
                if loop_weight is not None:
                    act.wait_ge(turned, c + 1)
                    act.wait_ge(mixed, 1 + c)
                    nc.scalar.activation(xt[:, :], bank_t[:, 0:CW], ACT.Copy).then_inc(xt_ready, 1)
                if out_degree and not isinstance(c, int):
                    for i in range(4):
                        count(4 * c + i, 4 * c + i + 1)

            if out_degree:
                act.sem_inc(counted, 1)
                assert SB == 4 * (NC - 1) + 1
                count(SB - 1, 0)
            with act.Fori(0, NC - 1) as c:
                body(c)
            body(NC - 1)

        @block.gpsimd
        def _(pool):
            if norm:
                with pool.Fori(0, NC) as c:
                    inverse_roots(pool, m, mv, sd, normed, rooted, c)

        @block.vector
        def _(v):
            v.sem_inc(finished, 1)
            v.sem_inc(rows_used, 1)
            flat = [RB, RPC, D]
            if loops:
                for b in range(SB):
                    a = m.at[:, b, b * P:(b + 1) * P]
                    v.tensor_tensor(a, a, m.identb[:, :], op=ALU.add if loops > 0 else ALU.subtract)\
                     .then_inc(looped, 1)
            s = Steps(v, step)
            for g in range(NSG):
                xg = xs[g % 2][:, :, :]
                v.wait_ge(xs_loaded[g % 2], 16 * (g // 2 + 1))
                if scale is not None:
                    s.link(v.tensor_tensor(xg, xg, scale[:, g * SG:(g + 1) * SG].unsqueeze(2)
                                           .to_broadcast([P, SG, D]), op=ALU.mult))
                split3(v, s, [q[:, g * SG:(g + 1) * SG, :] for q in parts], xg)
                v.sem_inc(split, 1)
            n0 = s.n

            def body(c, s):
                if aggr_d is not None:
                    v.wait_ge(summed, c + 1)
                    v.wait_ge(rows_loaded, 16 * nl * (c + 1))
                    v.wait_ge(mixed, 1 + c)
                    v.tensor_tensor(aggt[:, :], aggr[:, :], bank_agg[:, 0:CW], op=ALU.add).then_inc(aggt_ready, 1)
                v.wait_ge(mixed, 1 + c + 1)
                rows = bank_rows[0:RB, :].rearrange("p (j f) -> p j f", f=D)
                s.link(v.tensor_tensor(y[:, :, :], rows, post[:, ds(c * RPC, RPC)].unsqueeze(2).to_broadcast(flat),
                                       op=ALU.mult))
                if bias is not None:
                    s.link(v.tensor_tensor(y[:, :, :], y[:, :, :], bb[:, :].unsqueeze(1).to_broadcast(flat),
                                           op=ALU.add))
                if loop_weight is not None:
                    s.link(v.tensor_tensor(y[:, :, :], y[:, :, :],
                                           bank_loop[0:RB, :].rearrange("p (j f) -> p j f", f=D), op=ALU.add))
                if relu:
                    s.link(v.tensor_single_scalar(y[:, :, :], y[:, :, :], 0.0, op=ALU.max))
                if residual is not None:
                    v.wait_ge(rows_loaded, 16 * nl * (c + 1))
                    s.link(v.tensor_tensor(y[:, :, :], y[:, :, :], xr[:, :, :], op=ALU.add))
                if nl:
                    v.sem_inc(rows_used, 1)
                v.wait_ge(out_free, c + 1)
                if norm:
                    layer_norm(v, s, m, y, o, st, mv, sd, normed, rooted, c).then_inc(finished, 1)
                else:
                    v.tensor_copy(o[:, :, :], y[:, :, :]).then_inc(finished, 1)
                return s.n

            v.wait_ge(w_loaded, 16 * nw)
            n = 1 + (bias is not None) + (loop_weight is not None) + relu + (residual is not None) + \
                (RPC + 1 if norm else 0)
            with v.Fori(0, NC) as c:
                s = Steps(v, step, n * c + n0)
                assert body(c, s) == n


HEADS = 8
HD = D // HEADS
NX = 6
KS = NX * HD
KM = KS + 3
Q_PIECES = (0, 1, 0, 1, 2, 0)
K_PIECES = (0, 0, 1, 1, 0, 2)
VW = 32
DG = 5
NDG = SB // DG
NS = 3
PARTS = ((0, 3), (3, 5), (5, 7))
NE = 5


def turn_and_project(nc, m, ad, x1, wq, bq, wk, bk, wv, qs, ks, vd):
    with ExitStack() as ctx:
        sb = lambda name, shape, dt: ctx.enter_context(nc.sbuf_tensor("prj_" + name, shape, dt))
        w = sb("w", [P, 3, D], F32)
        b2 = sb("b2", [P, 2], F32)
        xr = sb("xr", [RB, RPC, D], F32)
        xt = sb("xt", [P, CW], F32)
        qk = [sb(f"qk{k}", [P, CW], F32) for k in range(2)]
        pieces = [sb(f"pieces{k}", [P, 3, CW], BF16) for k in range(2)]
        vals = sb("vals", [RB, RPC, HEADS, VW], F32)
        onesb = sb("onesb", [P, (KM - KS) * HEADS * ND // P], BF16)
        zeros = sb("zeros", [P, HEADS, ND - NP], BF16)
        zerov = sb("zerov", [ND - NP, HEADS * VW], F32)
        TPC = 4
        rows = [sb(f"rows{i}", [P, ND], BF16) for i in range(TPC)]
        sem = lambda name: ctx.enter_context(nc.semaphore("prj_" + name))
        (w_loaded, rows_loaded, x_turned, xt_ready, made, relued, step, split, valued, stored, filled,
         padded, out_free, turned, looped, clipped) = \
            (sem(n) for n in ("w_loaded rows_loaded x_turned xt_ready made relued step split valued stored "
                              "filled padded out_free turned looped clipped").split())
        evac = [sem(f"evac{h}") for h in range(2)]
        turned_stored = [sem(f"turned_stored{h}") for h in range(2)]
        rows_free = [sem(f"rows_free{h}") for h in range(2)]
        block = ctx.enter_context(nc.Block())
        per = 2 * NX + 1
        groups = ((0, 8), (8, 16), (16, 24), (24, 25))
        bank_x, bank_qk, bank_v = m.bank[0], m.bank[1:3], m.bank[3]

        assert SB == TPC * (NC - 1) + 1

        def over_chunks(eng, body):
            with eng.Fori(0, NC - 1) as c:
                body(c)
            body(NC - 1)

        @block.sync
        def _(sp):
            sp.sem_inc(out_free, 1)
            sp.sem_inc(rows_free[0], 1)
            sp.sem_inc(rows_free[1], 1)
            sp.dma_start(xr[:, :, :], chunk_rows(x1, 0)).then_inc(rows_loaded, 16)
            for k, a in enumerate((wq, wk, wv)):
                sp.dma_start(w[:, k, :], a).then_inc(w_loaded, 16)
            for k, a in enumerate((bq, bk)):
                sp.dma_start(b2[:, k:k + 1], a.rearrange("(p a) -> p a", a=1)).then_inc(w_loaded, 16)
            sp.wait_ge(filled, 1)
            sp.dma_start(ks[KS:KM, :, :].rearrange("r h n -> (r h n)").rearrange("(p f) -> p f", p=P), onesb[:, :])\
              .then_inc(padded, 16)
            for a in (qs, ks):
                sp.dma_start(a[0:KS, :, NP:ND], zeros[0:KS, :, :]).then_inc(padded, 16)
            sp.dma_start(vd[NP:ND, :], zerov[:, :]).then_inc(padded, 16)

            def store_turned(c, t):
                i = TPC * c + t
                for h in range(2):
                    hold(sp, evac[h], 1 + 2 * (i + 1), m.passed)
                sp.dma_start(ad[ds(i * P, P), :], rows[t][:, 0:NP]).then_inc(turned_stored[t // 2], 16)

            def body(c):
                if not isinstance(c, int):
                    hold(sp, x_turned, c + 1, m.passed)
                    sp.dma_start(xr[:, :, :], chunk_rows(x1, c + 1)).then_inc(rows_loaded, 16)
                store_turned(c, 0)
                hold(sp, split, 1 + 2 * (c + 1), m.passed)
                for k, (pcs, a) in enumerate(((Q_PIECES, qs), (K_PIECES, ks))):
                    for g in range(NX):
                        sp.dma_start(a[g * HD:(g + 1) * HD, :, ds(c * CW, CW)].rearrange("r h n -> h r n"),
                                     pieces[k][:, pcs[g], :]).then_inc(stored, 16)
                if not isinstance(c, int):
                    store_turned(c, 1)
                hold(sp, valued, 1 + c + 1, m.passed)
                sp.dma_start(vd[ds(c * CW, CW), :].rearrange("(j p) f -> p j f", p=RB),
                             vals[:, :, :, :].rearrange("p j h w -> p j (h w)")).then_inc(stored, 16)
                if not isinstance(c, int):
                    store_turned(c, 2)
                    hold(sp, turned_stored[0], 32 * (c + 1), m.passed)
                    sp.sem_inc(rows_free[0], 1)
                    store_turned(c, 3)
                hold(sp, stored, 16 * per * (c + 1), m.passed)
                sp.sem_inc(out_free, 1)
                if not isinstance(c, int):
                    hold(sp, turned_stored[1], 32 * (c + 1), m.passed)
                    sp.sem_inc(rows_free[1], 1)

            over_chunks(sp, body)
            sp.wait_ge(turned_stored[0], 32 * (NC - 1) + 16)
            sp.wait_ge(padded, 16 * 4)

        @block.tensor
        def _(pe):
            pe.sem_inc(made, 1)
            pe.wait_ge(looped, SB)

            def turn(c, t):
                i = TPC * c + t
                for g, (lo, hi) in enumerate(groups):
                    pe.wait_ge(evac[g % 2], 2 * i + 1 + g // 2)
                    for b in range(lo, hi):
                        bank = m.bank[4 + 2 * (g % 2) + (b - lo) // 4]
                        last = nc.tensor.matmul(bank[:, (b - lo) % 4 * P:((b - lo) % 4 + 1) * P],
                                                m.at[:, b, ds(i * P, P)], m.identb[:, :], start=True, stop=True)
                    last.then_inc(turned, 1)

            def body(c):
                pe.wait_ge(rows_loaded, 16 * (c + 1))
                pe.wait_ge(xt_ready, c + 1)
                for j in range(RPC):
                    last = nc.tensor.transpose(bank_x[:, j * RB:(j + 1) * RB], xr[:, j, :], m.ident[0:RB, 0:RB])
                last.then_inc(x_turned, 1)
                turn(c, 0)
                pe.wait_ge(xt_ready, c + 2)
                for k in range(2):
                    pe.wait_ge(relued, 1 + 2 * c)
                    nc.tensor.matmul(bank_qk[k][:, 0:CW], w[:, k, :], xt[:, :], start=True, stop=True)\
                      .then_inc(made, 1)
                if not isinstance(c, int):
                    turn(c, 1)
                pe.wait_ge(valued, 1 + c)
                for j in range(RPC):
                    last = nc.tensor.matmul(bank_v[0:RB, j * D:(j + 1) * D], xt[:, j * RB:(j + 1) * RB],
                                            w[:, 2, :], start=True, stop=True)
                last.then_inc(made, 1)
                if not isinstance(c, int):
                    turn(c, 2)
                    turn(c, 3)

            pe.wait_ge(w_loaded, 80)
            over_chunks(pe, body)

        def copy_groups(wait, copy, engine, c, t, done):
            i = TPC * c + t
            wait(rows_free[t // 2], c + 1)
            for g in (engine, engine + 2):
                lo, hi = groups[g]
                first = 4 + 2 * (g % 2)
                wait(turned, 4 * i + g + 1)
                if hi - lo == 8:
                    copy(rows[t][:, lo * P:hi * P].rearrange("p (k n) -> p k n", n=512),
                         m.ps[:, first:first + 2, :]).then_inc(done, 1)
                else:
                    copy(rows[t][:, lo * P:hi * P], m.ps[:, first, 0:(hi - lo) * P]).then_inc(done, 1)

        @block.scalar
        def _(act):
            act.sem_inc(relued, 1)
            act.sem_inc(evac[0], 1)
            act.sem_inc(xt_ready, 1)
            act.wait_ge(w_loaded, 80)

            def copy_out(c, t):
                copy_groups(act.wait_ge, lambda out, in_: nc.scalar.activation(out, in_, ACT.Copy), 0, c, t, evac[0])

            def body(c):
                act.wait_ge(x_turned, c + 1)
                act.wait_ge(made, 1 + 3 * c)
                nc.scalar.activation(xt[:, :], bank_x[:, 0:CW], ACT.Copy).then_inc(xt_ready, 1)
                copy_out(c, 0)
                act.wait_ge(split, 1 + 2 * c)
                for k in range(2):
                    act.wait_ge(made, 1 + 3 * c + k + 1)
                    nc.scalar.activation(qk[k][:, :], bank_qk[k][:, 0:CW], ACT.Relu, bias=b2[:, k:k + 1])\
                      .then_inc(relued, 1)
                if not isinstance(c, int):
                    for t in range(1, TPC):
                        copy_out(c, t)

            over_chunks(act, body)

        @block.gpsimd
        def _(pool):
            pool.wait_ge(clipped, 1)
            pool.tensor_tensor(m.out_norm[:, :], m.out_norm[:, :], m.minus_half[:, 0:SB], op=ALU.pow)

        @block.vector
        def _(v):
            v.sem_inc(valued, 1)
            v.sem_inc(split, 1)
            v.sem_inc(evac[1], 1)
            for b in range(SB):
                a = m.at[:, b, b * P:(b + 1) * P]
                v.tensor_tensor(a, a, m.identb[:, :], op=ALU.add).then_inc(looped, 1)
            v.tensor_single_scalar(m.out_norm[:, :], m.out_norm[:, :], 1.0, op=ALU.max).then_inc(clipped, 1)
            v.memset(zeros[:, :, :], 0.0)
            v.memset(zerov[:, :], 0.0)
            v.memset(onesb[:, :], 1.0).then_inc(filled, 1)
            v.memset(vals[:, :, :, HD + 1:VW], 0.0)
            v.memset(vals[:, :, :, HD:HD + 1], 1.0).then_inc(filled, 1)
            v.wait_ge(filled, 2)

            def copy_out(c, t):
                copy_groups(v.wait_ge, v.tensor_copy, 1, c, t, evac[1])

            def body(c):
                s = Steps(v, step, 6 * c)
                copy_out(c, 0)
                v.wait_ge(out_free, c + 1)
                for k in range(2):
                    v.wait_ge(relued, 1 + 2 * c + k + 1)
                    s.link(v.tensor_copy(pieces[k][:, 0, :], qk[k][:, :]))
                    s.link(v.tensor_tensor(qk[k][:, :], qk[k][:, :], pieces[k][:, 0, :], op=ALU.subtract))
                    s.link(v.tensor_copy(pieces[k][:, 1, :], qk[k][:, :]))
                    v.tensor_tensor(pieces[k][:, 2, :], qk[k][:, :], pieces[k][:, 1, :], op=ALU.subtract)\
                     .then_inc(split, 1)
                if not isinstance(c, int):
                    copy_out(c, 1)
                v.wait_ge(made, 1 + 3 * c + 3)
                v.tensor_copy(vals[:, :, :, 0:HD],
                              bank_v[0:RB, :].rearrange("p (j h f) -> p j h f", j=RPC, h=HEADS))\
                 .then_inc(valued, 1)
                if not isinstance(c, int):
                    copy_out(c, 2)
                    copy_out(c, 3)

            over_chunks(v, body)


def score_maxima(nc, m, qs, ks):
    with ExitStack() as ctx:
        sb = lambda name, shape, dt: ctx.enter_context(nc.sbuf_tensor("max_" + name, shape, dt))
        HH = HEADS // 2
        mall = sb("mall", [P, SB, HEADS], F32)
        with ExitStack() as c2:
            sb2 = lambda name, shape, dt: c2.enter_context(nc.sbuf_tensor("max_" + name, shape, dt))
            kk = sb2("keys", [KS, HH, NP], BF16)
            q = [sb2(f"q{i}", [KS, HH, P], BF16) for i in range(2)]
            mask = [sb2(f"mask{i}", [P, NC, CW], BF16) for i in range(2)]
            mx = [sb2(f"mx{i}", [P, HH, len(PARTS)], F32) for i in range(2)]
            names = "keys_loaded q_used scored maxed masked stepped".split()
            sems = {n: c2.enter_context(nc.semaphore("max_" + n)) for n in names}
            keys_loaded, q_used, scored, maxed, masked, stepped = (sems[n] for n in names)
            block = c2.enter_context(nc.Block())
            q_loaded = [c2.enter_context(nc.semaphore(f"max_q_loaded{i}")) for i in range(2)]
            NPT = len(PARTS)
            per = NPT * HH

            @block.sync
            def _(sp):
                for hh in range(2):
                    at = hh * SB
                    if hh:
                        sp.wait_ge(q_used, SB + 1)
                    sp.dma_start(kk[:, :, :], ks[0:KS, hh * HH:(hh + 1) * HH, 0:NP]).then_inc(keys_loaded, 16)

                    def load(b, slot, used):
                        if used is not None:
                            hold(sp, q_used, used + 1, m.passed)
                        sp.dma_start(q[slot][:, :, :], qs[0:KS, hh * HH:(hh + 1) * HH, ds(b * P, P)])\
                          .then_inc(q_loaded[slot], 16)

                    load(0, at % 2, None if hh == 0 else at - 1)
                    with sp.Fori(0, SB // 2) as i:
                        load(2 * i + 1, (at + 1) % 2, at + 2 * i)
                        load(2 * i + 2, at % 2, at + 2 * i + 1)

            @block.tensor
            def _(pe):
                for hh in range(2):
                    at = hh * SB

                    def scores(b, slot, uses):
                        r = at + b
                        pe.wait_ge(q_loaded[slot], 16 * uses)
                        for h in range(HH):
                            for part, (lo, hi) in enumerate(PARTS):
                                pe.wait_ge(maxed, per * r + NPT * h + part + 1)
                                for k in range(lo, hi):
                                    last = nc.tensor.matmul(m.bank[k][:, 0:CW], q[slot][:, h, :],
                                                            kk[:, h, k * CW:(k + 1) * CW], start=True, stop=True)
                                last.then_inc(scored, 1)

                    pe.wait_ge(keys_loaded, 16 * (hh + 1))
                    scores(0, at % 2, at // 2 + 1)
                    with pe.Fori(0, SB // 2) as i:
                        scores(2 * i + 1, (at + 1) % 2, (at + 1) // 2 + 1 + i)
                        scores(2 * i + 2, at % 2, (at + 2) // 2 + 1 + i)

            @block.scalar
            def _(act):
                def make(b, r):
                    if not (isinstance(r, int) and r < 2):
                        act.wait_ge(q_used, r)
                    return m.at[:, ds(b, 1), 0:NP].rearrange("p a (k n) -> p (a k) n", n=CW)

                for hh in range(2):
                    at = hh * SB
                    nc.scalar.activation(mask[at % 2][:, :, :], make(0, at), ACT.Sign).then_inc(masked, 1)
                    with act.Fori(0, SB // 2) as i:
                        for z in (1, 2):
                            nc.scalar.activation(mask[(at + z) % 2][:, :, :], make(2 * i + z, at + 2 * i + z),
                                                 ACT.Sign).then_inc(masked, 1)

            @block.vector
            def _(v):
                v.sem_inc(q_used, 1)
                v.memset(mx[0][:, :, :], 0.0).then_inc(maxed, NPT)
                v.wait_ge(maxed, NPT)

                def head(r, h, slot):
                    for part, (lo, hi) in enumerate(PARTS):
                        hold(v, scored, per * r + NPT * h + part + 1, m.passed)
                        v.tensor_tensor_reduce(
                            out=m.ps[:, lo:hi, 0:CW], in0=m.ps[:, lo:hi, 0:CW], in1=mask[slot][:, lo:hi, :],
                            scale=1.0, scalar=0.0, op0=ALU.mult, op1=ALU.max,
                            accum_out=mx[slot][:, h, part:part + 1]).then_inc(maxed, 1)

                def finish(b, r, hh, slot):
                    v.wait_ge(maxed, per * (r + 1) + NPT)
                    v.tensor_reduce(mall[:, ds(b, 1), hh * HH:(hh + 1) * HH].rearrange("p a h -> p (a h)"),
                                    mx[slot][:, :, :], axis=AX.X, op=ALU.max).then_inc(q_used, 1)

                for hh in range(2):
                    at = hh * SB

                    def body(b, r, slot, before):
                        hold(v, masked, r + 1, m.passed)
                        head(r, 0, slot)
                        if before is not None:
                            finish(before, r - 1, hh, 1 - slot)
                        for h in range(1, HH):
                            head(r, h, slot)

                    body(0, at, at % 2, None)
                    with v.Fori(0, SB // 2) as i:
                        body(2 * i + 1, at + 2 * i + 1, (at + 1) % 2, 2 * i)
                        body(2 * i + 2, at + 2 * i + 2, at % 2, 2 * i + 1)
                    finish(SB - 1, at + SB - 1, hh, at % 2)
        with ExitStack() as c2:
            sb2 = lambda name, shape, dt: c2.enter_context(nc.sbuf_tensor("neg_" + name, shape, dt))
            pcs = sb2("pieces", [P, SB, 3, HEADS], BF16)
            rows = sb2("rows", [3 * HEADS, ND], BF16)
            step = c2.enter_context(nc.semaphore("neg_step"))
            split = c2.enter_context(nc.semaphore("neg_split"))
            turned = c2.enter_context(nc.semaphore("neg_turned"))
            rowed = c2.enter_context(nc.semaphore("neg_rowed"))
            stored = c2.enter_context(nc.semaphore("neg_stored"))
            block = c2.enter_context(nc.Block())

            @block.vector
            def _(v):
                s = Steps(v, step)
                s.link(v.tensor_single_scalar(mall[:, :, :], mall[:, :, :], -1.0, op=ALU.mult))
                split3(v, s, [pcs[:, :, k, :] for k in range(3)], mall[:, :, :])
                v.memset(rows[0:1, 0:1], 0.0).then_inc(split, 1)
                v.wait_ge(split, 1)
                v.wait_ge(turned, 1)
                v.tensor_copy(rows[:, 0:6 * 512].rearrange("p (k n) -> p k n", n=512), m.ps[0:3 * HEADS, 0:6, :])
                v.tensor_copy(rows[:, 6 * 512:ND], m.ps[0:3 * HEADS, 6, 0:P]).then_inc(rowed, 1)

            @block.tensor
            def _(pe):
                pe.wait_ge(split, 1)
                for b in range(SB):
                    last = nc.tensor.matmul(m.bank[b // 4][0:3 * HEADS, (b % 4) * P:(b % 4 + 1) * P],
                                            pcs[:, b, :, :], m.identb[:, :], start=True, stop=True)
                last.then_inc(turned, 1)

            @block.sync
            def _(sp):
                sp.wait_ge(rowed, 1)
                for k in range(3):
                    sp.dma_start(qs[KS + k, :, :], rows[k * HEADS:(k + 1) * HEADS, :]).then_inc(stored, 16)
                sp.wait_ge(stored, 48)


def attend(nc, m, x1, qs, ks, vd, ad, bias, out):
    with ExitStack() as ctx:
        sb = lambda name, shape, dt: ctx.enter_context(nc.sbuf_tensor("att_" + name, shape, dt))
        q = sb("q", [KM, HEADS, CW], BF16)
        k = [sb(f"k{i}", [KM, HEADS, P], BF16) for i in range(DG)]
        vv = [sb(f"v{i}", [P, HEADS, VW], F32) for i in range(DG)]
        a = [sb(f"a{i}", [P, CW], BF16) for i in range(DG)]
        e = [sb(f"e{i}", [P, 2, CW], F32) for i in range(NE)]
        acc = e[0]
        bb = sb("bias", [RB, D], F32)
        xr = sb("xr", [RB, RPC, D], F32)
        y = sb("y", [RB, RPC, D], F32)
        o = y
        rden = sb("rden", [RB, 2, RPC, HEADS // 2], F32)
        st = sb("st", [RB, RPC, 6], F32)
        mv = sb("mv", [RB, RPC, 2], F32)
        sd = sb("sd", [RB, RPC], F32)
        names = ("b_loaded q_loaded x_loaded scored exped weighed summed acc_ready turned step "
                 "normed rooted finished stored out_free turned_used").split()
        sems = {n: ctx.enter_context(nc.semaphore("att_" + n)) for n in names}
        (b_loaded, q_loaded, x_loaded, scored, exped, weighed, summed, acc_ready, turned, step,
         normed, rooted, finished, stored, out_free, turned_used) = (sems[n] for n in names)
        slot_loaded = [ctx.enter_context(nc.semaphore(f"att_slot{i}")) for i in range(DG)]
        block = ctx.enter_context(nc.Block())
        HP = HEADS // 2
        PB = SB * HP
        E0, S0 = 2, DG * HP // 2

        @block.sync
        def _(sp):
            with sp.Fori(0, NC) as c:
                hold(sp, turned, 1 + c, m.passed)
                sp.dma_start(q[:, :, :], qs[:, :, ds(c * CW, CW)]).then_inc(q_loaded, 16)
                with sp.Fori(0, NDG) as g:
                    for i in range(DG):
                        hold(sp, summed, HP // 2 * ((c * NDG + g) * DG + i + 1), m.passed)
                        row = (g * DG + i) * P
                        sp.dma_start(k[i][:, :, :], ks[:, :, ds(row, P)]).then_inc(slot_loaded[i], 16)
                        sp.dma_start(a[i][:, :], ad[ds(row, P), ds(c * CW, CW)]).then_inc(slot_loaded[i], 16)
                        sp.dma_start(vv[i][:, :, :], vd[ds(row, P), :].rearrange("p (h w) -> p h w", w=VW))\
                          .then_inc(slot_loaded[i], 16)

        @block.gpsimd
        def _(pool):
            pool.sem_inc(out_free, 1)
            pool.dma_start(bb[:, :], bias.unsqueeze(0).to_broadcast([RB, D])).then_inc(b_loaded, 16)
            with pool.Fori(0, NC) as c:
                hold(pool, finished, 1 + c, m.passed)
                pool.dma_start(xr[:, :, :], chunk_rows(x1, c)).then_inc(x_loaded, 16)
                inverse_roots(pool, m, mv, sd, normed, rooted, c)
                hold(pool, finished, 1 + c + 1, m.passed)
                pool.dma_start(chunk_rows(out, c), o[:, :, :]).then_inc(stored, 16)
                hold(pool, stored, 16 * (c + 1), m.passed)
                pool.sem_inc(out_free, 1)

        @block.tensor
        def _(pe):
            pe.sem_inc(turned, 1)
            with pe.Fori(0, NC) as c:
                pe.wait_ge(q_loaded, 16 * (c + 1))

                def scores(n, i, h):
                    j = i * HP + h
                    pe.wait_ge(exped, n - (1 if j < 2 else 2) + E0)
                    for z in range(2):
                        last = nc.tensor.matmul(m.bank[2 * (j % NS) + z][:, 0:CW], k[i][:, 2 * h + z, :],
                                                q[:, 2 * h + z, :], start=True, stop=True)
                    last.then_inc(scored, 1)

                def sums(n, j, start, stop):
                    pe.wait_ge(weighed, n + 1)
                    for z in range(4):
                        head = 2 * (j % HP - 1) + z
                        last = nc.tensor.matmul(m.bank[2 * NS + head // 4][VW * z:VW * (z + 1), 0:CW],
                                                vv[j // HP][:, head, :], e[(j - 1 + z // 2) % NE][:, z % 2, :],
                                                start=start, stop=stop)
                    last.then_inc(summed, 1)

                def group(g, first):
                    n0 = (c * SB + g * DG) * HP
                    for i in range(DG):
                        pe.wait_ge(slot_loaded[i], 48 * (c * NDG + g + 1))
                        for h in range(HP):
                            j = i * HP + h
                            scores(n0 + j, i, h)
                            if j % 2 == 0 and j < 4 and not first:
                                sums(n0 + j - 3, DG * HP + j - 3, False, False)
                            if first and j == 4:
                                pe.wait_ge(turned_used, c + 1)
                            if j % 2 == 0 and j >= 4:
                                sums(n0 + j - 3, j - 3, first and j - 3 < HP, False)

                group(0, True)
                with pe.Fori(1, NDG - 1) as g:
                    group(g, False)
                group(NDG - 1, False)
                n1 = (c + 1) * SB * HP
                for j in (DG * HP - 3, DG * HP - 1):
                    sums(n1 - DG * HP + j, j, False, True)
                pe.wait_ge(acc_ready, c + 1)
                for z in range(2):
                    for j in range(RPC):
                        last = nc.tensor.transpose(m.bank[2 * NS + z][0:RB, j * P:(j + 1) * P],
                                                   acc[:, z, j * RB:(j + 1) * RB], m.ident[:, :])
                last.then_inc(turned, 1)

        @block.scalar
        def _(act):
            act.sem_inc(exped, E0)
            with act.Fori(0, NC) as c:
                act.wait_ge(turned, c + 1)
                with act.Fori(0, NDG) as g:
                    for j in range(DG * HP):
                        n = (c * NDG + g) * DG * HP + j
                        old = j - NE + 1 - (j - NE) % 2
                        act.wait_ge(summed, (c * NDG + g) * (DG * HP // 2) + (old + 1) // 2 + S0)
                        act.wait_ge(scored, n + 1)
                        nc.scalar.activation(e[j % NE][:, :, :], m.ps[:, 2 * (j % NS):2 * (j % NS) + 2, 0:CW],
                                             ACT.Exp).then_inc(exped, 1)

        @block.vector
        def _(v):
            v.sem_inc(finished, 1)
            v.sem_inc(turned_used, 1)
            v.sem_inc(summed, S0)
            v.wait_ge(b_loaded, 16)
            with v.Fori(0, NC) as c:
                with v.Fori(0, NDG) as g:
                    for i in range(DG):
                        v.wait_ge(slot_loaded[i], 48 * (c * NDG + g + 1))
                        for h in range(HP):
                            n = ((c * NDG + g) * DG + i) * HP + h
                            w = e[(i * HP + h) % NE][:, :, :]
                            v.wait_ge(exped, n + 1 + E0)
                            v.scalar_tensor_tensor(w, w, 1.0,
                                                   a[i][:, :].unsqueeze(1).to_broadcast([P, 2, CW]),
                                                   op0=ALU.min, op1=ALU.mult).then_inc(weighed, 1)
                s = Steps(v, step, (6 + RPC + 1) * c)
                v.wait_ge(summed, PB // 2 * (c + 1) + S0)
                v.tensor_copy(acc[:, :, :], m.ps[:, 2 * NS:2 * NS + 2, 0:CW]).then_inc(acc_ready, 1)
                v.wait_ge(turned, 1 + c + 1)
                v.wait_ge(out_free, c + 1)
                sums = [m.bank[2 * NS + z][0:RB, :].rearrange("p (j h w) -> p j h w", j=RPC, w=VW) for z in range(2)]
                for z in range(2):
                    s.done(v.reciprocal(rden[:, z, :, :], sums[z][:, :, :, HD]))
                s.wait()
                half = D // 2
                for z in range(2):
                    s.done(v.tensor_tensor(y[:, :, z * half:(z + 1) * half].rearrange("p j (h f) -> p j h f", f=HD),
                                           sums[z][:, :, :, 0:HD],
                                           rden[:, z, :, :].unsqueeze(3).to_broadcast([RB, RPC, HEADS // 2, HD]),
                                           op=ALU.mult))
                v.wait_ge(x_loaded, 16 * (c + 1))
                s.wait()
                v.sem_inc(turned_used, 1)
                s.link(v.tensor_tensor(xr[:, :, :], xr[:, :, :], bb[:, :].unsqueeze(1).to_broadcast([RB, RPC, D]),
                                       op=ALU.add))
                s.link(v.tensor_tensor(y[:, :, :], y[:, :, :], xr[:, :, :], op=ALU.add))
                layer_norm(v, s, m, y, o, st, mv, sd, normed, rooted, c).then_inc(finished, 1)
                assert s.n == 6 + RPC + 1


def pad_input(nc, m, x, x_pad, states):
    with ExitStack() as ctx:
        zeros = ctx.enter_context(nc.sbuf_tensor("pad_zeros", [ND - N, D], F32))
        zeroed = ctx.enter_context(nc.semaphore("pad_zeroed"))
        stored = ctx.enter_context(nc.semaphore("pad_stored"))
        block = ctx.enter_context(nc.Block())

        @block.vector
        def _(v):
            v.memset(zeros[:, :], 0.0).then_inc(zeroed, 1)

        @block.sync
        def _(sp):
            sp.dma_start(x_pad[0:N, :], x).then_inc(stored, 16)
            sp.wait_ge(zeroed, 1)
            sp.dma_start(x_pad[N:ND, :], zeros[:, :]).then_inc(stored, 16)
            for a in states:
                sp.dma_start(a[NP:ND, :], zeros[0:ND - NP, :]).then_inc(stored, 16)
            sp.wait_ge(stored, 16 * (2 + len(states)))


def build_program(nc, x, src, dst, edge_type_500, L0_gnn_rel_emb, L0_gnn_W_neighbor, L0_gnn_loop_weight,
                  L1_gnn_query_kernel, L1_gnn_query_bias, L1_gnn_key_kernel, L1_gnn_key_bias, L1_gnn_kernel,
                  L1_gnn_bias, L2_gnn_weight, L3_gnn_W1, L3_gnn_b1, L3_gnn_W2, L3_gnn_b2, out):
    def dram(name, shape, dt):
        return nc.dram_tensor(name, shape, dt, kind="Internal").ap()

    x0, x1, x2, x3, x4 = (dram(f"state{i}", [ND, D], F32) for i in range(5))
    base_d, deg_d, aggr_d = dram("base_d", [NT], I32), dram("deg_d", [ND], F32), dram("aggr_d", [P, NP], F32)
    qs, ks = (dram(n, [KM, HEADS, ND], BF16) for n in ("queries", "keys"))
    vd, ad = dram("values", [ND, HEADS * VW], F32), dram("counts_turned", [ND, NP], BF16)

    with ExitStack() as ctx:
        sb = lambda name, shape, dt: ctx.enter_context(nc.sbuf_tensor(name, shape, dt))
        m = allocate(nc, ctx)
        m.in_norm = sb("in_norm", [RB, NRB], F32)
        m.loop_norm = sb("loop_norm", [RB, NRB], F32)
        m.loop_norm_s = sb("loop_norm_s", [P, SB], F32)
        m.out_norm = sb("out_norm", [P, SB], F32)
        m.at = sb("at", [P, SB, ND], BF16)
        pad_input(nc, m, x, x0, (x1, x2, x3, x4))
        with ExitStack() as tctx:
            t = Mem()
            tb = lambda name, shape, dt: tctx.enter_context(nc.sbuf_tensor(name, shape, dt))
            t.bad = tb("bad", [1, 1], I32)
            t.iota = tb("iota", [P, W * SB], F16)
            t.base = tb("base", [1, NT], I32)
            t.key = [tb(f"key{k}", [P, NT], F16) for k in range(4)]
            t.far = tb("far", [P, 2 * NT], F32)
            t.key += [t.far[:, 0:NT], t.far[:, NT:NT + NT // 2].bitcast(F16), t.far[:, NT + NT // 2:2 * NT].bitcast(F16)]
            with ExitStack() as ectx:
                edge_tables(nc, m, src, dst, edge_type_500, base_d, t)
            t.rt = tb("rt", [P, TB, NP], BF16)
            count_edges(nc, m, t)
            column_sums(nc, m, t, L0_gnn_rel_emb, aggr_d, deg_d)
        graph_conv(nc, m, "L0", x0, None, L0_gnn_W_neighbor, m.in_norm, x1, residual=x0,
                   loop_weight=L0_gnn_loop_weight, aggr_d=aggr_d, relu=True, out_degree=True)
        turn_and_project(nc, m, ad, x1, L1_gnn_query_kernel, L1_gnn_query_bias, L1_gnn_key_kernel,
                         L1_gnn_key_bias, L1_gnn_kernel, qs, ks, vd)
        score_maxima(nc, m, qs, ks)
        attend(nc, m, x1, qs, ks, vd, ad, L1_gnn_bias, x2)
        graph_conv(nc, m, "L2", x2, m.out_norm, L2_gnn_weight, m.in_norm, x3, residual=x2, loops=-1)
        graph_conv(nc, m, "L3a", x3, m.loop_norm_s, L3_gnn_W1, m.loop_norm, x4, bias=L3_gnn_b1, relu=True,
                   norm=False, loops=1)
        graph_conv(nc, m, "L3b", x4, m.loop_norm_s, L3_gnn_W2, m.loop_norm, out, residual=x3, bias=L3_gnn_b2)


_NAMES = ["x", "src", "dst", "edge_type_500", "L0_gnn_rel_emb", "L0_gnn_W_neighbor", "L0_gnn_loop_weight",
          "L1_gnn_query_kernel", "L1_gnn_query_bias", "L1_gnn_key_kernel", "L1_gnn_key_bias", "L1_gnn_kernel",
          "L1_gnn_bias", "L2_gnn_weight", "L3_gnn_W1", "L3_gnn_b1", "L3_gnn_W2", "L3_gnn_b2"]


def kernel(**inputs):
    import numpy as np
    import concourse.bacc as bacc
    from concourse.bass_utils import run_bass_kernel_spmd

    nc = bacc.Bacc("TRN2", target_bir_lowering=False, num_devices=1)
    arrays, args = {}, []
    for name in _NAMES:
        a = np.ascontiguousarray(inputs[name])
        arrays[f"in_{name}"] = a
        args.append(nc.dram_tensor(f"in_{name}", a.shape, mybir.dt.from_np(a.dtype), kind="ExternalInput").ap())
    args.append(nc.dram_tensor("out", (N, D), F32, kind="ExternalOutput").ap())
    build_program(nc, *args)
    result = run_bass_kernel_spmd(nc, [arrays], core_ids=[0])
    return result.results[0]["out"]
```
